# Optimizing a Trainium2 kernel written in Bass

```python
import numpy as np
import jax
import jax.numpy as jnp

def _softmax(x, axis=-1):
    return jax.nn.softmax(x, axis=axis)

def _gelu(x):
    return jax.nn.gelu(x, approximate=True)

def _silu(x):
    return jax.nn.silu(x)

def _sigmoid(x):
    return jax.nn.sigmoid(x)

def _layernorm(x, axis=-1, eps=1e-05):
    m = jnp.mean(x, axis=axis, keepdims=True)
    v = jnp.var(x, axis=axis, keepdims=True)
    return (x - m) / jnp.sqrt(v + eps)

def _scatter_add(tgt, idx, src, axis=0):
    return tgt.at[idx].add(src)

def _segment_sum(src, seg, n):
    return jax.ops.segment_sum(src, seg, n)
kernel_name = 'mk_recurrent_d1_jaxref_r8_0e30f8'

def setup_inputs(seed: int=0):
    np.random.seed(seed)
    _w = jnp.asarray

    def _L0_attn_setup():
        import jax, jax.numpy as jnp
        import numpy as np
        D_MODEL = 256
        N_HEAD = 16
        MLP_HIDDEN = 704
        NORMALIZER = 16.0

        def rmsnorm(x, w, eps=1e-05):
            return x * jax.lax.rsqrt(jnp.mean(x * x, axis=-1, keepdims=True) + eps) * w

        def _reference_tuple_inner(x, Wq, Wk, Wkg1, Wkg2, bkg2, Wv, Wg, bg, Wo, ln1_w, ln2_w, W1, W3, W2):
            B, L, d = x.shape
            H = N_HEAD
            hd = d // H
            kd = d // 2 // H
            scaling = (d // H) ** (-0.5)
            xn = rmsnorm(x, ln1_w)
            q = xn @ Wq
            k = xn @ Wk * scaling
            gk = jax.nn.log_sigmoid(xn @ Wkg1 @ Wkg2 + bkg2) / NORMALIZER
            v = xn @ Wv
            g = xn @ Wg + bg
            split = lambda t, dh: t.reshape(B, L, H, dh).transpose(1, 0, 2, 3)
            qh, kh, gh = (split(q, kd), split(k, kd), split(gk, kd))
            vh = split(v, hd)
            S0 = jnp.zeros((B, H, kd, hd), x.dtype)

            def step(S, inp):
                qt, kt, vt, gt = inp
                S = S * jnp.exp(gt)[..., None] + kt[..., None] * vt[..., None, :]
                ot = jnp.einsum('bhk,bhkd->bhd', qt, S)
                return (S, ot)
            Sf, o = jax.lax.scan(step, S0, (qh, kh, vh, gh))
            mu = jnp.mean(o, axis=-1, keepdims=True)
            var = jnp.var(o, axis=-1, keepdims=True)
            o = (o - mu) * jax.lax.rsqrt(var + 1e-05)
            o = o.transpose(1, 0, 2, 3).reshape(B, L, d)
            o = jax.nn.silu(g) * o
            x = x + o @ Wo
            xn2 = rmsnorm(x, ln2_w)
            x = x + jax.nn.silu(xn2 @ W1) * (xn2 @ W3) @ W2
            return (x, Sf)
        key = jax.random.key(seed)
        d, B, L, Hd = (D_MODEL, 2, 512, MLP_HIDDEN)
        ks = jax.random.split(key, 12)
        w = lambda k, shape, s=0.02: jax.random.normal(k, shape, jnp.float32) * s
        return {'x': jax.random.normal(ks[0], (B, L, d), jnp.float32), 'Wq': w(ks[1], (d, d // 2)), 'Wk': w(ks[2], (d, d // 2)), 'Wkg1': w(ks[3], (d, 16)), 'Wkg2': w(ks[4], (16, d // 2)), 'bkg2': jnp.zeros((d // 2,), jnp.float32), 'Wv': w(ks[5], (d, d)), 'Wg': w(ks[6], (d, d)), 'bg': jnp.zeros((d,), jnp.float32), 'Wo': w(ks[7], (d, d)), 'ln1_w': jnp.ones((d,), jnp.float32), 'ln2_w': jnp.ones((d,), jnp.float32), 'W1': w(ks[8], (d, Hd)), 'W3': w(ks[9], (d, Hd)), 'W2': w(ks[10], (Hd, d))}
    _L0_attn_in = _L0_attn_setup()

    def _L0_ffn_setup():
        import jax, jax.numpy as jnp
        import numpy as np
        TOP_K = 4
        NUM_EXPERTS = 16
        key = jax.random.key(seed)
        ks = jax.random.split(key, 6)
        B, S, H, I, E = (2, 128, 256, 224, NUM_EXPERTS)
        return {'x': jax.random.normal(ks[0], (B, S, H), dtype=jnp.float32), 'router_w': jax.random.normal(ks[1], (E, H), dtype=jnp.float32) * 0.02, 'expert_bias': jnp.zeros((E,), dtype=jnp.float32), 'gate_proj': jax.random.normal(ks[2], (E, H, I), dtype=jnp.float32) * 0.02, 'up_proj': jax.random.normal(ks[3], (E, H, I), dtype=jnp.float32) * 0.02, 'down_proj': jax.random.normal(ks[4], (E, I, H), dtype=jnp.float32) * 0.02}
    _L0_ffn_in = _L0_ffn_setup()
    _d = {'L0_attn_x': _L0_attn_in['x'], 'L0_attn_Wq': _L0_attn_in['Wq'], 'L0_attn_Wk': _L0_attn_in['Wk'], 'L0_attn_Wkg1': _L0_attn_in['Wkg1'], 'L0_attn_Wkg2': _L0_attn_in['Wkg2'], 'L0_attn_bkg2': _L0_attn_in['bkg2'], 'L0_attn_Wv': _L0_attn_in['Wv'], 'L0_attn_Wg': _L0_attn_in['Wg'], 'L0_attn_bg': _L0_attn_in['bg'], 'L0_attn_Wo': _L0_attn_in['Wo'], 'L0_attn_ln1_w': _L0_attn_in['ln1_w'], 'L0_attn_ln2_w': _L0_attn_in['ln2_w'], 'L0_attn_W1': _L0_attn_in['W1'], 'L0_attn_W3': _L0_attn_in['W3'], 'L0_attn_W2': _L0_attn_in['W2'], 'L0_ffn_router_w': _L0_ffn_in['router_w'], 'L0_ffn_expert_bias': _L0_ffn_in['expert_bias'], 'L0_ffn_gate_proj': _L0_ffn_in['gate_proj'], 'L0_ffn_up_proj': _L0_ffn_in['up_proj'], 'L0_ffn_down_proj': _L0_ffn_in['down_proj']}
    _x0 = _d['L0_attn_x']
    _d['L0_attn_x'] = jax.random.normal(jax.random.fold_in(jax.random.key(seed), 1), (4, 512, 256), dtype=_x0.dtype)
    del _x0
    return _d

def reference(L0_attn_x, L0_attn_Wq, L0_attn_Wk, L0_attn_Wkg1, L0_attn_Wkg2, L0_attn_bkg2, L0_attn_Wv, L0_attn_Wg, L0_attn_bg, L0_attn_Wo, L0_attn_ln1_w, L0_attn_ln2_w, L0_attn_W1, L0_attn_W3, L0_attn_W2, L0_ffn_router_w, L0_ffn_expert_bias, L0_ffn_gate_proj, L0_ffn_up_proj, L0_ffn_down_proj):

    def _L0_attn_ref(x, Wq, Wk, Wkg1, Wkg2, bkg2, Wv, Wg, bg, Wo, ln1_w, ln2_w, W1, W3, W2):
        import jax, jax.numpy as jnp
        import numpy as np
        D_MODEL = 256
        N_HEAD = 16
        MLP_HIDDEN = 704
        NORMALIZER = 16.0

        def rmsnorm(x, w, eps=1e-05):
            return x * jax.lax.rsqrt(jnp.mean(x * x, axis=-1, keepdims=True) + eps) * w

        def _reference_tuple_inner(x, Wq, Wk, Wkg1, Wkg2, bkg2, Wv, Wg, bg, Wo, ln1_w, ln2_w, W1, W3, W2):
            B, L, d = x.shape
            H = N_HEAD
            hd = d // H
            kd = d // 2 // H
            scaling = (d // H) ** (-0.5)
            xn = rmsnorm(x, ln1_w)
            q = xn @ Wq
            k = xn @ Wk * scaling
            gk = jax.nn.log_sigmoid(xn @ Wkg1 @ Wkg2 + bkg2) / NORMALIZER
            v = xn @ Wv
            g = xn @ Wg + bg
            split = lambda t, dh: t.reshape(B, L, H, dh).transpose(1, 0, 2, 3)
            qh, kh, gh = (split(q, kd), split(k, kd), split(gk, kd))
            vh = split(v, hd)
            S0 = jnp.zeros((B, H, kd, hd), x.dtype)

            def step(S, inp):
                qt, kt, vt, gt = inp
                S = S * jnp.exp(gt)[..., None] + kt[..., None] * vt[..., None, :]
                ot = jnp.einsum('bhk,bhkd->bhd', qt, S)
                return (S, ot)
            Sf, o = jax.lax.scan(step, S0, (qh, kh, vh, gh))
            mu = jnp.mean(o, axis=-1, keepdims=True)
            var = jnp.var(o, axis=-1, keepdims=True)
            o = (o - mu) * jax.lax.rsqrt(var + 1e-05)
            o = o.transpose(1, 0, 2, 3).reshape(B, L, d)
            o = jax.nn.silu(g) * o
            x = x + o @ Wo
            xn2 = rmsnorm(x, ln2_w)
            x = x + jax.nn.silu(xn2 @ W1) * (xn2 @ W3) @ W2
            return (x, Sf)
        return _reference_tuple_inner(x, Wq, Wk, Wkg1, Wkg2, bkg2, Wv, Wg, bg, Wo, ln1_w, ln2_w, W1, W3, W2)[0]

    def _L0_ffn_ref(x, router_w, expert_bias, gate_proj, up_proj, down_proj):
        import jax, jax.numpy as jnp
        import numpy as np
        TOP_K = 4
        NUM_EXPERTS = 16
        logits = jnp.einsum('bsh,eh->bse', x, router_w) + expert_bias
        scores = jax.nn.softmax(logits, axis=-1)
        top_w, top_idx = jax.lax.top_k(scores, TOP_K)
        top_w = top_w / jnp.sum(top_w, axis=-1, keepdims=True)
        g = jnp.einsum('bsh,khe->bske', x, gate_proj)
        u = jnp.einsum('bsh,khe->bske', x, up_proj)
        act = jax.nn.silu(g) * u
        out = jnp.einsum('bske,keh->bskh', act, down_proj)
        sel = jnp.take_along_axis(out, top_idx[..., None], axis=2)
        return jnp.sum(sel * top_w[..., None], axis=2)
    x = L0_attn_x
    xn = _layernorm(x, axis=-1)
    s = _L0_attn_ref(xn, L0_attn_Wq, L0_attn_Wk, L0_attn_Wkg1, L0_attn_Wkg2, L0_attn_bkg2, L0_attn_Wv, L0_attn_Wg, L0_attn_bg, L0_attn_Wo, L0_attn_ln1_w, L0_attn_ln2_w, L0_attn_W1, L0_attn_W3, L0_attn_W2)
    g = _silu(_L0_ffn_ref(xn, L0_ffn_router_w, L0_ffn_expert_bias, L0_ffn_gate_proj, L0_ffn_up_proj, L0_ffn_down_proj))
    x = x + s * g
    return x

_drawn_inputs = setup_inputs


def setup_inputs(seed=0):
    import zlib

    import numpy as np

    out = dict(_drawn_inputs(seed))
    spreads = {'L0_attn_bkg2': (0.0, 0.8),
     'L0_attn_bg': (0.0, 0.8),
     'L0_attn_ln1_w': (1.0, 0.6),
     'L0_attn_ln2_w': (1.0, 0.6),
     'L0_ffn_expert_bias': (0.0, 0.8)}
    factors = {'L0_attn_Wq': 8.0,
     'L0_attn_Wk': 8.0,
     'L0_attn_Wkg1': 8.0,
     'L0_attn_Wkg2': 8.0,
     'L0_attn_Wv': 8.0,
     'L0_attn_Wg': 8.0,
     'L0_attn_Wo': 8.0,
     'L0_attn_W1': 8.0,
     'L0_attn_W3': 8.0,
     'L0_attn_W2': 8.0,
     'L0_ffn_router_w': 8.0,
     'L0_ffn_gate_proj': 8.0,
     'L0_ffn_up_proj': 8.0,
     'L0_ffn_down_proj': 8.0}
    for name, (base, spread) in spreads.items():
        noise = np.random.default_rng([zlib.crc32(name.encode()), seed]).standard_normal(out[name].shape)
        drawn = base * np.exp(spread * noise) if base else spread * noise
        out[name] = jnp.asarray(drawn.astype(out[name].dtype))
    for name, factor in factors.items():
        out[name] = (out[name] * factor).astype(out[name].dtype)
    return out
```

```python
from contextlib import ExitStack

import concourse.bass as bass
from concourse import mybir

F32 = mybir.dt.float32
F32R = mybir.dt.float32r
F16 = mybir.dt.float16
I32 = mybir.dt.int32
U32 = mybir.dt.uint32
ALU = mybir.AluOpType
ACT = mybir.ActivationFunctionType
AX = mybir.AxisListType

P = 128
EPS = 1e-5
RSQRT_MAGIC = 0x5F3759DF
HALF_MAGIC = RSQRT_MAGIC - 0x400000
NEWTON = 3


def sem_chain(eng, sem, base, per=0, it=0):
    count = [base]

    def step(ins):
        count[0] += 1
        ins.then_inc(sem, 1)
        eng.wait_ge(sem, it * per + count[0])
        return count[0]

    return step


def build_block(nc, x, Wq, Wk, Wkg1, Wkg2, bkg2, Wv, Wg, bg, Wo, ln1_w, ln2_w, W1, W3, W2,
                router_w, expert_bias, gate_proj, up_proj, down_proj, out):
    B, L, D = x.shape
    T = B * L
    NT = T // P
    TPB = L // P
    KC = D // P
    E, _, I = gate_proj.shape
    F = W1.shape[1]
    QK = Wq.shape[1]
    R = Wkg1.shape[1]
    H = 16
    KD = QK // H
    HD = D // H
    DH = HD // KC
    KS = float(HD) ** -0.5
    NORMALIZER = 16.0
    TOP = 4
    SLOT_TILES = -(-(T * TOP // P + E - 1) // 4) * 4
    SLOTS = SLOT_TILES * P
    ROW = D + 2 + E
    SCALE_C, TOKEN_C, WEIGHT_C = D, D + 1, D + 2
    HK = I // 2
    IC = 2
    assert QK == P and D == 2 * P and B * H * KD * HD == 4 * P * HD and L == 512

    QC, KCOL, ZC, VC, GC = 0, QK, 2 * QK, 3 * QK, 3 * QK + D
    WA = 3 * QK + 2 * D
    FT = [(c * P, min(P, F - c * P)) for c in range((F + P - 1) // P)]
    NF = len(FT)

    xr = x.rearrange("b l d -> (b l) d").rearrange("(t p) d -> p t d", p=P)
    outr = out.rearrange("b l d -> (b l) d").rearrange("(t p) d -> p t d", p=P)

    v_dram = nc.dram_tensor("v_scratch", (B, HD, H, L), F32, kind="Internal").ap()
    rows_dram = nc.dram_tensor("rows_scratch", (SLOTS, ROW), F32, kind="Internal").ap()
    y_dram = [nc.dram_tensor(f"y_scratch{i}", (T + P, D), F32, kind="Internal").ap() for i in range(2)]

    with ExitStack() as ctx:
        def sem(name):
            return ctx.enter_context(nc.semaphore(name))

        def sb(name, shape, dt, scope=ctx):
            return scope.enter_context(nc.sbuf_tensor(name, shape, dt))

        xn = sb("xn", [P, NT, D], F32)
        ident = sb("ident", [P, P], F32)
        ident16 = sb("ident16", [P, P], F16)
        slot_u = sb("slot_u", [P, TOP, NT], U32)
        tile_expert = sb("tile_expert", [1, SLOT_TILES], U32)

        ones16 = sb("ones16", [P, P], F16)
        before16 = sb("before16", [P, P], F16)
        sumk = sb("sumk", [P, 2 * P - H], F32)
        head_i = sb("head_i", [P, H], I32)
        head_m = sb("head_m", [P, H], I32)
        restart = sb("restart", [P, NT, E], F32)
        one_e = sb("one_e", [P, E], F32)
        steps128 = sb("steps128", [P, E, NT], F32)
        tile_no = sb("tile_no", [1, SLOT_TILES], F32)
        c15 = sb("c15", [P, TPB * H], F32)
        zrow = sb("zrow", [P, ROW], F32)
        ln1 = sb("ln1", [P, KC], F32)
        ln1k = sb("ln1k", [P, KC], F32)
        ln2 = sb("ln2", [P, KC], F32)
        bz = sb("bz", [P, 1], F32)
        bgT = sb("bgT", [P, KC], F32)
        eb = sb("eb", [P, E], F32)
        bst = sb("bst", [P, NT, 6], F32)
        mv = sb("mv", [P, NT, 2], F32)
        rs_v = sb("rs_v", [P, 4, NT], F32)
        rstd = sb("rstd", [P, NT], F32)
        r1 = sb("r1", [P, NT], F32)
        negmr = sb("negmr", [P, NT], F32)

        att = ExitStack()
        q_sb = sb("q_sb", [P, T], F32, att)
        k_sb = sb("k_sb", [P, T], F32, att)
        a_sb = sb("a_sb", [P, T], F32, att)
        pre1 = ExitStack()
        w13_raw = sb("w13_raw", [P, KC, 2 * F], F32, pre1)
        wo_raw = sb("wo_raw", [P, KC, D], F32, pre1)
        w2_raw = sb("w2_raw", [P, NF, D], F32, pre1)
        vt = sb("vt", [P, 2, L], F32, pre1)
        zb = sb("zb", [P, L], F32, pre1)
        zabs = sb("zabs", [P, L], F32, pre1)
        zexp = sb("zexp", [P, L], F32, pre1)
        zln = sb("zln", [P, L], F32, pre1)
        pre1.close()
        vrep = sb("vrep", [P, 2, 2, L], F32, att)
        kv = sb("kv", [P, 2, 2, L], F32, att)
        st = sb("st", [P, 2, 2, L], F32, att)
        qs = sb("qs", [P, 2, 2, L], F32, att)
        g_sb = sb("g_sb", [P, KC, T], F32, att)
        wo_h = sb("wo_h", [P, KC, D], F32R, att)
        wo_l = sb("wo_l", [P, KC, D], F32R, att)
        w13 = sb("w13", [P, 2, KC, 2 * F], F16, att)
        w2_h = sb("w2_h", [P, NF, D], F32R, att)
        w2_l = sb("w2_l", [P, NF, D], F32R, att)
        rows = sb("rows", [P, NT, ROW], F32, att)
        rows16 = rows[:, :, :].bitcast(F16)
        pre = ExitStack()
        w_a = sb("w_a", [P, 2, KC, WA], F16, pre)
        anT = sb("anT", [P, 2, KC, T], F16, pre)
        wa_raw = sb("wa_raw", [P, KC, WA], F32, pre)
        wk2 = sb("wk2", [R, QK], F32, pre)
        wk1 = sb("wk1", [P, KC, R], F32, pre)
        wk1T = sb("wk1T", [R, KC, P], F32, pre)
        rw_raw = sb("rw_raw", [E, D], F32, pre)
        rw = sb("rw", [P, 2, KC, E], F16, pre)
        zls = sb("zls", [P, L], F32, pre)
        pre.close()
        oT = sb("oT", [P, KC, L], F32, att)
        ot = sb("ot", [P, TPB, D], F32, att)
        on = sb("on", [P, TPB, D], F32, att)
        gs = sb("gs", [P, KC, L], F32, att)
        og_h = sb("og_h", [P, KC, L], F32R, att)
        og_l = sb("og_l", [P, KC, L], F32R, att)
        an2 = sb("an2", [P, TPB, 2, D], F16, att)
        an2T = sb("an2T", [P, 2, KC, L], F16, att)
        ghead = [sb(f"ghead{i}", [P, TPB * H], F32, att) for i in range(4)]
        grow = [sb(f"grow{i}", [P, TPB], F32, att) for i in range(4)]
        rt = ExitStack()
        def rsb(name, shape=(P, NT, E), dt=F32):
            return sb(name, list(shape), dt, rt)
        lg = rsb("lg")
        mx = rsb("mx", (P, NT))
        m8 = rsb("m8", (P, NT, 8))
        gt = rsb("gt")
        eq = rsb("eq")
        need = rsb("need", (P, NT))
        eqc = rsb("eqc")
        Msel = rsb("Msel")
        M16 = rsb("M16", dt=F16)
        ex = rsb("ex")
        sm = rsb("sm", (P, NT))
        wgt = rsb("wgt")
        tot = rsb("tot", (P, E, NT))
        inc = rsb("inc", (P, E, NT))
        over = rsb("over", (P, E, NT))
        ntl = rsb("ntl", (P, E))
        ntc = rsb("ntc", (P, E))
        base = rsb("base", (P, E))
        slot = rsb("slot")
        cnt = rsb("cnt")
        pick = rsb("pick")
        prod = rsb("prod")
        slot_f = rsb("slot_f", (P, TOP, NT))
        owner = rsb("owner", (1, SLOT_TILES, E))
        own1 = rsb("own1", (1, SLOT_TILES))


        rt.close()
        sg = sb("sg", [P, 2, L], F32, att)
        hf = sb("hf", [P, 2, L], F32, att)
        h_h = sb("h_h", [P, NF, L], F32R, att)
        h_l = sb("h_l", [P, NF, L], F32R, att)
        att.close()

        UN = 16
        RAW = 8
        w_gu = sb("w_gu", [P, E, 2, KC, 2 * I], F16)
        gu_raw = sb("gu_raw", [P, RAW, KC, 2 * I], F32)
        wd = sb("wd", [HK, E, IC, D], F32)
        X = sb("X", [P, UN, ROW], F32)
        X16 = X[:, :, :].bitcast(F16)
        xT = sb("xT", [P, 2, 2, KC, P], F16)
        sl = sb("sl", [P, 2, I], F32)
        h = sb("h", [P, 2, I], F32)
        hT = sb("hT", [HK, 2, IC, P], F32)
        y = sb("y", [P, UN, D], F32)
        w_gu_f = w_gu[:, :, :, :, :].rearrange("p e a c n -> p (e a c n)").bitcast(F32)
        raw_f = gu_raw[:, :, :, :].rearrange("p r c n -> p (r c n)")
        turn_ps = ctx.enter_context(nc.psum_tensor("turn_ps", [P, 2, 512], F32))
        mm_ps = ctx.enter_context(nc.psum_tensor("mm_ps", [P, 4, 512], F32))
        sum_ps = ctx.enter_context(nc.psum_tensor("sum_ps", [P, 2, 512], F32))
        PS = T0, T1 = [turn_ps[:, i, :] for i in range(2)]
        M = [mm_ps[:, i, :] for i in range(4)]
        O0, O1 = [sum_ps[:, i, :] for i in range(2)]


        s = {n: sem(n) for n in """const_pool const_dve x_in0 x_in1 x_in2 x_in3 wa_in wz_in wb_in small_in
            stats rsq_seed rsq_done1 rsq_seed2 rsq_done2 norm_const xn_ready anh_ready anl_ready
            wk1_t wk1_copied wz_ready rw_t wprep_act wprep_dve wprep_pool w13_in wo_in w2_in zero_fill
            tp_ready tp_evac anT_ready proj_ready evac_act evac_dve zb_ready zln_ready zls_ready a_ready
            logits_ready dve_chain pool_chain act_chain exp_ready m16_ready cum_ready route_ready
            ex_in scatter zero_row ln1k_ready cscale dve_max vt_ready vt_out0 vt_out1 prep_done lg_ready
            pool_head pool_row vr_in0 vr_in1 kv_ready st_ready qs_ready gla_used oT_evac pool_turn act_turn tpo_ready ot_ready oc_ready sq_ready
            head_dve head_seed head_rstd on_ready on_part tpb_ready gs_ready og_ready ogh_ready ogl_ready wo_ready xb_ready
            ms_ready row_dve row_seed row_rstd an2h_ready an2l_ready tpn_ready an2T_evac
            gu_ready sg_ready hf_ready hh_ready hl_ready w2_ready xc_ready
            ew_ready wd_in xt_ready xe_ready eg_ready sl_ready hm_ready ht_ready he_ready dn_ready ye_ready
            y_out0 y_out1 y_slots act_turn3 xr_in fin_in0 fin_in1 fin_in2 fin_in3 ysum_ready silu_ready fin_mul out_ready
            out_done""".split()}
        y_out = [s["y_out0"], s["y_out1"]]
        x_in = [sem(f"row_in{i}") for i in range(UN)]
        raw_in = [sem(f"raw_in{i}") for i in range(RAW)]
        fin_in = [s[f"fin_in{c}"] for c in range(B)]
        vr_in = [s["vr_in0"], s["vr_in1"]]
        vt_out = [s["vt_out0"], s["vt_out1"]]

        def rsqrt_seed(step, r, v, magic=RSQRT_MAGIC):
            step(nc.vector.tensor_scalar(r.bitcast(I32), v.bitcast(I32), 1, None, ALU.logical_shift_right))
            nc_i = nc.vector.tensor_scalar(r.bitcast(I32), r.bitcast(I32), -1.0, float(magic), ALU.mult, ALU.add)
            return nc_i

        def rsqrt_newton(eng, step, r, v, t):
            for n in range(NEWTON):
                step(eng.tensor_tensor(t, r, r, ALU.mult))
                step(eng.tensor_tensor(t, t, v, ALU.mult))
                step(eng.tensor_scalar(t, t, -0.5, 1.5, ALU.mult, ALU.add))
                ins = eng.tensor_tensor(r, r, t, ALU.mult)
                if n < NEWTON - 1:
                    step(ins)
            return ins

        def rsqrt_newton_half(eng, step, r, half_v, t):
            for n in range(NEWTON):
                step(eng.tensor_tensor(t, r, r, ALU.mult))
                step(eng.tensor_tensor(t, t, half_v, ALU.mult))
                step(eng.tensor_tensor(t, c15[:, 0:t.shape[1]], t, ALU.subtract))
                ins = eng.tensor_tensor(r, r, t, ALU.mult)
                if n < NEWTON - 1:
                    step(ins)
            return ins

        xq = [s[f"x_in{c}"] for c in range(B)]
        NSMALL = 2 + KD + HD + 1
        NWPREP = 4 * KC + KC + 1
        WK1p = T0[0:R, 0:KC * P].rearrange("p (c n) -> p c n", c=KC)
        RWp = T1[:, 0:KC * E].rearrange("p (c n) -> p c n", c=KC)
        Zp = M[0][:, 0:KC * QK].rearrange("p (c n) -> p c n", c=KC)

        def hk_view(ap, from_hk):
            return ap.rearrange("p (h k) -> p k h", k=KD) if from_hk else ap.rearrange("p (k h) -> p k h", k=KD)

        def wparts(c, part):
            w = lambda col: w_a[:, part, c, col:col + QK]
            for col, scale in ((QC, ln1[:, c:c + 1]), (KCOL, ln1k[:, c:c + 1])):
                yield hk_view(w(col), False), hk_view(wa_raw[:, c, col:col + QK], True), scale
            for col in (VC, GC):
                yield (w_a[:, part, c, col:col + D].rearrange("p (d h) -> p d h", d=HD),
                       wa_raw[:, c, col:col + D].rearrange("p (h d) -> p d h", d=HD), ln1[:, c:c + 1])

        def triple(pe, out_ap, pairs):
            for n, (lhsT, rhs) in enumerate(pairs):
                last = nc.tensor.matmul(out_ap, lhsT, rhs, start=(n == 0), stop=(n == len(pairs) - 1))
            return last

        U = HD // 2
        TOK = lambda b: bass.ds(b * L, L)
        TILES = lambda b, i=0, n=TPB: bass.ds(b * TPB + i, n)
        pair_bc = lambda ap: ap.rearrange("p (a l) -> p a l", a=1).to_broadcast((P, 2, L))

        def wait(eng, sem_, value):
            if not isinstance(value, int) or value > 0:
                eng.wait_ge(sem_, value)

        def turns(eng, step_fn):
            for it in (0, 1):
                for u in range(U):
                    step_fn(it, it - 1 if it else None, None, u)
            with eng.Fori(2, B) as it:
                for u in range(U):
                    step_fn(it, it - 1, it - 2, u)
            for it in (B, B + 1):
                for u in range(U):
                    step_fn(None, it - 1 if it == B else None, it - 2, u)

        head4 = lambda ap: ap.rearrange("p (t h) -> p t h", t=TPB)

        def attention_over(eng):
            eng.wait_ge(s["xc_ready"], 2 * B + 2)
            eng.wait_ge(s["scatter"], 16 * NT * TOP)

        GROUPS = SLOT_TILES // UN

        def expert(eng, t, u):
            return eng.value_load(tile_expert[0:1, bass.ds(t, 1)], min_val=0, max_val=E - 1)

        ysum = [w_gu_f[:, c * TPB * D:(c + 1) * TPB * D] for c in range(B)]
        ysum2 = [w_gu_f[:, (B + c) * TPB * D:(B + c + 1) * TPB * D] for c in range(B)]
        xback = [raw_f[:, c * TPB * D:(c + 1) * TPB * D] for c in range(B)]

        block = ctx.enter_context(nc.Block())

        @block.sync
        def _(sp):
            for c in range(B):
                sp.dma_start(xn[:, c * TPB:(c + 1) * TPB, :], xr[:, c * TPB:(c + 1) * TPB, :]).then_inc(xq[c], 16)
            for w, col in ((Wq, QC), (Wk, KCOL)):
                sp.dma_start(wa_raw[:, :, col:col + QK], w.rearrange("(c p) n -> p c n", p=P)).then_inc(s["wa_in"], 16)
            for w, col in ((Wv, VC), (Wg, GC)):
                sp.dma_start(wa_raw[:, :, col:col + D], w.rearrange("(c p) n -> p c n", p=P)).then_inc(s["wa_in"], 16)
            sp.dma_start(w13_raw[:, :, 0:F], W1.rearrange("(c p) n -> p c n", p=P)).then_inc(s["w13_in"], 16)
            sp.dma_start(w13_raw[:, :, F:2 * F], W3.rearrange("(c p) n -> p c n", p=P)).then_inc(s["w13_in"], 16)
            for d in range(HD):
                c, dd = d // DH, d % DH
                sp.dma_start(wo_raw[dd * H:(dd + 1) * H, c, :],
                             Wo.rearrange("(h d) n -> d h n", d=HD)[d]).then_inc(s["wo_in"], 16)
            nfull = F // P
            sp.dma_start(w2_raw[:, 0:nfull, :], W2[0:nfull * P].rearrange("(c p) n -> p c n", p=P)).then_inc(s["w2_in"], 16)
            sp.dma_start(w2_raw[0:F - nfull * P, nfull, :], W2[nfull * P:F]).then_inc(s["w2_in"], 16)
            sp.sem_inc(vt_out[0], 16)
            sp.sem_inc(vt_out[1], 16)
            with sp.Fori(0, B) as b:
                for c in range(2):
                    sp.wait_ge(s["vt_ready"], b * 2 + (c + 1))
                    sp.dma_start(v_dram[bass.ds(b, 1), c * DH:(c + 1) * DH].rearrange("b d h l -> (b d h) l"),
                                 vt[:, c, :]).then_inc(vt_out[c], 16)
            for c in range(2):
                sp.wait_ge(vt_out[c], 16 * (B + 1))
            sp.wait_ge(s["a_ready"], B)
            sp.wait_ge(s["prep_done"], 1)
            with sp.Fori(0, B) as b:
                for u in range(U):
                    sp.wait_ge(s["kv_ready"], b * U + (u + 1))
                    for j in range(2):
                        src = v_dram[bass.ds(b, 1), 2 * u + j].rearrange("b h l -> (b h) l")
                        sp.dma_start(vrep[:, u % 2, j, :], bass.AP(tensor=src.tensor, offset=src.offset,
                                                                   ap=[[0, KD], [L, H], [1, L]])).then_inc(vr_in[u % 2], 16)

            attention_over(sp)

            def load_weights(e):
                if e >= RAW:
                    sp.wait_ge(s["ew_ready"], e - RAW + 1)
                for i, w in enumerate((gate_proj, up_proj)):
                    sp.dma_start(gu_raw[:, e % RAW, :, i * I:(i + 1) * I],
                                 w[e].rearrange("(c p) n -> p c n", p=P)).then_inc(raw_in[e % RAW], 16)

            def load_rows(g, u):
                sp.dma_start(X[:, u, :], rows_dram[bass.ds((g * UN + u) * P, P), :]).then_inc(x_in[u], 16)

            for e in range(2):
                load_weights(e)
            for u in range(UN):
                load_rows(0, u)
            for e in range(2, E):
                load_weights(e)
            with sp.Fori(1, GROUPS) as g:
                for u in range(UN):
                    sp.wait_ge(s["y_slots"], g * UN + (u + 3))
                    load_rows(g, u)
            sp.wait_ge(s["ew_ready"], E)
            for c in range(B):
                sp.dma_start(xback[c].rearrange("p (t d) -> p t d", t=TPB), xr[:, c * TPB:(c + 1) * TPB, :]).then_inc(s["xr_in"], 16)
            for i in range(2):
                sp.wait_ge(y_out[i], 16 * SLOT_TILES // 2)
            sp.wait_ge(s["eg_ready"], SLOT_TILES + 2)
            for c in range(B):
                for i, dst in enumerate((ysum, ysum2)):
                    sp.dma_start(dst[c].rearrange("p (t d) -> p t d", t=TPB),
                                 y_dram[i].rearrange("(t p) d -> p t d", p=P)[:, c * TPB:(c + 1) * TPB, :])\
                        .then_inc(fin_in[c], 16)
            for c in range(B):
                sp.wait_ge(s["out_ready"], c + 1)
                sp.dma_start(outr[:, c * TPB:(c + 1) * TPB, :], ysum[c].rearrange("p (t d) -> p t d", t=TPB))\
                    .then_inc(s["out_done"], 16)
            sp.wait_ge(s["out_done"], 16 * B)

        @block.gpsimd
        def _(pool):
            step = sem_chain(pool, s["pool_chain"], 0)
            step(nc.gpsimd.memset(zrow[:, :], 0.0))
            nc.gpsimd.iota(zrow[:, TOKEN_C:TOKEN_C + 1].bitcast(U32), pattern=[[0, 1]], base=T,
                           channel_multiplier=1).then_inc(s["zero_row"], 1)
            step(nc.gpsimd.iota(rows[:, :, TOKEN_C:TOKEN_C + 1].bitcast(U32), pattern=[[P, NT], [0, 1]], base=0,
                                channel_multiplier=1))
            for m in (ident, ident16):
                step(nc.gpsimd.memset(m[:, :], 0.0))
                step(nc.gpsimd.affine_select(out=m[:, :], in_=m[:, :], compare_op=ALU.not_equal, fill=1.0, base=0,
                                             pattern=[[-1, P]], channel_multiplier=1))
            step(nc.gpsimd.memset(ones16[:, :], 1.0))
            step(nc.gpsimd.affine_select(out=before16[:, :], in_=ones16[:, :], compare_op=ALU.is_gt, fill=0.0, base=0,
                                         pattern=[[1, P]], channel_multiplier=-1))
            step(nc.gpsimd.iota(head_i[:, :], pattern=[[-1, H]], base=H, channel_multiplier=1))
            step(nc.gpsimd.memset(sumk[:, :], 0.0))
            step(nc.gpsimd.memset(restart[:, :, :], 1.0))
            step(nc.gpsimd.memset(restart[:, :, 0:1], 0.0))
            step(nc.gpsimd.memset(one_e[:, :], 1.0))
            step(nc.gpsimd.memset(c15[:, :], 1.5))
            step(nc.gpsimd.iota(steps128[:, :, :], pattern=[[0, E], [P, NT]], base=0, channel_multiplier=0,
                                allow_small_or_imprecise_dtypes=True))
            nc.gpsimd.iota(tile_no[:, :], pattern=[[1, SLOT_TILES]], base=0, channel_multiplier=0,
                           allow_small_or_imprecise_dtypes=True).then_inc(s["const_pool"], 1)
            pool.wait_ge(s["rsq_seed"], 1)
            rsqrt_newton(nc.gpsimd, step, rstd[:, :], rs_v[:, 0, :], rs_v[:, 1, :]).then_inc(s["rsq_done1"], 1)
            pool.wait_ge(s["rsq_seed2"], 1)
            rsqrt_newton(nc.gpsimd, step, r1[:, :], rs_v[:, 2, :], rs_v[:, 3, :]).then_inc(s["rsq_done2"], 1)
            pool.wait_ge(s["rsq_done2"], 1)
            for t in range(NT):
                pool.wait_ge(s["xn_ready"], t + 1)
                nc.gpsimd.tensor_scalar(rows16[:, t, 0:D], xn[:, t, :], r1[:, t:t + 1], 1.0, ALU.mult,
                                        ALU.mult).then_inc(s["anh_ready"], 1)
            pool.wait_ge(s["w13_in"], 32)
            pool.wait_ge(s["small_in"], 16 * NSMALL)
            for c in range(KC):
                raw = w13_raw[:, c, :]
                step(nc.gpsimd.tensor_scalar(raw, raw, ln2[:, c:c + 1], 1.0, ALU.mult, ALU.mult))
                step(nc.gpsimd.tensor_scalar(w13[:, 0, c, :], raw, 1.0, 1.0, ALU.mult, ALU.mult))
                step(nc.gpsimd.tensor_tensor(w13[:, 1, c, :], raw, w13[:, 0, c, :], ALU.subtract))
            pool.wait_ge(s["wo_in"], 16 * HD)
            pool.wait_ge(s["w2_in"], 32)
            nf, fr = F // P, F % P
            parts = [(wo_raw[:, :, :], wo_h[:, :, :], wo_l[:, :, :]),
                     (w2_raw[:, 0:nf, :], w2_h[:, 0:nf, :], w2_l[:, 0:nf, :]),
                     (w2_raw[0:fr, nf, :], w2_h[0:fr, nf, :], w2_l[0:fr, nf, :])]
            for raw, hi, lo in parts:
                step(nc.gpsimd.tensor_scalar(hi, raw, 1.0, 1.0, ALU.mult, ALU.mult))
                step(nc.gpsimd.tensor_tensor(lo, raw, hi.bitcast(F32), ALU.subtract))
            pool.sem_inc(s["prep_done"], 1)
            scatters = iter([(t, j) for t in range(NT) for j in range(TOP)])

            def scatter(n):
                for _, (t, j) in zip(range(n), scatters):
                    nc.gpsimd.indirect_dma_start(
                        rows_dram, bass.IndirectOffsetOnAxis(ap=slot_u[:, j, t:t + 1], axis=0),
                        rows[:, t, :], None).then_inc(s["scatter"], 16)

            pool.sem_inc(s["qs_ready"], 2)
            pool.wait_ge(s["route_ready"], 1)
            pool.wait_ge(s["zero_fill"], 48)
            pool.wait_ge(s["anl_ready"], NT)

            def newton(sem_seed, sem_done, sem_chain_, b, r, v, t):
                pool.wait_ge(sem_seed, b + 1)
                step = sem_chain(pool, sem_chain_, 0, 4 * NEWTON - 1, b)
                rsqrt_newton_half(nc.gpsimd, step, r, v, t).then_inc(sem_done, 1)

            def step_fn(a, b, c, u):
                if a is not None:
                    pool.wait_ge(s["st_ready"], a * 2 * U + (2 * u + 6))
                    pool.wait_ge(s["gla_used"], a * U + (u + 1))
                    pool.sem_inc(s["pool_turn"], 1)
                    nc.gpsimd.tensor_tensor(qs[:, u % 2, :, :], st[:, u % 2, :, :], pair_bc(q_sb[:, TOK(a)]),
                                            ALU.mult).then_inc(s["qs_ready"], 1)
                if b is not None and u == 1:
                    newton(s["head_seed"], s["head_rstd"], s["pool_head"], b, ghead[1][:, :], ghead[0][:, :], ghead[2][:, :])
                if b is not None and u == 6:
                    newton(s["row_seed"], s["row_rstd"], s["pool_row"], b, grow[1][:, :], grow[0][:, :], grow[2][:, :])
                if isinstance(a, int):
                    scatter(3)
                elif isinstance(c, int) and b is not None:
                    scatter(2)

            turns(pool, step_fn)
            pool.wait_ge(s["pool_turn"], U * B)
            pool.wait_ge(s["scatter"], 16 * NT * TOP)

            attention_over(pool)
            for e in range(E):
                pool.wait_ge(raw_in[e % RAW], 32 * (e // RAW + 1))
                raw = gu_raw[:, e % RAW, :, :]
                step(nc.gpsimd.tensor_scalar(w_gu[:, e, 0, :, :], raw, 1.0, 1.0, ALU.mult, ALU.mult))
                nc.gpsimd.tensor_tensor(w_gu[:, e, 1, :, :], raw, w_gu[:, e, 0, :, :], ALU.subtract).then_inc(s["ew_ready"], 1)
            pool.sem_inc(s["y_slots"], UN)

            def add_out(g, u):
                pool.wait_ge(s["ye_ready"], g * UN + (u + 3))
                wait(pool, y_out[u % 2], g * (16 * UN // 2) + 16 * (u // 2))
                pool.sem_inc(s["y_slots"], 1)
                nc.gpsimd.indirect_dma_start(
                    y_dram[u % 2], bass.IndirectOffsetOnAxis(ap=X[:, u, TOKEN_C:TOKEN_C + 1].bitcast(U32), axis=0),
                    y[:, u, :], None, compute_op=ALU.add).then_inc(y_out[u % 2], 16)

            for u in range(UN):
                add_out(0, u)
            with pool.Fori(1, GROUPS) as g:
                for u in range(UN):
                    add_out(g, u)

        @block.scalar
        def _(act):
            chain = sem_chain(act, s["act_chain"], 0)
            act.dma_start(wk1[:, :, :], Wkg1.rearrange("(c p) n -> p c n", p=P)).then_inc(s["wz_in"], 16)
            act.dma_start(wk2[:, :], Wkg2).then_inc(s["wz_in"], 16)
            act.dma_start(rw_raw[:, :], router_w).then_inc(s["wz_in"], 16)
            with nc.allow_non_contiguous_dma(reason="a few hundred numbers"):
                act.dma_start(ln1[:, :], ln1_w.rearrange("(c p) -> p c", p=P)).then_inc(s["small_in"], 16)
                act.dma_start(ln2[:, :], ln2_w.rearrange("(c p) -> p c", p=P)).then_inc(s["small_in"], 16)
                for k in range(KD):
                    act.dma_start(bz[k * H:(k + 1) * H, :],
                                  bkg2.rearrange("(h k a) -> k h a", k=KD, a=1)[k]).then_inc(s["small_in"], 16)
                for d in range(HD):
                    c, dd = d // DH, d % DH
                    act.dma_start(bgT[dd * H:(dd + 1) * H, c:c + 1],
                                  bg.rearrange("(h d a) -> d h a", d=HD, a=1)[d]).then_inc(s["small_in"], 16)
                act.dma_start(eb[:, :], expert_bias.rearrange("(a e) -> a e", a=1).to_broadcast((P, E))).then_inc(s["small_in"], 16)
            act.wait_ge(s["zero_row"], 1)
            act.dma_start(rows_dram.rearrange("(n p) c -> p n c", p=P),
                          zrow[:, :].rearrange("p (a c) -> p a c", a=1).to_broadcast((P, SLOT_TILES, ROW)))\
                .then_inc(s["zero_fill"], 16)
            for acc in y_dram:
                act.dma_start(acc.rearrange("(n p) d -> p n d", p=P),
                              zrow[:, 0:D].rearrange("p (a c) -> p a c", a=1).to_broadcast((P, NT + 1, D)))\
                    .then_inc(s["zero_fill"], 16)
            nc.scalar.preload_act_table(ACT.Ln)
            act.wait_ge(s["wa_in"], 64)
            act.wait_ge(s["small_in"], 16 * NSMALL)
            act.wait_ge(s["ln1k_ready"], 1)
            for c in range(KC):
                for out_ap, in_ap, scale in wparts(c, 0):
                    nc.scalar.activation(out_ap, in_ap, ACT.Copy, scale=scale).then_inc(s["wprep_act"], 1)
            act.wait_ge(s["wz_ready"], 1)
            for c in range(KC):
                nc.scalar.activation(hk_view(w_a[:, 0, c, ZC:ZC + QK], False), hk_view(Zp[:, c, :], True), ACT.Copy,
                                     scale=ln1[:, c:c + 1]).then_inc(s["wprep_act"], 1)
            act.wait_ge(s["rw_t"], 1)
            nc.scalar.activation(rw[:, 0, :, :], RWp, ACT.Copy).then_inc(s["wprep_act"], 1)
            act.sem_inc(s["tp_evac"], 2)
            act.sem_inc(s["evac_act"], 2)
            def evac_rows(t, j):
                act.wait_ge(s["tp_ready"], t + 1)
                nc.scalar.activation(anT[:, :, :, bass.ds(t * P, P)],
                                     PS[j % 2].rearrange("p (a c n) -> p a c n", a=2, c=KC),
                                     ACT.Copy).then_inc(s["tp_evac"], 1)

            def turn(b, more):
                def evac(i, out_ap, **kw):
                    act.wait_ge(s["proj_ready"], b * 7 + (i + 1))
                    nc.scalar.activation(out_ap, M[i % 4], kw.get("func", ACT.Copy),
                                         **({"bias": kw["bias"]} if "bias" in kw else {})).then_inc(s["evac_act"], 1)

                def next_rows(j):
                    if more:
                        evac_rows((b + 1) * TPB + j, j)

                evac(0, q_sb[:, bass.ds(b * L, L)])
                act.wait_ge(s["zb_ready"], b + 1)
                nc.scalar.activation(zabs[:, :], zb[:, :], ACT.Abs).then_inc(s["act_chain"], 1)
                next_rows(0)
                act.wait_ge(s["act_chain"], b * 2 + 1)
                nc.scalar.activation(zexp[:, :], zabs[:, :], ACT.Exp, scale=-1.0).then_inc(s["act_chain"], 1)
                evac(2, k_sb[:, bass.ds(b * L, L)])
                next_rows(1)
                act.wait_ge(s["act_chain"], b * 2 + 2)
                nc.scalar.activation(zln[:, :], zexp[:, :], ACT.Ln, bias=1.0).then_inc(s["zln_ready"], 1)
                next_rows(2)
                next_rows(3)
                evac(5, g_sb[:, 0, bass.ds(b * L, L)], func=ACT.Identity, bias=bgT[:, 0:1])
                evac(6, g_sb[:, 1, bass.ds(b * L, L)], func=ACT.Identity, bias=bgT[:, 1:2])
                act.wait_ge(s["zls_ready"], b + 2)
                nc.scalar.activation(a_sb[:, bass.ds(b * L, L)], zls[:, :], ACT.Exp, scale=1.0 / NORMALIZER)\
                    .then_inc(s["a_ready"], 1)

            for j in range(TPB):
                evac_rows(j, j)
            with act.Fori(0, B - 1) as b:
                turn(b, True)
            turn(B - 1, False)
            act.wait_ge(s["ex_in"], 1)
            nc.scalar.activation(ex[:, :, :], prod[:, :, :], ACT.Exp).then_inc(s["exp_ready"], 1)

            act.wait_ge(s["exp_ready"], 1)
            nc.scalar.preload_act_table(ACT.Silu)
            act.sem_inc(s["oT_evac"], 2)
            act.wait_ge(s["lg_ready"], 1)

            def step_fn(a, b, c, u):
                if c is not None and u < NF:
                    rows_m = FT[u][1]
                    act.wait_ge(s["gu_ready"], c * 2 * NF + (2 * u + 1))
                    act.wait_ge(s["hf_ready"], c * NF + (u + 1))
                    nc.scalar.activation(sg[0:rows_m, u % 2, :], M[2 * (u % 2)][0:rows_m, :], ACT.Silu).then_inc(s["sg_ready"], 1)
                if b is not None:
                    if u == 0:
                        wait(act, s["on_ready"], b)
                        for i in range(2):
                            act.wait_ge(s["tpo_ready"], b * 2 + (i + 1))
                            nc.scalar.activation(
                                ot[:, 2 * i:2 * i + 2, :].rearrange("p t (h d) -> p t d h", d=HD),
                                PS[i].rearrange("p (t d h) -> p t d h", t=2, d=HD), ACT.Copy).then_inc(s["ot_ready"], 1)
                        wait(act, s["tpb_ready"], b * 2)
                        act.wait_ge(s["oc_ready"], b + 1)
                        nc.scalar.activation(on[:, :, :], ot[:, :, :], ACT.Square).then_inc(s["sq_ready"], 1)
                    if u == 1:
                        wait(act, s["ogl_ready"], b * 2)
                        act.sem_inc(s["act_turn"], 1)
                        nc.scalar.activation(gs[:, :, :], g_sb[:, :, TOK(b)], ACT.Silu).then_inc(s["gs_ready"], 1)
                    if u == 3:
                        wait(act, s["wo_ready"], b * 2)
                        for i in range(2):
                            act.wait_ge(s["og_ready"], b * 2 + (i + 1))
                            nc.scalar.activation(og_h[:, i, :], gs[:, i, :], ACT.Copy).then_inc(s["ogh_ready"], 1)
                    if u == 5:
                        act.wait_ge(s["xb_ready"], b * 2 + 2)
                        act.sem_inc(s["act_turn"], 1)
                        for t in range(TPB):
                            nc.scalar.activation(ot[:, t, :], xn[:, TILES(b, t, 1), :].rearrange("p a d -> p (a d)"), ACT.Square,
                                                 accum_out=grow[3][:, t:t + 1]).then_inc(s["ms_ready"], 1)
                    if u == 6:
                        act.wait_ge(s["row_rstd"], b + 1)
                        wait(act, s["tpn_ready"], b * 4)
                        act.sem_inc(s["act_turn"], 1)
                        for t in range(TPB):
                            nc.scalar.activation(an2[:, t, 0, :], xn[:, TILES(b, t, 1), :].rearrange("p a d -> p (a d)"), ACT.Copy,
                                                 scale=grow[1][:, t:t + 1]).then_inc(s["an2h_ready"], 1)
                    if u == 7:
                        for part in range(2):
                            for i in range(KC):
                                act.wait_ge(s["tpn_ready"], b * 4 + (part * 2 + i + 1))
                                if part == 0 and i == 0:
                                    wait(act, s["gu_ready"], b * 2 * NF)
                                nc.scalar.activation(an2T[:, part, i, :], PS[i], ACT.Copy).then_inc(s["an2T_evac"], 1)
                if a is not None and u in (4, 7):
                    half = u == 7
                    act.wait_ge(s["gla_used"], a * U + (2 + (8 if half else 4)))
                    wait(act, s["tpo_ready"], a * 2)
                    nc.scalar.activation(oT[:, int(half), :], sum_ps[:, int(half), :], ACT.Copy).then_inc(s["oT_evac"], 1)
                if c is not None and u < NF:
                    act.wait_ge(s["hf_ready"], c * NF + (u + 3))
                    wait(act, s["w2_ready"], c * 2 + 1)
                    nc.scalar.activation(h_h[0:rows_m, u, :], hf[0:rows_m, u % 2, :], ACT.Copy).then_inc(s["hh_ready"], 1)

            turns(act, step_fn)
            act.wait_ge(s["act_turn"], 3 * B)

            attention_over(act)
            act.dma_start(wd[:, :, :, :].rearrange("p e i d -> p (e i) d"),
                          down_proj.rearrange("e (i p) d -> p (e i) d", p=HK)).then_inc(s["wd_in"], 16)
            act.sem_inc(s["he_ready"], 2)
            act.sem_inc(s["ye_ready"], 2)

            def tile_silu(g, u):
                t = g * UN
                act.wait_ge(s["eg_ready"], t + (u + 3))
                act.wait_ge(s["hm_ready"], t + (u + 1))
                nc.scalar.activation(sl[:, u % 2, :], M[u % 2][:, 0:I], ACT.Silu, scale=X[:, u, SCALE_C:SCALE_C + 1])\
                    .then_inc(s["sl_ready"], 1)

            def tile_rest(g, u):
                t = g * UN
                act.wait_ge(s["ht_ready"], t + (u + 3))
                act.wait_ge(s["dn_ready"], t + (u + 1))
                nc.scalar.activation(hT[:, u % 2, :, :], M[2 + u % 2][0:HK, 0:IC * P].rearrange("p (i n) -> p i n", i=IC),
                                     ACT.Copy).then_inc(s["he_ready"], 1)

            def tile_out(g, u):
                t = g * UN
                e = expert(act, t + u, u)
                act.wait_ge(s["dn_ready"], t + (u + 3))
                act.wait_ge(s["y_slots"], g * UN + (u + 3))
                act.sem_inc(s["act_turn3"], 1)
                nc.scalar.activation(y[:, u, :], sum_ps[:, u % 2, 0:D], ACT.Copy, scale=X[:, u, bass.ds(e + WEIGHT_C, 1)])\
                    .then_inc(s["ye_ready"], 1)

            def tiles(g, last):
                for u in range(UN):
                    tile_rest(g, u)
                    if not (last and u == UN - 1):
                        tile_silu(g + (u + 1) // UN, (u + 1) % UN)
                    tile_out(g, u)

            tile_silu(0, 0)
            with act.Fori(0, GROUPS - 1) as g:
                tiles(g, False)
            tiles(GROUPS - 1, True)
            act.wait_ge(s["act_turn3"], SLOT_TILES)
            for c in range(B):
                act.wait_ge(s["ysum_ready"], c + 1)
                nc.scalar.activation(ysum2[c], ysum[c], ACT.Silu).then_inc(s["silu_ready"], 1)

        @block.vector
        def _(dve):
            step = sem_chain(dve, s["dve_chain"], 0)
            dve.wait_ge(s["const_pool"], 1)
            step(nc.vector.tensor_scalar(head_m[:, :], head_i[:, :], H - 1, None, ALU.bitwise_and))
            nc.vector.tensor_scalar(sumk[:, P - H:P], head_m[:, :], 0.0, None, ALU.is_equal).then_inc(s["const_dve"], 1)
            for c in range(B):
                dve.wait_ge(xq[c], 16)
                with dve.Fori(c * TPB, (c + 1) * TPB) as t:
                    nc.vector.bn_stats(bst[:, bass.ds(t, 1), :].rearrange("p a d -> p (a d)"),
                                       xn[:, bass.ds(t, 1), :].rearrange("p a d -> p (a d)")).then_inc(s["stats"], 1)
            dve.wait_ge(s["stats"], NT)
            for t in range(NT):
                nc.vector.bn_aggr(mv[:, t, :], bst[:, t, :]).then_inc(s["stats"], 1)
            dve.wait_ge(s["stats"], 2 * NT)
            mean, var = mv[:, :, 0], mv[:, :, 1]
            step(nc.vector.tensor_scalar(rs_v[:, 0, :], var, EPS, None, ALU.add))
            rsqrt_seed(step, rstd[:, :], rs_v[:, 0, :]).then_inc(s["rsq_seed"], 1)
            dve.wait_ge(s["rsq_done1"], 1)
            step(nc.vector.tensor_tensor(rs_v[:, 2, :], rstd[:, :], rstd[:, :], ALU.mult))
            step(nc.vector.tensor_tensor(rs_v[:, 2, :], rs_v[:, 2, :], var, ALU.mult))
            step(nc.vector.tensor_scalar(rs_v[:, 2, :], rs_v[:, 2, :], EPS, None, ALU.add))
            rsqrt_seed(step, r1[:, :], rs_v[:, 2, :]).then_inc(s["rsq_seed2"], 1)
            step(nc.vector.scalar_tensor_tensor(out=negmr[:, :], in0=mean, scalar=-1.0, in1=rstd[:, :],
                                                op0=ALU.mult, op1=ALU.mult))
            with dve.Fori(0, NT) as t:
                xt = xn[:, bass.ds(t, 1), :].rearrange("p a d -> p (a d)")
                nc.vector.tensor_scalar(xt, xt, rstd[:, bass.ds(t, 1)], negmr[:, bass.ds(t, 1)],
                                        ALU.mult, ALU.add).then_inc(s["xn_ready"], 1)
            dve.wait_ge(s["small_in"], 16 * NSMALL)
            nc.vector.tensor_scalar(ln1k[:, :], ln1[:, :], KS, None, ALU.mult).then_inc(s["ln1k_ready"], 1)
            dve.wait_ge(s["wk1_t"], 1)
            nc.vector.tensor_copy(wk1T[:, :, :], WK1p).then_inc(s["wk1_copied"], 1)
            dve.wait_ge(s["ln1k_ready"], 1)
            n = 0
            for c in range(KC):
                for (lo_ap, in_ap, scale), (hi_ap, _, _) in zip(wparts(c, 1), wparts(c, 0)):
                    n += 1
                    dve.wait_ge(s["wprep_act"], n)
                    nc.vector.scalar_tensor_tensor(out=lo_ap, in0=in_ap, scalar=scale, in1=hi_ap,
                                                   op0=ALU.mult, op1=ALU.subtract).then_inc(s["wprep_dve"], 1)
            n += KC
            dve.wait_ge(s["wprep_act"], n)
            for c in range(KC):
                nc.vector.scalar_tensor_tensor(out=hk_view(w_a[:, 1, c, ZC:ZC + QK], False), in0=hk_view(Zp[:, c, :], True),
                                               scalar=ln1[:, c:c + 1], in1=hk_view(w_a[:, 0, c, ZC:ZC + QK], False),
                                               op0=ALU.mult, op1=ALU.subtract).then_inc(s["wprep_dve"], 1)
            dve.wait_ge(s["wprep_act"], n + 1)
            nc.vector.tensor_tensor(rw[:, 1, :, :], RWp, rw[:, 0, :, :], ALU.subtract).then_inc(s["wprep_dve"], 1)
            dve.wait_ge(s["rsq_done2"], 1)
            with dve.Fori(0, NT) as t:
                dve.wait_ge(s["anh_ready"], t + 1)
                nc.vector.scalar_tensor_tensor(
                    out=rows16[:, bass.ds(t, 1), D:2 * D].rearrange("p a d -> p (a d)"),
                    in0=xn[:, bass.ds(t, 1), :].rearrange("p a d -> p (a d)"), scalar=r1[:, bass.ds(t, 1)],
                    in1=rows16[:, bass.ds(t, 1), 0:D].rearrange("p a d -> p (a d)"),
                    op0=ALU.mult, op1=ALU.subtract).then_inc(s["anl_ready"], 1)
            cview = rows[:, :, SCALE_C:SCALE_C + 1]
            nc.vector.tensor_tensor(cview, rs_v[:, 2, :].rearrange("p (t a) -> p t a", a=1),
                                    r1[:, :].rearrange("p (t a) -> p t a", a=1), ALU.mult).then_inc(s["cscale"], 1)
            dve.sem_inc(s["evac_dve"], 2)
            dve.sem_inc(s["zls_ready"], 1)
            with dve.Fori(0, B) as b:
                dve.wait_ge(s["zls_ready"], b + 1)
                dve.wait_ge(s["proj_ready"], b * 7 + 2)
                nc.vector.tensor_scalar(zb[:, :], M[1], bz[:, 0:1], None, ALU.add).then_inc(s["evac_dve"], 1)
                dve.wait_ge(s["evac_dve"], b * 3 + 3)
                dve.sem_inc(s["zb_ready"], 1)
                for c in range(2):
                    dve.wait_ge(s["proj_ready"], b * 7 + (4 + c))
                    dve.wait_ge(vt_out[c], b * 16 + 16)
                    nc.vector.tensor_copy(vt[:, c, :], M[(3 + c) % 4]).then_inc(s["evac_dve"], 1)
                    dve.wait_ge(s["evac_dve"], b * 3 + (4 + c))
                    dve.sem_inc(s["vt_ready"], 1)
                dve.wait_ge(s["zln_ready"], b + 1)
                nc.vector.scalar_tensor_tensor(out=zls[:, :], in0=zb[:, :], scalar=0.0, in1=zln[:, :],
                                               op0=ALU.min, op1=ALU.subtract).then_inc(s["zls_ready"], 1)
            dve.wait_ge(s["logits_ready"], NT)
            dve.wait_ge(s["cscale"], 1)
            cb = cview.to_broadcast((P, NT, E))
            LG = O1[:, 0:NT * E].rearrange("p (t e) -> p t e", e=E)
            dve.wait_ge(s["proj_ready"], 7 * B)
            dve.wait_ge(s["a_ready"], B)
            dve.wait_ge(s["prep_done"], 1)
            for c in range(2):
                dve.wait_ge(vt_out[c], 16 * (B + 1))
            nc.vector.tensor_tensor(lg[:, :, :], LG, cb, ALU.mult).then_inc(s["lg_ready"], 1)
            dve.wait_ge(s["lg_ready"], 1)
            step(nc.vector.tensor_tensor(lg[:, :, :], lg[:, :, :],
                                         eb[:, :].rearrange("p (a e) -> p a e", a=1).to_broadcast((P, NT, E)), ALU.add))
            nc.vector.tensor_reduce(mx[:, :], lg[:, :, :], AX.X, ALU.max).then_inc(s["dve_max"], 1)
            for t in range(NT):
                nc.vector.max(m8[:, t, :], lg[:, t, :]).then_inc(s["dve_max"], 1)
            dve.wait_ge(s["dve_max"], NT + 1)
            un = lambda ap: ap.rearrange("p (t a) -> p t a", a=1).to_broadcast((P, NT, E))
            flat = lambda ap: ap.rearrange("p t e -> p (t e)")
            nc.vector.tensor_tensor(prod[:, :, :], lg[:, :, :], un(mx[:, :]), ALU.subtract).then_inc(s["ex_in"], 1)
            v4 = m8[:, :, TOP - 1:TOP].to_broadcast((P, NT, E))
            step(nc.vector.tensor_tensor(gt[:, :, :], lg[:, :, :], v4, ALU.is_gt))
            step(nc.vector.tensor_tensor(eq[:, :, :], lg[:, :, :], v4, ALU.is_equal))
            step(nc.vector.tensor_reduce(need[:, :], gt[:, :, :], AX.X, ALU.add))
            step(nc.vector.tensor_scalar(need[:, :], need[:, :], -1.0, float(TOP), ALU.mult, ALU.add))
            step(nc.vector.tensor_tensor_scan(flat(eqc[:, :, :]), flat(restart[:, :, :]), flat(eq[:, :, :]), 0.0,
                                              ALU.mult, ALU.add))
            step(nc.vector.tensor_tensor(eqc[:, :, :], eqc[:, :, :], un(need[:, :]), ALU.is_le))
            step(nc.vector.tensor_tensor(eq[:, :, :], eq[:, :, :], eqc[:, :, :], ALU.mult))
            step(nc.vector.tensor_tensor(Msel[:, :, :], gt[:, :, :], eq[:, :, :], ALU.add))
            nc.vector.tensor_copy(M16[:, :, :], Msel[:, :, :]).then_inc(s["m16_ready"], 1)
            dve.wait_ge(s["exp_ready"], 1)
            step(nc.vector.tensor_tensor(wgt[:, :, :], ex[:, :, :], Msel[:, :, :], ALU.mult))
            step(nc.vector.tensor_reduce(sm[:, :], wgt[:, :, :], AX.X, ALU.add))
            step(nc.vector.reciprocal(sm[:, :], sm[:, :]))
            step(nc.vector.tensor_tensor(rows[:, :, WEIGHT_C:ROW], wgt[:, :, :], un(sm[:, :]), ALU.mult))
            dve.wait_ge(s["cum_ready"], 1)
            CUM = O0[:, 0:NT * E].rearrange("p (t e) -> p t e", e=E)
            TOT = O0[:, NT * E:2 * NT * E].rearrange("p (t e) -> p e t", e=E)
            step(nc.vector.tensor_copy(tot[:, :, :], TOT))
            step(nc.vector.tensor_tensor_scan(flat(inc[:, :, :]), flat(restart[:, :, :]), flat(tot[:, :, :]), 0.0,
                                              ALU.mult, ALU.add))
            step(nc.vector.tensor_tensor(over[:, :, :], inc[:, :, NT - 1:NT].to_broadcast((P, E, NT)),
                                         steps128[:, :, :], ALU.is_gt))
            step(nc.vector.tensor_reduce(ntl[:, :], over[:, :, :], AX.X, ALU.add))
            step(nc.vector.tensor_tensor_scan(ntc[:, :], one_e[:, :], ntl[:, :], 0.0, ALU.mult, ALU.add))
            step(nc.vector.tensor_tensor(base[:, :], ntc[:, :], ntl[:, :], ALU.subtract))
            step(nc.vector.tensor_scalar(base[:, :], base[:, :], float(P), None, ALU.mult))
            step(nc.vector.tensor_tensor(inc[:, :, :], inc[:, :, :], tot[:, :, :], ALU.subtract))
            step(nc.vector.tensor_tensor(slot[:, :, :], CUM, inc[:, :, :].rearrange("p e t -> p t e"), ALU.add))
            step(nc.vector.tensor_tensor(slot[:, :, :], slot[:, :, :],
                                         base[:, :].rearrange("p (a e) -> p a e", a=1).to_broadcast((P, NT, E)), ALU.add))
            step(nc.vector.tensor_tensor_scan(flat(cnt[:, :, :]), flat(restart[:, :, :]), flat(Msel[:, :, :]), 0.0,
                                              ALU.mult, ALU.add))
            for j in range(TOP):
                step(nc.vector.scalar_tensor_tensor(out=pick[:, :, :], in0=cnt[:, :, :], scalar=float(j + 1),
                                                    in1=Msel[:, :, :], op0=ALU.is_equal, op1=ALU.mult))
                step(nc.vector.tensor_tensor(prod[:, :, :], pick[:, :, :], slot[:, :, :], ALU.mult))
                step(nc.vector.tensor_reduce(slot_f[:, j, :], prod[:, :, :], AX.X, ALU.add))
            step(nc.vector.tensor_copy(slot_u[:, :, :], slot_f[:, :, :]))
            step(nc.vector.tensor_tensor(owner[:, :, :],
                                         ntc[0:1, :].rearrange("p (a e) -> p a e", a=1).to_broadcast((1, SLOT_TILES, E)),
                                         tile_no[:, :].rearrange("p (t a) -> p t a", a=1).to_broadcast((1, SLOT_TILES, E)),
                                         ALU.is_le))
            step(nc.vector.tensor_reduce(own1[:, :], owner[:, :, :], AX.X, ALU.add))
            nc.vector.tensor_scalar(tile_expert[:, 0:SLOT_TILES], own1[:, :], float(E - 1), None, ALU.min)\
                .then_inc(s["route_ready"], 1)

            dve.wait_ge(s["route_ready"], 1)
            dve.sem_inc(s["kv_ready"], 2)
            dve.sem_inc(s["st_ready"], 4)
            dve.sem_inc(s["hf_ready"], 2)
            dve.sem_inc(s["hl_ready"], 2)
            dve.sem_inc(s["xc_ready"], 2)

            def low_h(c, m):
                rows_m = FT[m][1]
                dve.wait_ge(s["hh_ready"], c * NF + (m + 1))
                nc.vector.tensor_tensor(h_l[0:rows_m, m, :], hf[0:rows_m, m % 2, :], h_h[0:rows_m, m, :].bitcast(F32),
                                        ALU.subtract).then_inc(s["hl_ready"], 1)

            def step_fn(a, b, c, u):
                if a is not None:
                    r = u % 2
                    dve.wait_ge(vr_in[r], a * 16 * U + 32 * (u // 2 + 1))
                    dve.wait_ge(s["st_ready"], a * 2 * U + (2 * u + 2))
                    nc.vector.tensor_tensor(kv[:, r, :, :], vrep[:, r, :, :], pair_bc(k_sb[:, TOK(a)]),
                                            ALU.mult).then_inc(s["kv_ready"], 1)
                    dve.wait_ge(s["kv_ready"], a * U + (u + 3))
                    dve.wait_ge(s["qs_ready"], a * U + (u + 1))
                    for j in range(2):
                        nc.vector.tensor_tensor_scan(st[:, r, j, :], a_sb[:, TOK(a)], kv[:, r, j, :], 0.0,
                                                     ALU.mult, ALU.add).then_inc(s["st_ready"], 1)
                if b is not None:
                    if u == 0:
                        chain = sem_chain(dve, s["head_dve"], 0, 5, b)
                        dve.wait_ge(s["ot_ready"], b * 2 + 2)
                        ot_h = ot[:, :, :].rearrange("p t (h d) -> p (t h) d", d=HD)
                        chain(nc.vector.tensor_reduce(ghead[3][:, :], ot_h, AX.X, ALU.add))
                        chain(nc.vector.tensor_scalar(ghead[3][:, :], ghead[3][:, :], 1.0 / HD, None, ALU.mult))
                        nc.vector.tensor_tensor(ot_h, ot_h,
                                                ghead[3][:, :].rearrange("p (g a) -> p g a", a=1).to_broadcast((P, TPB * H, HD)),
                                                ALU.subtract).then_inc(s["oc_ready"], 1)
                    if u == 1:
                        chain = sem_chain(dve, s["head_dve"], 2, 5, b)
                        dve.wait_ge(s["sq_ready"], b + 1)
                        chain(nc.vector.tensor_reduce(ghead[0][:, :], on[:, :, :].rearrange("p t (h d) -> p (t h) d", d=HD),
                                                      AX.X, ALU.add))
                        chain(nc.vector.tensor_scalar(ghead[0][:, :], ghead[0][:, :], 0.5 / HD, 0.5 * EPS, ALU.mult, ALU.add))
                        rsqrt_seed(chain, ghead[1][:, :], ghead[0][:, :], HALF_MAGIC).then_inc(s["head_seed"], 1)
                    if u == 2:
                        dve.wait_ge(s["head_rstd"], b + 1)
                        for t in range(TPB):
                            nc.vector.tensor_tensor(
                                on[:, t, :].rearrange("p (d h) -> p h d", d=HD), ot[:, t, :].rearrange("p (h d) -> p h d", d=HD),
                                ghead[1][:, t * H:(t + 1) * H].rearrange("p (h a) -> p h a", a=1).to_broadcast((P, H, HD)),
                                ALU.mult).then_inc(s["on_ready"] if t == TPB - 1 else s["on_part"], 1)
                        dve.wait_ge(s["on_part"], b * (TPB - 1) + (TPB - 1))
                    if u == 3:
                        dve.wait_ge(s["gs_ready"], b + 1)
                        for i in range(2):
                            dve.wait_ge(s["tpb_ready"], b * 2 + (i + 1))
                            nc.vector.tensor_tensor(gs[:, i, :], PS[i], gs[:, i, :], ALU.mult).then_inc(s["og_ready"], 1)
                    if u == 4:
                        for i in range(2):
                            dve.wait_ge(s["ogh_ready"], b * 2 + (i + 1))
                            nc.vector.tensor_tensor(og_l[:, i, :], gs[:, i, :], og_h[:, i, :].bitcast(F32),
                                                    ALU.subtract).then_inc(s["ogl_ready"], 1)
                    if u == 5:
                        for i in range(2):
                            dve.wait_ge(s["wo_ready"], b * 2 + (i + 1))
                            xt = xn[:, TILES(b, 2 * i, 2), :].rearrange("p t d -> p (t d)")
                            nc.vector.tensor_tensor(xt, PS[i], xt, ALU.add).then_inc(s["xb_ready"], 1)
                    if u == 6:
                        chain = sem_chain(dve, s["row_dve"], 0, 2, b)
                        dve.wait_ge(s["ms_ready"], b * 4 + 4)
                        chain(nc.vector.tensor_scalar(grow[0][:, :], grow[3][:, :], 0.5 / D, 0.5 * EPS, ALU.mult, ALU.add))
                        rsqrt_seed(chain, grow[1][:, :], grow[0][:, :], HALF_MAGIC).then_inc(s["row_seed"], 1)
                    if u == 7:
                        for t in range(TPB):
                            dve.wait_ge(s["an2h_ready"], b * 4 + (t + 1))
                            nc.vector.scalar_tensor_tensor(
                                out=an2[:, t, 1, :], in0=xn[:, TILES(b, t, 1), :].rearrange("p a d -> p (a d)"), scalar=grow[1][:, t:t + 1],
                                in1=an2[:, t, 0, :], op0=ALU.mult, op1=ALU.subtract).then_inc(s["an2l_ready"], 1)
                if c is not None:
                    if 1 <= u <= NF:
                        low_h(c, u - 1)
                    if u < NF:
                        rows_m = FT[u][1]
                        dve.wait_ge(s["sg_ready"], c * NF + (u + 1))
                        dve.wait_ge(s["gu_ready"], c * 2 * NF + (2 * u + 2))
                        dve.wait_ge(s["hl_ready"], c * NF + (u + 1))
                        nc.vector.tensor_tensor(hf[0:rows_m, u % 2, :], M[2 * (u % 2) + 1][0:rows_m, :], sg[0:rows_m, u % 2, :],
                                                ALU.mult).then_inc(s["hf_ready"], 1)
                    if u == 7:
                        for i in range(2):
                            dve.wait_ge(s["w2_ready"], c * 2 + (i + 3))
                            xt = xn[:, TILES(c, 2 * i, 2), :].rearrange("p t d -> p (t d)")
                            nc.vector.tensor_tensor(xt, M[i], xt, ALU.add).then_inc(s["xc_ready"], 1)

            turns(dve, step_fn)

            attention_over(dve)
            dve.sem_inc(s["xe_ready"], 2)
            dve.sem_inc(s["hm_ready"], 2)

            def rows_out(g, u):
                dve.wait_ge(s["xt_ready"], g * UN + (u + 1))
                dve.wait_ge(s["eg_ready"], g * UN + (u + 1))
                nc.vector.tensor_copy(xT[:, u % 2, :, :, :].rearrange("p a c n -> p (a c n)"), PS[u % 2]).then_inc(s["xe_ready"], 1)

            def hidden(g, u):
                dve.wait_ge(s["sl_ready"], g * UN + (u + 1))
                dve.wait_ge(s["ht_ready"], g * UN + (u + 1))
                nc.vector.scalar_tensor_tensor(out=h[:, u % 2, :], in0=M[u % 2][:, I:2 * I], scalar=X[:, u, SCALE_C:SCALE_C + 1],
                                               in1=sl[:, u % 2, :], op0=ALU.mult, op1=ALU.mult).then_inc(s["hm_ready"], 1)

            def tiles(g, last):
                for u in range(UN):
                    hidden(g, u)
                    if not (last and u >= UN - 2):
                        rows_out(g + (u + 2) // UN, (u + 2) % UN)

            rows_out(0, 0)
            rows_out(0, 1)
            with dve.Fori(0, GROUPS - 1) as g:
                tiles(g, False)
            tiles(GROUPS - 1, True)
            for c in range(B):
                dve.wait_ge(fin_in[c], 32)
                nc.vector.tensor_tensor(ysum[c], ysum[c], ysum2[c], ALU.add).then_inc(s["ysum_ready"], 1)
            dve.wait_ge(s["xr_in"], 16 * B)
            for c in range(B):
                dve.wait_ge(s["silu_ready"], c + 1)
                nc.vector.tensor_tensor(ysum[c], ysum2[c], xn[:, c * TPB:(c + 1) * TPB, :].rearrange("p t d -> p (t d)"),
                                        ALU.mult).then_inc(s["fin_mul"], 1)
                dve.wait_ge(s["fin_mul"], c + 1)
                nc.vector.tensor_tensor(ysum[c], ysum[c], xback[c], ALU.add).then_inc(s["out_ready"], 1)

        @block.tensor
        def _(pe):
            pe.wait_ge(s["const_pool"], 1)
            pe.wait_ge(s["wz_in"], 48)
            for c in range(KC):
                last = nc.tensor.transpose(WK1p[:, c, :], wk1[:, c, :], ident[:, :])
            last.then_inc(s["wk1_t"], 1)
            for c in range(KC):
                last = nc.tensor.transpose(RWp[:, c, :], rw_raw[:, c * P:(c + 1) * P], ident[0:E, 0:E])
            last.then_inc(s["rw_t"], 1)
            pe.wait_ge(s["wk1_copied"], 1)
            for c in range(KC):
                last = nc.tensor.matmul(Zp[:, c, :], wk1T[:, c, :], wk2[:, :], start=True, stop=True)
            last.then_inc(s["wz_ready"], 1)
            pe.wait_ge(s["wprep_dve"], NWPREP)

            def turn_rows(t, j):
                pe.wait_ge(s["anl_ready"], t + 1)
                pe.wait_ge(s["tp_evac"], t + 1)
                for n in range(2 * KC):
                    last = nc.tensor.matmul(PS[j % 2][:, n * P:(n + 1) * P],
                                            rows16[:, bass.ds(t, 1), n * P:(n + 1) * P].rearrange("p a d -> p (a d)"),
                                            ident16[:, :], start=True, stop=True)
                last.then_inc(s["tp_ready"], 1)

            def turn(b, more):
                cols = [QC, ZC, KCOL, VC, VC + P, GC, GC + P]
                free = [(s["evac_dve"], b * 3 + 2), (s["evac_act"], b * 4 + 1), (s["evac_act"], b * 4 + 2),
                        (s["evac_dve"], b * 3 + 1), (s["evac_act"], b * 4 + 3), (s["evac_dve"], b * 3 + 3),
                        (s["evac_act"], b * 4 + 4)]
                pe.wait_ge(s["tp_evac"], b * TPB + TPB + 2)
                for i, col in enumerate(cols):
                    pe.wait_ge(*free[i])
                    triple(pe, M[i % 4],
                           [(w_a[:, wl, c, col:col + P], anT[:, hl, c, bass.ds(b * L, L)])
                            for c in range(KC) for hl, wl in ((0, 0), (0, 1), (1, 0))]).then_inc(s["proj_ready"], 1)
                    if i < TPB:
                        t = b * TPB + i
                        triple(pe, O1[:, bass.ds(t * E, E)],
                               [(anT[:, hl, c, bass.ds(t * P, P)], rw[:, wl, c, :])
                                for c in range(KC) for hl, wl in ((0, 0), (0, 1), (1, 0))]).then_inc(s["logits_ready"], 1)
                        if more:
                            turn_rows((b + 1) * TPB + i, i)

            for j in range(TPB):
                turn_rows(j, j)
            with pe.Fori(0, B - 1) as b:
                turn(b, True)
            turn(B - 1, False)
            pe.wait_ge(s["m16_ready"], 1)
            sel = M16[:, :, :].rearrange("p t e -> p (t e)")
            nc.tensor.matmul(O0[:, 0:NT * E], before16[:, :], sel, start=True, stop=True)
            nc.tensor.matmul(O0[:, NT * E:2 * NT * E], ones16[:, :], sel, start=True, stop=True).then_inc(s["cum_ready"], 1)

            pe.wait_ge(s["lg_ready"], 1)
            pe.wait_ge(s["evac_dve"], 3 * B + 2)
            pe.wait_ge(s["evac_act"], 4 * B + 2)
            pe.sem_inc(s["gla_used"], 2)
            pe.sem_inc(s["w2_ready"], 2)

            def read_out(a, u):
                pe.wait_ge(s["qs_ready"], a * U + (u + 3))
                if u % 4 == 0:
                    pe.wait_ge(s["oT_evac"], a * 2 + (u // 4 + 1))
                for j in range(2):
                    dd = (2 * u + j) % DH
                    off = P - H - dd * H
                    last = nc.tensor.matmul(sum_ps[:, u // 4, :], sumk[:, off:off + P], qs[:, u % 2, j, :],
                                            start=(dd == 0), stop=(dd == DH - 1))
                last.then_inc(s["gla_used"], 1)

            def step_fn(a, b, c, u):
                if c is not None and u < NF:
                    f, rows_m = FT[u]
                    if u == 0:
                        pe.wait_ge(s["an2T_evac"], c * 4 + 4)
                        pe.wait_ge(s["xc_ready"], c * 2 + 2)
                    pe.wait_ge(s["hf_ready"], c * NF + (u + 1))
                    for i in range(2):
                        triple(pe, M[2 * (u % 2) + i][0:rows_m, :],
                               [(w13[:, wl, kc, i * F + f:i * F + f + rows_m], an2T[:, hl, kc, :])
                                for kc in range(KC) for hl, wl in ((0, 0), (0, 1), (1, 0))]).then_inc(s["gu_ready"], 1)
                if a is not None and u > 0:
                    read_out(a, u - 1)
                if b is not None:
                    if u == 0:
                        wait(pe, s["an2T_evac"], b * 4)
                        for i in range(2):
                            for n in range(4):
                                t, kc = 2 * i + n // 2, n % 2
                                pe.wait_ge(s["oT_evac"], b * 2 + (kc + 3))
                                last = nc.tensor.transpose(PS[i][:, n * P:(n + 1) * P], oT[:, kc, t * P:(t + 1) * P], ident[:, :])
                            last.then_inc(s["tpo_ready"], 1)
                    if u == 2:
                        pe.wait_ge(s["on_ready"], b + 1)
                        for i in range(2):
                            for t in range(TPB):
                                last = nc.tensor.transpose(PS[i][:, t * P:(t + 1) * P], on[:, t, i * P:(i + 1) * P], ident[:, :])
                            last.then_inc(s["tpb_ready"], 1)
                    if u == 4:
                        pe.wait_ge(s["ogl_ready"], b * 2 + 2)
                        for t in range(TPB):
                            last = triple(pe, PS[t // 2][:, (t % 2) * D:(t % 2 + 1) * D],
                                          [(og[:, kc, t * P:(t + 1) * P], wo[:, kc, :])
                                           for kc in range(KC) for og, wo in ((og_h, wo_h), (og_h, wo_l), (og_l, wo_h))])
                            if t % 2:
                                last.then_inc(s["wo_ready"], 1)
                    if u == 7:
                        pe.wait_ge(s["an2l_ready"], b * 4 + 4)
                        for part in range(2):
                            for i in range(KC):
                                if part:
                                    pe.wait_ge(s["an2T_evac"], b * 4 + (i + 1))
                                for t in range(TPB):
                                    last = nc.tensor.matmul(PS[i][:, t * P:(t + 1) * P], an2[:, t, part, i * P:(i + 1) * P],
                                                            ident16[:, :], start=True, stop=True)
                                last.then_inc(s["tpn_ready"], 1)
                if c is not None and u >= NF:
                    pe.wait_ge(s["hl_ready"], c * NF + (NF + 2))
                    for t in (2 * (u - NF), 2 * (u - NF) + 1):
                        last = triple(pe, M[u - NF][:, (t % 2) * D:(t % 2 + 1) * D],
                                      [(h[0:mw, m, t * P:(t + 1) * P], w[0:mw, m, :])
                                       for m, (_, mw) in enumerate(FT)
                                       for h, w in ((h_h, w2_h), (h_h, w2_l), (h_l, w2_h))])
                    last.then_inc(s["w2_ready"], 1)
                if a is not None and u == U - 1:
                    read_out(a, u)

            turns(pe, step_fn)

            attention_over(pe)
            pe.sem_inc(s["eg_ready"], 2)
            pe.sem_inc(s["ht_ready"], 2)
            pe.sem_inc(s["dn_ready"], 2)

            def transpose_rows(g, u):
                pe.wait_ge(x_in[u], 16 * (g + 1))
                pe.wait_ge(s["xe_ready"], g * UN + (u + 1))
                for n in range(2 * KC):
                    last = nc.tensor.matmul(PS[u % 2][:, n * P:(n + 1) * P], X16[:, u, n * P:(n + 1) * P], ident16[:, :],
                                            start=True, stop=True)
                last.then_inc(s["xt_ready"], 1)

            def gate_up(g, u):
                e = expert(pe, g * UN + u, u)
                pe.wait_ge(s["ew_ready"], e + 1)
                pe.wait_ge(s["xe_ready"], g * UN + (u + 3))
                pe.wait_ge(s["hm_ready"], g * UN + (u + 1))
                triple(pe, M[u % 2][:, 0:2 * I],
                       [(xT[:, u % 2, hl, kc, :], w_gu[:, bass.ds(e, 1), wl, kc, :].rearrange("p a n -> p (a n)"))
                        for kc in range(KC) for hl, wl in ((0, 0), (0, 1), (1, 0))]).then_inc(s["eg_ready"], 1)

            def transpose_hidden(g, u):
                pe.wait_ge(s["hm_ready"], g * UN + (u + 3))
                pe.wait_ge(s["he_ready"], g * UN + (u + 1))
                for i in range(IC):
                    last = nc.tensor.transpose(M[2 + u % 2][0:HK, i * P:(i + 1) * P], h[:, u % 2, i * HK:(i + 1) * HK], ident[:, :])
                last.then_inc(s["ht_ready"], 1)

            def down(g, u):
                e = expert(pe, g * UN + u, u)
                pe.wait_ge(s["he_ready"], g * UN + (u + 3))
                pe.wait_ge(s["ye_ready"], g * UN + (u + 1))
                triple(pe, sum_ps[:, u % 2, 0:D],
                       [(hT[:, u % 2, i, :], wd[:, bass.ds(e, 1), i, :].rearrange("p a n -> p (a n)")) for i in range(IC)])\
                    .then_inc(s["dn_ready"], 1)

            def tiles(g, last):
                for u in range(UN):
                    if not (last and u >= UN - 2):
                        transpose_rows(g + (u + 2) // UN, (u + 2) % UN)
                    transpose_hidden(g, u)
                    if not (last and u == UN - 1):
                        gate_up(g + (u + 1) // UN, (u + 1) % UN)
                    down(g, u)

            transpose_rows(0, 0)
            transpose_rows(0, 1)
            gate_up(0, 0)
            pe.wait_ge(s["wd_in"], 16)
            with pe.Fori(0, GROUPS - 1) as g:
                tiles(g, False)
            tiles(GROUPS - 1, True)


_INS = [f"L0_attn_{n}" for n in ("x", "Wq", "Wk", "Wkg1", "Wkg2", "bkg2", "Wv", "Wg", "bg", "Wo", "ln1_w", "ln2_w",
                                 "W1", "W3", "W2")] + \
       [f"L0_ffn_{n}" for n in ("router_w", "expert_bias", "gate_proj", "up_proj", "down_proj")]
_OUTS = [((4, 512, 256), "float32")]


def kernel(**inputs):
    import numpy as _np
    import concourse.bacc as _bacc
    from concourse import mybir as _mybir
    from concourse.bass_utils import run_bass_kernel_spmd as _run

    nc = _bacc.Bacc("TRN2", target_bir_lowering=False, num_devices=1)
    arrays, args = {}, []
    for name in _INS:
        a = _np.ascontiguousarray(inputs[name])
        arrays[f"in_{name}_dram"] = a
        args.append(nc.dram_tensor(f"in_{name}_dram", a.shape, _mybir.dt.from_np(a.dtype), kind="ExternalInput").ap())
    for i, (shape, dtype) in enumerate(_OUTS):
        dt = _mybir.dt.from_np(_np.dtype(dtype))
        args.append(nc.dram_tensor(f"out_{i}_dram", shape, dt, kind="ExternalOutput").ap())
    build_block(nc, *args)
    r = _run(nc, [arrays], core_ids=[0])
    return r.results[0]["out_0_dram"]
```

```python
from contextlib import ExitStack

import concourse.bass as bass
from concourse import mybir

F32 = mybir.dt.float32
F32R = mybir.dt.float32r
F16 = mybir.dt.float16
I32 = mybir.dt.int32
U32 = mybir.dt.uint32
ALU = mybir.AluOpType
ACT = mybir.ActivationFunctionType
AX = mybir.AxisListType

P = 128
EPS = 1e-5
RSQRT_MAGIC = 0x5F3759DF
HALF_MAGIC = RSQRT_MAGIC - 0x400000
NEWTON = 3


def sem_chain(eng, sem, base, per=0, it=0, between=None):
    count = [base]

    def step(ins):
        if ins is None:
            return count[0]
        count[0] += 1
        ins.then_inc(sem, 1)
        if between:
            between()
        eng.wait_ge(sem, it * per + count[0])
        return count[0]

    return step


def build_block(nc, x, Wq, Wk, Wkg1, Wkg2, bkg2, Wv, Wg, bg, Wo, ln1_w, ln2_w, W1, W3, W2,
                router_w, expert_bias, gate_proj, up_proj, down_proj, out):
    B, L, D = x.shape
    T = B * L
    NT = T // P
    TPB = L // P
    KC = D // P
    E, _, I = gate_proj.shape
    F = W1.shape[1]
    QK = Wq.shape[1]
    R = Wkg1.shape[1]
    H = 16
    KD = QK // H
    HD = D // H
    DH = HD // KC
    KS = float(HD) ** -0.5
    NORMALIZER = 16.0
    TOP = 4
    SLOT_TILES = -(-(T * TOP // P + E - 1) // 4) * 4
    SLOTS = SLOT_TILES * P
    ROW = D + 2 + E
    SCALE_C, TOKEN_C, WEIGHT_C = D, D + 1, D + 2
    HK = I // 2
    IC = 2
    assert QK == P and D == 2 * P and B * H * KD * HD == 4 * P * HD and L == 512

    QC, KCOL, ZC, VC, GC = 0, QK, 2 * QK, 3 * QK, 3 * QK + D
    WA = 3 * QK + 2 * D
    FT = [(c * P, min(P, F - c * P)) for c in range((F + P - 1) // P)]
    NF = len(FT)

    xr = x.rearrange("b l d -> (b l) d").rearrange("(t p) d -> p t d", p=P)
    outr = out.rearrange("b l d -> (b l) d").rearrange("(t p) d -> p t d", p=P)

    v_dram = nc.dram_tensor("v_scratch", (B, HD, H, L), F32, kind="Internal").ap()
    rows_dram = nc.dram_tensor("rows_scratch", (SLOTS, ROW), F32, kind="Internal").ap()
    y_dram = [nc.dram_tensor(f"y_scratch{i}", (T + P, D), F32, kind="Internal").ap() for i in range(2)]

    with ExitStack() as ctx:
        def sem(name):
            return ctx.enter_context(nc.semaphore(name))

        def sb(name, shape, dt, scope=ctx):
            return scope.enter_context(nc.sbuf_tensor(name, shape, dt))

        xn = sb("xn", [P, NT, D], F32)
        ident = sb("ident", [P, P], F32)
        ident16 = sb("ident16", [P, P], F16)
        slot_u = sb("slot_u", [P, TOP, NT], U32)
        tile_expert = sb("tile_expert", [1, SLOT_TILES], U32)

        ones16 = sb("ones16", [P, P], F16)
        before16 = sb("before16", [P, P], F16)
        sumk = sb("sumk", [P, 2 * P - H], F32)
        head_i = sb("head_i", [P, H], I32)
        head_m = sb("head_m", [P, H], I32)
        restart = sb("restart", [P, NT, E], F32)
        one_e = sb("one_e", [P, E], F32)
        steps128 = sb("steps128", [P, E, NT], F32)
        tile_no = sb("tile_no", [1, SLOT_TILES], F32)
        c15 = sb("c15", [P, TPB * H], F32)
        ln1 = sb("ln1", [P, KC], F32)
        ln1k = sb("ln1k", [P, KC], F32)
        ln2 = sb("ln2", [P, KC], F32)
        bz = sb("bz", [P, 1], F32)
        bgT = sb("bgT", [P, KC], F32)
        eb = sb("eb", [P, E], F32)
        bst = sb("bst", [P, NT, 6], F32)
        mv = sb("mv", [P, NT, 2], F32)
        rs_v = sb("rs_v", [P, 4, NT], F32)
        rstd = sb("rstd", [P, NT], F32)
        r1 = sb("r1", [P, NT], F32)
        negmr = sb("negmr", [P, NT], F32)

        att = ExitStack()
        q_sb = sb("q_sb", [P, T], F32, att)
        k_sb = sb("k_sb", [P, T], F32, att)
        a_sb = sb("a_sb", [P, T], F32, att)
        pre1 = ExitStack()
        w13_raw = sb("w13_raw", [P, KC, 2 * F], F32, pre1)
        wo_raw = sb("wo_raw", [P, KC, D], F32, pre1)
        w2_raw = sb("w2_raw", [P, NF, D], F32, pre1)
        vt = sb("vt", [P, 2, L], F32, pre1)
        zb = sb("zb", [P, L], F32, pre1)
        zabs = sb("zabs", [P, L], F32, pre1)
        zexp = sb("zexp", [P, L], F32, pre1)
        zln = sb("zln", [P, L], F32, pre1)
        pre1.close()
        vrep = sb("vrep", [P, 2, 2, L], F32, att)
        kv = sb("kv", [P, 2, 2, L], F32, att)
        st = sb("st", [P, 2, 2, L], F32, att)
        qs = sb("qs", [P, 2, 2, L], F32, att)
        fill1 = sb("fill1", [P, KC * 2 * I], F32, att)
        g_sb = sb("g_sb", [P, KC, T], F32, att)
        wo_h = sb("wo_h", [P, KC, D], F32R, att)
        wo_l = sb("wo_l", [P, KC, D], F32R, att)
        w13 = sb("w13", [P, 2, KC, 2 * F], F16, att)
        w2_h = sb("w2_h", [P, NF, D], F32R, att)
        w2_l = sb("w2_l", [P, NF, D], F32R, att)
        rows = sb("rows", [P, NT, ROW], F32, att)
        rows16 = rows[:, :, :].bitcast(F16)
        pre = ExitStack()
        w_a = sb("w_a", [P, 2, KC, WA], F16, pre)
        anT = sb("anT", [P, 2, KC, T], F16, pre)
        wa_raw = sb("wa_raw", [P, KC, WA], F32, pre)
        wk2 = sb("wk2", [R, QK], F32, pre)
        wk1 = sb("wk1", [P, KC, R], F32, pre)
        wk1T = sb("wk1T", [R, KC, P], F32, pre)
        rw_raw = sb("rw_raw", [E, D], F32, pre)
        rw = sb("rw", [P, 2, KC, E], F16, pre)
        zls = sb("zls", [P, L], F32, pre)
        zrow = sb("zrow", [P, ROW], F32, pre)
        pre.close()
        oT = sb("oT", [P, KC, L], F32, att)
        ot = sb("ot", [P, TPB, D], F32, att)
        on = sb("on", [P, TPB, D], F32, att)
        gs = sb("gs", [P, KC, L], F32, att)
        og_h = sb("og_h", [P, KC, L], F32R, att)
        og_l = sb("og_l", [P, KC, L], F32R, att)
        an2 = sb("an2", [P, TPB, 2, D], F16, att)
        an2T = sb("an2T", [P, 2, KC, L], F16, att)
        ghead = [sb(f"ghead{i}", [P, TPB * H], F32, att) for i in range(4)]
        grow = [sb(f"grow{i}", [P, TPB], F32, att) for i in range(4)]
        rt = ExitStack()
        def rsb(name, shape=(P, NT, E), dt=F32):
            return sb(name, list(shape), dt, rt)
        lg = rsb("lg")
        mx = rsb("mx", (P, NT))
        m8 = rsb("m8", (P, NT, 8))
        gt = rsb("gt")
        eq = rsb("eq")
        need = rsb("need", (P, NT))
        eqc = rsb("eqc")
        Msel = rsb("Msel")
        M16 = rsb("M16", dt=F16)
        ex = rsb("ex")
        sm = rsb("sm", (P, NT))
        wgt = rsb("wgt")
        tot = rsb("tot", (P, E, NT))
        inc = rsb("inc", (P, E, NT))
        over = rsb("over", (P, E, NT))
        ntl = rsb("ntl", (P, E))
        ntc = rsb("ntc", (P, E))
        base = rsb("base", (P, E))
        slot = rsb("slot")
        cnt = rsb("cnt")
        pick = rsb("pick")
        prod = rsb("prod")
        slot_f = rsb("slot_f", (P, TOP, NT))
        owner = rsb("owner", (1, SLOT_TILES, E))
        own1 = rsb("own1", (1, SLOT_TILES))


        rt.close()
        sg = sb("sg", [P, 2, L], F32, att)
        hf = sb("hf", [P, 2, L], F32, att)
        h_h = sb("h_h", [P, NF, L], F32R, att)
        h_l = sb("h_l", [P, NF, L], F32R, att)
        att.close()

        UN = 16
        w_gu_f = sb("w_gu", [P, E + 1, KC * 2 * I], F32)
        w_gu = w_gu_f[:, :, :].bitcast(F16).rearrange("p e (a c n) -> p e a c n", a=2, c=KC)
        gu_raw = w_gu_f[:, :, :].rearrange("p e (c n) -> p e c n", c=KC)
        X = sb("X", [P, UN, ROW], F32)
        X16 = X[:, :, :].bitcast(F16)
        sb("fill2", [P, KC * T + 2 * KC * D - UN * ROW], F32)
        y = sb("y", [P, UN, D], F32)
        xT = sb("xT", [P, 2, 2, KC, P], F16)
        sl = sb("sl", [P, 2, I], F32)
        h = sb("h", [P, 2, I], F32)
        hT = sb("hT", [HK, 2, IC, P], F32)
        xback_f = sb("xback", [P, NT, D], F32)
        sb("fill3", [P, 2 * KC * F + 2 * NF * D + NT * ROW - UN * D - 2 * KC * P - 4 * I - 2 * IC * P - NT * D], F32)
        wd = sb("wd", [HK, E, IC, D], F32)
        sum_f = w_gu_f[:, :, :].rearrange("p e n -> p (e n)")

        turn_ps = ctx.enter_context(nc.psum_tensor("turn_ps", [P, 2, 512], F32))
        mm_ps = ctx.enter_context(nc.psum_tensor("mm_ps", [P, 4, 512], F32))
        sum_ps = ctx.enter_context(nc.psum_tensor("sum_ps", [P, 2, 512], F32))
        PS = T0, T1 = [turn_ps[:, i, :] for i in range(2)]
        M = [mm_ps[:, i, :] for i in range(4)]
        O0, O1 = [sum_ps[:, i, :] for i in range(2)]


        s = {n: sem(n) for n in """const_pool const_dve x_in0 x_in1 x_in2 x_in3 wa_in wz_in small_in
            stats rsq_seed rsq_done1 rsq_seed2 rsq_done2 xn_ready anh_ready anl_ready
            wk1_t wk1_copied wz_ready rw_t wprep_act wprep_dve w13_in wo_in w2_in zero_fill
            tp_ready tp_evac proj_ready evac_act evac_dve zb_ready zln_ready zls_ready a_ready
            logits_ready dve_chain pool_chain act_chain exp_ready m16_ready cum_ready route_ready
            ex_in scatter zero_row ln1k_ready cscale dve_max vt_ready vt_out0 vt_out1 prep_done lg_ready
            pool_head pool_row vr_in0 vr_in1 kv_ready st_ready qs_ready gla_used oT_evac pool_turn act_turn tpo_ready ot_ready oc_ready sq_ready
            head_dve head_seed head_rstd on_ready on_part tpb_ready gs_ready og_ready ogh_ready ogl_ready wo_ready xb_ready
            ms_ready row_dve row_seed row_rstd an2h_ready an2l_ready tpn_ready an2T_evac
            gu_ready sg_ready hf_ready hh_ready hl_ready w2_ready xc_ready
            ew_ready ewh_ready wd_in xt_ready xe_ready eg_ready sl_ready hm_ready ht_ready he_ready dn_ready ye_ready
            y_out0 y_out1 y_slots act_turn3 xr_in fin_in0 fin_in1 fin_in2 fin_in3 ysum_ready silu_ready fin_mul out_ready
            out_done""".split()}
        y_out = [s["y_out0"], s["y_out1"]]
        x_in = [sem(f"row_in{i}") for i in range(UN)]
        raw_in = [sem(f"raw_in{i}") for i in range(E // 2)]
        fin_in = [s[f"fin_in{c}"] for c in range(B)]
        vr_in = [s["vr_in0"], s["vr_in1"]]
        vt_out = [s["vt_out0"], s["vt_out1"]]

        def rsqrt_seed(step, r, v, magic=RSQRT_MAGIC):
            step(nc.vector.tensor_scalar(r.bitcast(I32), v.bitcast(I32), 1, None, ALU.logical_shift_right))
            nc_i = nc.vector.tensor_scalar(r.bitcast(I32), r.bitcast(I32), -1.0, float(magic), ALU.mult, ALU.add)
            return nc_i

        def rsqrt_newton(eng, step, r, v, t):
            for n in range(NEWTON):
                step(eng.tensor_tensor(t, r, r, ALU.mult))
                step(eng.tensor_tensor(t, t, v, ALU.mult))
                step(eng.tensor_scalar(t, t, -0.5, 1.5, ALU.mult, ALU.add))
                ins = eng.tensor_tensor(r, r, t, ALU.mult)
                if n < NEWTON - 1:
                    step(ins)
            return ins

        def rsqrt_newton_half(eng, step, r, half_v, t):
            for n in range(NEWTON):
                step(eng.tensor_tensor(t, r, r, ALU.mult))
                step(eng.tensor_tensor(t, t, half_v, ALU.mult))
                step(eng.tensor_tensor(t, c15[:, 0:t.shape[1]], t, ALU.subtract))
                ins = eng.tensor_tensor(r, r, t, ALU.mult)
                if n < NEWTON - 1:
                    step(ins)
            return ins

        xq = [s[f"x_in{c}"] for c in range(B)]
        NSMALL = 2 + KD + HD + 1
        NWPREP = 4 * KC + KC + 1
        WK1p = T0[0:R, 0:KC * P].rearrange("p (c n) -> p c n", c=KC)
        RWp = T1[:, 0:KC * E].rearrange("p (c n) -> p c n", c=KC)
        Zp = M[0][:, 0:KC * QK].rearrange("p (c n) -> p c n", c=KC)

        def hk_view(ap, from_hk):
            return ap.rearrange("p (h k) -> p k h", k=KD) if from_hk else ap.rearrange("p (k h) -> p k h", k=KD)

        def wparts(c, part):
            w = lambda col: w_a[:, part, c, col:col + QK]
            for col, scale in ((QC, ln1[:, c:c + 1]), (KCOL, ln1k[:, c:c + 1])):
                yield hk_view(w(col), False), hk_view(wa_raw[:, c, col:col + QK], True), scale
            for col in (VC, GC):
                yield (w_a[:, part, c, col:col + D].rearrange("p (d h) -> p d h", d=HD),
                       wa_raw[:, c, col:col + D].rearrange("p (h d) -> p d h", d=HD), ln1[:, c:c + 1])

        def triple(pe, out_ap, pairs):
            for n, (lhsT, rhs) in enumerate(pairs):
                last = nc.tensor.matmul(out_ap, lhsT, rhs, start=(n == 0), stop=(n == len(pairs) - 1))
            return last

        U = HD // 2
        CHUNKS = {1: (0,), 2: (1,), 3: (2,), 4: (3,), 5: (4, 5)}
        TOK = lambda b: bass.ds(b * L, L)
        TILES = lambda b, i=0, n=TPB: bass.ds(b * TPB + i, n)
        pair_bc = lambda ap: ap.rearrange("p (a l) -> p a l", a=1).to_broadcast((P, 2, L))

        def wait(eng, sem_, value):
            if not isinstance(value, int) or value > 0:
                eng.wait_ge(sem_, value)

        def turns(eng, step_fn):
            for it in (0, 1):
                for u in range(U):
                    step_fn(it, it - 1 if it else None, None, u)
            with eng.Fori(2, B) as it:
                for u in range(U):
                    step_fn(it, it - 1, it - 2, u)
            for it in (B, B + 1):
                for u in range(U):
                    step_fn(None, it - 1 if it == B else None, it - 2, u)

        head4 = lambda ap: ap.rearrange("p (t h) -> p t h", t=TPB)

        def attention_over(eng):
            eng.wait_ge(s["xc_ready"], 2 * B + 2)

        GROUPS = SLOT_TILES // UN

        def expert(eng, t):
            return eng.value_load(tile_expert[0:1, bass.ds(t, 1)], min_val=0, max_val=E - 1)

        ysum = [sum_f[:, c * TPB * D:(c + 1) * TPB * D] for c in range(B)]
        ysum2 = [sum_f[:, (B + c) * TPB * D:(B + c + 1) * TPB * D] for c in range(B)]
        xback = [xback_f[:, c * TPB:(c + 1) * TPB, :].rearrange("p t d -> p (t d)") for c in range(B)]

        def experts_at(c, b, u):
            if not isinstance(c, int):
                return ()
            q = (c - B + 2) * U + u - 2
            n = 2 * U - 2
            return range(q * E // n, (q + 1) * E // n) if q >= 0 else ()

        block = ctx.enter_context(nc.Block())

        @block.sync
        def _(sp):
            for c in range(B):
                sp.dma_start(xn[:, c * TPB:(c + 1) * TPB, :], xr[:, c * TPB:(c + 1) * TPB, :]).then_inc(xq[c], 16)
            for w, col in ((Wq, QC), (Wk, KCOL)):
                sp.dma_start(wa_raw[:, :, col:col + QK], w.rearrange("(c p) n -> p c n", p=P)).then_inc(s["wa_in"], 16)
            for w, col in ((Wv, VC), (Wg, GC)):
                sp.dma_start(wa_raw[:, :, col:col + D], w.rearrange("(c p) n -> p c n", p=P)).then_inc(s["wa_in"], 16)
            sp.dma_start(w13_raw[:, :, 0:F], W1.rearrange("(c p) n -> p c n", p=P)).then_inc(s["w13_in"], 16)
            sp.dma_start(w13_raw[:, :, F:2 * F], W3.rearrange("(c p) n -> p c n", p=P)).then_inc(s["w13_in"], 16)
            for d in range(HD):
                c, dd = d // DH, d % DH
                sp.dma_start(wo_raw[dd * H:(dd + 1) * H, c, :],
                             Wo.rearrange("(h d) n -> d h n", d=HD)[d]).then_inc(s["wo_in"], 16)
            nfull = F // P
            sp.dma_start(w2_raw[:, 0:nfull, :], W2[0:nfull * P].rearrange("(c p) n -> p c n", p=P)).then_inc(s["w2_in"], 16)
            sp.dma_start(w2_raw[0:F - nfull * P, nfull, :], W2[nfull * P:F]).then_inc(s["w2_in"], 16)
            sp.sem_inc(vt_out[0], 16)
            sp.sem_inc(vt_out[1], 16)
            with sp.Fori(0, B) as b:
                for c in range(2):
                    sp.wait_ge(s["vt_ready"], b * 2 + (c + 1))
                    sp.dma_start(v_dram[bass.ds(b, 1), c * DH:(c + 1) * DH].rearrange("b d h l -> (b d h) l"),
                                 vt[:, c, :]).then_inc(vt_out[c], 16)
            for c in range(2):
                sp.wait_ge(vt_out[c], 16 * (B + 1))
            sp.wait_ge(s["a_ready"], B)
            sp.wait_ge(s["prep_done"], 1)
            with sp.Fori(0, B) as b:
                for u in range(U):
                    sp.wait_ge(s["kv_ready"], b * U + (u + 1))
                    for j in range(2):
                        src = v_dram[bass.ds(b, 1), 2 * u + j].rearrange("b h l -> (b h) l")
                        sp.dma_start(vrep[:, u % 2, j, :], bass.AP(tensor=src.tensor, offset=src.offset,
                                                                   ap=[[0, KD], [L, H], [1, L]])).then_inc(vr_in[u % 2], 16)

            sp.wait_ge(s["gla_used"], U * B + 2)
            for e in range(E):
                for i, w in enumerate((gate_proj, up_proj)):
                    sp.dma_start(gu_raw[:, e + 1, :, i * I:(i + 1) * I],
                                 w[e].rearrange("(c p) n -> p c n", p=P)).then_inc(raw_in[e // 2], 16)
            def load_down(e0, e1):
                sp.dma_start(wd[:, e0:e1, :, :].rearrange("p e i d -> p (e i) d"),
                             down_proj[e0:e1].rearrange("e (i p) d -> p (e i) d", p=HK)).then_inc(s["wd_in"], 16)

            def load_rows(g, u):
                sp.dma_start(X[:, u, :], rows_dram[bass.ds((g * UN + u) * P, P), :]).then_inc(x_in[u], 16)

            sp.wait_ge(s["tpn_ready"], 4 * B)
            load_down(0, E - 2)
            sp.wait_ge(s["scatter"], 16 * NT * TOP)
            for u in range(UN):
                load_rows(0, u)
            sp.wait_ge(s["gu_ready"], 2 * NF * B)
            load_down(E - 2, E)
            attention_over(sp)
            for c in range(B):
                sp.dma_start(xback[c].rearrange("p (t d) -> p t d", t=TPB), xr[:, c * TPB:(c + 1) * TPB, :]).then_inc(s["xr_in"], 16)
            with sp.Fori(1, GROUPS) as g:
                for u in range(UN):
                    sp.wait_ge(s["y_slots"], g * UN + (u + 3))
                    load_rows(g, u)
            for i in range(2):
                sp.wait_ge(y_out[i], 16 * SLOT_TILES // 2)
            sp.wait_ge(s["eg_ready"], SLOT_TILES + 2)
            for c in range(B):
                for i, dst in enumerate((ysum, ysum2)):
                    sp.dma_start(dst[c].rearrange("p (t d) -> p t d", t=TPB),
                                 y_dram[i].rearrange("(t p) d -> p t d", p=P)[:, c * TPB:(c + 1) * TPB, :])\
                        .then_inc(fin_in[c], 16)
            for c in range(B):
                sp.wait_ge(s["out_ready"], c + 1)
                sp.dma_start(outr[:, c * TPB:(c + 1) * TPB, :], ysum[c].rearrange("p (t d) -> p t d", t=TPB))\
                    .then_inc(s["out_done"], 16)
            sp.wait_ge(s["out_done"], 16 * B)

        @block.gpsimd
        def _(pool):
            step = sem_chain(pool, s["pool_chain"], 0)
            step(nc.gpsimd.memset(zrow[:, :], 0.0))
            nc.gpsimd.iota(zrow[:, TOKEN_C:TOKEN_C + 1].bitcast(U32), pattern=[[0, 1]], base=T,
                           channel_multiplier=1).then_inc(s["zero_row"], 1)
            step(nc.gpsimd.iota(rows[:, :, TOKEN_C:TOKEN_C + 1].bitcast(U32), pattern=[[P, NT], [0, 1]], base=0,
                                channel_multiplier=1))
            for m in (ident, ident16):
                step(nc.gpsimd.memset(m[:, :], 0.0))
                step(nc.gpsimd.affine_select(out=m[:, :], in_=m[:, :], compare_op=ALU.not_equal, fill=1.0, base=0,
                                             pattern=[[-1, P]], channel_multiplier=1))
            step(nc.gpsimd.memset(ones16[:, :], 1.0))
            step(nc.gpsimd.affine_select(out=before16[:, :], in_=ones16[:, :], compare_op=ALU.is_gt, fill=0.0, base=0,
                                         pattern=[[1, P]], channel_multiplier=-1))
            step(nc.gpsimd.iota(head_i[:, :], pattern=[[-1, H]], base=H, channel_multiplier=1))
            step(nc.gpsimd.memset(sumk[:, :], 0.0))
            step(nc.gpsimd.memset(restart[:, :, :], 1.0))
            step(nc.gpsimd.memset(restart[:, :, 0:1], 0.0))
            step(nc.gpsimd.memset(one_e[:, :], 1.0))
            step(nc.gpsimd.memset(c15[:, :], 1.5))
            step(nc.gpsimd.iota(steps128[:, :, :], pattern=[[0, E], [P, NT]], base=0, channel_multiplier=0,
                                allow_small_or_imprecise_dtypes=True))
            nc.gpsimd.iota(tile_no[:, :], pattern=[[1, SLOT_TILES]], base=0, channel_multiplier=0,
                           allow_small_or_imprecise_dtypes=True).then_inc(s["const_pool"], 1)
            pool.wait_ge(s["rsq_seed"], 1)
            rsqrt_newton(nc.gpsimd, step, rstd[:, :], rs_v[:, 0, :], rs_v[:, 1, :]).then_inc(s["rsq_done1"], 1)
            pool.wait_ge(s["rsq_seed2"], 1)
            rsqrt_newton(nc.gpsimd, step, r1[:, :], rs_v[:, 2, :], rs_v[:, 3, :]).then_inc(s["rsq_done2"], 1)
            pool.wait_ge(s["rsq_done2"], 1)
            for t in range(NT):
                pool.wait_ge(s["xn_ready"], t + 1)
                nc.gpsimd.tensor_scalar(rows16[:, t, 0:D], xn[:, t, :], r1[:, t:t + 1], 1.0, ALU.mult,
                                        ALU.mult).then_inc(s["anh_ready"], 1)
            pool.wait_ge(s["w13_in"], 32)
            pool.wait_ge(s["small_in"], 16 * NSMALL)
            for c in range(KC):
                raw = w13_raw[:, c, :]
                step(nc.gpsimd.tensor_scalar(raw, raw, ln2[:, c:c + 1], 1.0, ALU.mult, ALU.mult))
                step(nc.gpsimd.tensor_scalar(w13[:, 0, c, :], raw, 1.0, 1.0, ALU.mult, ALU.mult))
                step(nc.gpsimd.tensor_tensor(w13[:, 1, c, :], raw, w13[:, 0, c, :], ALU.subtract))
            pool.wait_ge(s["wo_in"], 16 * HD)
            pool.wait_ge(s["w2_in"], 32)
            nf, fr = F // P, F % P
            parts = [(wo_raw[:, :, :], wo_h[:, :, :], wo_l[:, :, :]),
                     (w2_raw[:, 0:nf, :], w2_h[:, 0:nf, :], w2_l[:, 0:nf, :]),
                     (w2_raw[0:fr, nf, :], w2_h[0:fr, nf, :], w2_l[0:fr, nf, :])]
            for raw, hi, lo in parts:
                step(nc.gpsimd.tensor_scalar(hi, raw, 1.0, 1.0, ALU.mult, ALU.mult))
                step(nc.gpsimd.tensor_tensor(lo, raw, hi.bitcast(F32), ALU.subtract))
            pool.sem_inc(s["prep_done"], 1)
            scatters = iter([(t, j) for t in range(NT) for j in range(TOP)])

            def scatter(n):
                for _, (t, j) in zip(range(n), scatters):
                    nc.gpsimd.indirect_dma_start(
                        rows_dram, bass.IndirectOffsetOnAxis(ap=slot_u[:, j, t:t + 1], axis=0),
                        rows[:, t, :], None).then_inc(s["scatter"], 16)

            pool.sem_inc(s["qs_ready"], 2)

            def newton(sem_seed, sem_done, sem_chain_, b, r, v, t):
                pool.wait_ge(sem_seed, b + 1)
                step = sem_chain(pool, sem_chain_, 0, 4 * NEWTON - 1, b)
                rsqrt_newton_half(nc.gpsimd, step, r, v, t).then_inc(sem_done, 1)

            def step_fn(a, b, c, u):
                if a is not None:
                    pool.wait_ge(s["st_ready"], a * 2 * U + (2 * u + 6))
                    pool.wait_ge(s["gla_used"], a * U + (u + 1))
                    pool.sem_inc(s["pool_turn"], 1)
                    nc.gpsimd.tensor_tensor(qs[:, u % 2, :, :], st[:, u % 2, :, :], pair_bc(q_sb[:, TOK(a)]),
                                            ALU.mult).then_inc(s["qs_ready"], 1)
                if b is not None and u == 2:
                    newton(s["head_seed"], s["head_rstd"], s["pool_head"], b, ghead[1][:, :], ghead[0][:, :], ghead[2][:, :])
                if b is not None and u == 6:
                    newton(s["row_seed"], s["row_rstd"], s["pool_row"], b, grow[1][:, :], grow[0][:, :], grow[2][:, :])
                if isinstance(b, int) and b == 0 and u == 0:
                    pool.wait_ge(s["route_ready"], 1)
                    pool.wait_ge(s["zero_fill"], 48)
                    pool.wait_ge(s["anl_ready"], NT)
                if isinstance(b, int) and b == 0 or a is None:
                    scatter(4 if a is None and b is not None else 2)

            turns(pool, step_fn)
            pool.wait_ge(s["pool_turn"], U * B)
            pool.wait_ge(s["scatter"], 16 * NT * TOP)

            pool.sem_inc(s["y_slots"], UN)

            def add_out(g, u):
                pool.wait_ge(s["ye_ready"], g * UN + (u + 3))
                wait(pool, y_out[u % 2], g * (16 * UN // 2) + 16 * (u // 2))
                pool.sem_inc(s["y_slots"], 1)
                nc.gpsimd.indirect_dma_start(
                    y_dram[u % 2], bass.IndirectOffsetOnAxis(ap=X[:, u, TOKEN_C:TOKEN_C + 1].bitcast(U32), axis=0),
                    y[:, u, :], None, compute_op=ALU.add).then_inc(y_out[u % 2], 16)

            for u in range(UN):
                add_out(0, u)
            with pool.Fori(1, GROUPS) as g:
                for u in range(UN):
                    add_out(g, u)

        @block.scalar
        def _(act):
            chain = sem_chain(act, s["act_chain"], 0)
            act.dma_start(wk1[:, :, :], Wkg1.rearrange("(c p) n -> p c n", p=P)).then_inc(s["wz_in"], 16)
            act.dma_start(wk2[:, :], Wkg2).then_inc(s["wz_in"], 16)
            act.dma_start(rw_raw[:, :], router_w).then_inc(s["wz_in"], 16)
            with nc.allow_non_contiguous_dma(reason="a few hundred numbers"):
                act.dma_start(ln1[:, :], ln1_w.rearrange("(c p) -> p c", p=P)).then_inc(s["small_in"], 16)
                act.dma_start(ln2[:, :], ln2_w.rearrange("(c p) -> p c", p=P)).then_inc(s["small_in"], 16)
                for k in range(KD):
                    act.dma_start(bz[k * H:(k + 1) * H, :],
                                  bkg2.rearrange("(h k a) -> k h a", k=KD, a=1)[k]).then_inc(s["small_in"], 16)
                for d in range(HD):
                    c, dd = d // DH, d % DH
                    act.dma_start(bgT[dd * H:(dd + 1) * H, c:c + 1],
                                  bg.rearrange("(h d a) -> d h a", d=HD, a=1)[d]).then_inc(s["small_in"], 16)
                act.dma_start(eb[:, :], expert_bias.rearrange("(a e) -> a e", a=1).to_broadcast((P, E))).then_inc(s["small_in"], 16)
            act.wait_ge(s["zero_row"], 1)
            act.dma_start(rows_dram.rearrange("(n p) c -> p n c", p=P),
                          zrow[:, :].rearrange("p (a c) -> p a c", a=1).to_broadcast((P, SLOT_TILES, ROW)))\
                .then_inc(s["zero_fill"], 16)
            for acc in y_dram:
                act.dma_start(acc.rearrange("(n p) d -> p n d", p=P),
                              zrow[:, 0:D].rearrange("p (a c) -> p a c", a=1).to_broadcast((P, NT + 1, D)))\
                    .then_inc(s["zero_fill"], 16)
            nc.scalar.preload_act_table(ACT.Ln)
            act.wait_ge(s["wa_in"], 64)
            act.wait_ge(s["small_in"], 16 * NSMALL)
            act.wait_ge(s["ln1k_ready"], 1)
            for c in range(KC):
                for out_ap, in_ap, scale in wparts(c, 0):
                    nc.scalar.activation(out_ap, in_ap, ACT.Copy, scale=scale).then_inc(s["wprep_act"], 1)
            act.wait_ge(s["wz_ready"], 1)
            for c in range(KC):
                nc.scalar.activation(hk_view(w_a[:, 0, c, ZC:ZC + QK], False), hk_view(Zp[:, c, :], True), ACT.Copy,
                                     scale=ln1[:, c:c + 1]).then_inc(s["wprep_act"], 1)
            act.wait_ge(s["rw_t"], 1)
            nc.scalar.activation(rw[:, 0, :, :], RWp, ACT.Copy).then_inc(s["wprep_act"], 1)
            act.sem_inc(s["tp_evac"], 2)
            act.sem_inc(s["evac_act"], 2)
            def evac_rows(t, j):
                act.wait_ge(s["tp_ready"], t + 1)
                nc.scalar.activation(anT[:, :, :, bass.ds(t * P, P)],
                                     PS[j % 2].rearrange("p (a c n) -> p a c n", a=2, c=KC),
                                     ACT.Copy).then_inc(s["tp_evac"], 1)

            def turn(b, more):
                def evac(i, out_ap, **kw):
                    act.wait_ge(s["proj_ready"], b * 7 + (i + 1))
                    nc.scalar.activation(out_ap, M[i % 4], kw.get("func", ACT.Copy),
                                         **({"bias": kw["bias"]} if "bias" in kw else {})).then_inc(s["evac_act"], 1)

                def next_rows(j):
                    if more:
                        evac_rows((b + 1) * TPB + j, j)

                evac(0, q_sb[:, bass.ds(b * L, L)])
                act.wait_ge(s["zb_ready"], b + 1)
                nc.scalar.activation(zabs[:, :], zb[:, :], ACT.Abs).then_inc(s["act_chain"], 1)
                next_rows(0)
                act.wait_ge(s["act_chain"], b * 2 + 1)
                nc.scalar.activation(zexp[:, :], zabs[:, :], ACT.Exp, scale=-1.0).then_inc(s["act_chain"], 1)
                evac(2, k_sb[:, bass.ds(b * L, L)])
                next_rows(1)
                act.wait_ge(s["act_chain"], b * 2 + 2)
                nc.scalar.activation(zln[:, :], zexp[:, :], ACT.Ln, bias=1.0).then_inc(s["zln_ready"], 1)
                next_rows(2)
                next_rows(3)
                evac(5, g_sb[:, 0, bass.ds(b * L, L)], func=ACT.Identity, bias=bgT[:, 0:1])
                evac(6, g_sb[:, 1, bass.ds(b * L, L)], func=ACT.Identity, bias=bgT[:, 1:2])
                act.wait_ge(s["zls_ready"], b + 2)
                nc.scalar.activation(a_sb[:, bass.ds(b * L, L)], zls[:, :], ACT.Exp, scale=1.0 / NORMALIZER)\
                    .then_inc(s["a_ready"], 1)

            for j in range(TPB):
                evac_rows(j, j)
            with act.Fori(0, B - 1) as b:
                turn(b, True)
            turn(B - 1, False)
            act.wait_ge(s["ex_in"], 1)
            nc.scalar.activation(ex[:, :, :], prod[:, :, :], ACT.Exp).then_inc(s["exp_ready"], 1)

            act.wait_ge(s["exp_ready"], 1)
            nc.scalar.preload_act_table(ACT.Silu)
            act.sem_inc(s["oT_evac"], 2)
            act.wait_ge(s["lg_ready"], 1)

            def gate_silu(c, m):
                rows_m = FT[m][1]
                act.wait_ge(s["gu_ready"], c * 2 * NF + (2 * m + 1))
                act.wait_ge(s["hf_ready"], c * NF + (m + 1))
                nc.scalar.activation(sg[0:rows_m, m % 2, :], M[2 * (m % 2)][0:rows_m, :], ACT.Silu).then_inc(s["sg_ready"], 1)

            def high_h(c, m):
                rows_m = FT[m][1]
                act.wait_ge(s["hf_ready"], c * NF + (m + 3))
                wait(act, s["w2_ready"], c * 2 + 1)
                nc.scalar.activation(h_h[0:rows_m, m, :], hf[0:rows_m, m % 2, :], ACT.Copy).then_inc(s["hh_ready"], 1)

            def step_fn(a, b, c, u):
                chunks = CHUNKS.get(u, ()) if c is not None else ()
                for m in chunks[:1]:
                    gate_silu(c, m)
                if b is not None:
                    if u == 0:
                        wait(act, s["on_ready"], b)
                        for i in range(2):
                            act.wait_ge(s["tpo_ready"], b * 2 + (i + 1))
                            nc.scalar.activation(
                                ot[:, 2 * i:2 * i + 2, :].rearrange("p t (h d) -> p t d h", d=HD),
                                PS[i].rearrange("p (t d h) -> p t d h", t=2, d=HD), ACT.Copy).then_inc(s["ot_ready"], 1)
                    if u == 1:
                        wait(act, s["tpb_ready"], b * 2)
                        act.wait_ge(s["oc_ready"], b + 1)
                        nc.scalar.activation(on[:, :, :], ot[:, :, :], ACT.Square).then_inc(s["sq_ready"], 1)
                    if u == 2:
                        wait(act, s["ogl_ready"], b * 2)
                        act.sem_inc(s["act_turn"], 1)
                        nc.scalar.activation(gs[:, :, :], g_sb[:, :, TOK(b)], ACT.Silu).then_inc(s["gs_ready"], 1)
                    if u == 4:
                        wait(act, s["wo_ready"], b * 2)
                        for i in range(2):
                            act.wait_ge(s["og_ready"], b * 2 + (i + 1))
                            nc.scalar.activation(og_h[:, i, :], gs[:, i, :], ACT.Copy).then_inc(s["ogh_ready"], 1)
                    if u == 6:
                        for t in range(TPB):
                            if t % 2 == 0:
                                act.wait_ge(s["xb_ready"], b * 2 + (t // 2 + 1))
                                act.sem_inc(s["act_turn"], 1)
                            nc.scalar.activation(ot[:, t, :], xn[:, TILES(b, t, 1), :].rearrange("p a d -> p (a d)"), ACT.Square,
                                                 accum_out=grow[3][:, t:t + 1]).then_inc(s["ms_ready"], 1)
                    if u == 7:
                        act.wait_ge(s["row_rstd"], b + 1)
                        wait(act, s["tpn_ready"], b * 4)
                        act.sem_inc(s["act_turn"], 1)
                        for t in range(TPB):
                            nc.scalar.activation(an2[:, t, 0, :], xn[:, TILES(b, t, 1), :].rearrange("p a d -> p (a d)"), ACT.Copy,
                                                 scale=grow[1][:, t:t + 1]).then_inc(s["an2h_ready"], 1)
                    if u == 7:
                        for part in range(2):
                            for i in range(KC):
                                act.wait_ge(s["tpn_ready"], b * 4 + (part * 2 + i + 1))
                                if part == 0 and i == 0:
                                    wait(act, s["gu_ready"], b * 2 * NF)
                                nc.scalar.activation(an2T[:, part, i, :], PS[i], ACT.Copy).then_inc(s["an2T_evac"], 1)
                if a is not None and u in (4, 7):
                    half = u == 7
                    act.wait_ge(s["gla_used"], a * U + (2 + (8 if half else 4)))
                    wait(act, s["tpo_ready"], a * 2)
                    nc.scalar.activation(oT[:, int(half), :], sum_ps[:, int(half), :], ACT.Copy).then_inc(s["oT_evac"], 1)
                for m in chunks:
                    if m != chunks[0]:
                        gate_silu(c, m)
                    high_h(c, m)
                for e in experts_at(c, b, u):
                    act.wait_ge(raw_in[e // 2], 64)
                    wait(act, s["ew_ready"], e)
                    nc.scalar.activation(w_gu[:, e, 0, :, :], gu_raw[:, e + 1, :, :], ACT.Copy).then_inc(s["ewh_ready"], 1)

            turns(act, step_fn)
            act.wait_ge(s["act_turn"], 4 * B)

            attention_over(act)
            act.sem_inc(s["he_ready"], 2)
            act.sem_inc(s["ye_ready"], 2)

            def tile_silu(g, u):
                t = g * UN
                act.wait_ge(s["eg_ready"], t + (u + 3))
                act.wait_ge(s["hm_ready"], t + (u + 1))
                nc.scalar.activation(sl[:, u % 2, :], M[u % 2][:, 0:I], ACT.Silu, scale=X[:, u, SCALE_C:SCALE_C + 1])\
                    .then_inc(s["sl_ready"], 1)

            def tile_rest(g, u):
                t = g * UN
                act.wait_ge(s["ht_ready"], t + (u + 3))
                act.wait_ge(s["dn_ready"], t + (u + 1))
                nc.scalar.activation(hT[:, u % 2, :, :], M[2 + u % 2][0:HK, 0:IC * P].rearrange("p (i n) -> p i n", i=IC),
                                     ACT.Copy).then_inc(s["he_ready"], 1)

            def tile_out(g, u):
                t = g * UN
                e = expert(act, t + u)
                act.wait_ge(s["dn_ready"], t + (u + 3))
                act.wait_ge(s["y_slots"], g * UN + (u + 3))
                act.sem_inc(s["act_turn3"], 1)
                nc.scalar.activation(y[:, u, :], sum_ps[:, u % 2, 0:D], ACT.Copy, scale=X[:, u, bass.ds(e + WEIGHT_C, 1)])\
                    .then_inc(s["ye_ready"], 1)

            def tiles(g, last):
                for u in range(UN):
                    if not (last and u == UN - 1):
                        tile_silu(g + (u + 1) // UN, (u + 1) % UN)
                    tile_rest(g, u)
                    if u > 0:
                        tile_out(g, u - 1)
                tile_out(g, UN - 1)

            tile_silu(0, 0)
            with act.Fori(0, GROUPS - 1) as g:
                tiles(g, False)
            tiles(GROUPS - 1, True)
            act.wait_ge(s["act_turn3"], SLOT_TILES)
            for c in range(B):
                act.wait_ge(s["ysum_ready"], c + 1)
                nc.scalar.activation(ysum2[c], ysum[c], ACT.Silu).then_inc(s["silu_ready"], 1)

        @block.vector
        def _(dve):
            step = sem_chain(dve, s["dve_chain"], 0)
            dve.wait_ge(s["const_pool"], 1)
            step(nc.vector.tensor_scalar(head_m[:, :], head_i[:, :], H - 1, None, ALU.bitwise_and))
            nc.vector.tensor_scalar(sumk[:, P - H:P], head_m[:, :], 0.0, None, ALU.is_equal).then_inc(s["const_dve"], 1)
            for c in range(B):
                dve.wait_ge(xq[c], 16)
                with dve.Fori(c * TPB, (c + 1) * TPB) as t:
                    nc.vector.bn_stats(bst[:, bass.ds(t, 1), :].rearrange("p a d -> p (a d)"),
                                       xn[:, bass.ds(t, 1), :].rearrange("p a d -> p (a d)")).then_inc(s["stats"], 1)
            dve.wait_ge(s["stats"], NT)
            for t in range(NT):
                nc.vector.bn_aggr(mv[:, t, :], bst[:, t, :]).then_inc(s["stats"], 1)
            dve.wait_ge(s["stats"], 2 * NT)
            mean, var = mv[:, :, 0], mv[:, :, 1]
            step(nc.vector.tensor_scalar(rs_v[:, 0, :], var, EPS, None, ALU.add))
            rsqrt_seed(step, rstd[:, :], rs_v[:, 0, :]).then_inc(s["rsq_seed"], 1)
            dve.wait_ge(s["rsq_done1"], 1)
            step(nc.vector.tensor_tensor(rs_v[:, 2, :], rstd[:, :], rstd[:, :], ALU.mult))
            step(nc.vector.tensor_tensor(rs_v[:, 2, :], rs_v[:, 2, :], var, ALU.mult))
            step(nc.vector.tensor_scalar(rs_v[:, 2, :], rs_v[:, 2, :], EPS, None, ALU.add))
            rsqrt_seed(step, r1[:, :], rs_v[:, 2, :]).then_inc(s["rsq_seed2"], 1)
            step(nc.vector.scalar_tensor_tensor(out=negmr[:, :], in0=mean, scalar=-1.0, in1=rstd[:, :],
                                                op0=ALU.mult, op1=ALU.mult))
            with dve.Fori(0, NT) as t:
                xt = xn[:, bass.ds(t, 1), :].rearrange("p a d -> p (a d)")
                nc.vector.tensor_scalar(xt, xt, rstd[:, bass.ds(t, 1)], negmr[:, bass.ds(t, 1)],
                                        ALU.mult, ALU.add).then_inc(s["xn_ready"], 1)
            dve.wait_ge(s["small_in"], 16 * NSMALL)
            nc.vector.tensor_scalar(ln1k[:, :], ln1[:, :], KS, None, ALU.mult).then_inc(s["ln1k_ready"], 1)
            dve.wait_ge(s["wk1_t"], 1)
            nc.vector.tensor_copy(wk1T[:, :, :], WK1p).then_inc(s["wk1_copied"], 1)
            dve.wait_ge(s["ln1k_ready"], 1)
            n = 0
            for c in range(KC):
                for (lo_ap, in_ap, scale), (hi_ap, _, _) in zip(wparts(c, 1), wparts(c, 0)):
                    n += 1
                    dve.wait_ge(s["wprep_act"], n)
                    nc.vector.scalar_tensor_tensor(out=lo_ap, in0=in_ap, scalar=scale, in1=hi_ap,
                                                   op0=ALU.mult, op1=ALU.subtract).then_inc(s["wprep_dve"], 1)
            n += KC
            dve.wait_ge(s["wprep_act"], n)
            for c in range(KC):
                nc.vector.scalar_tensor_tensor(out=hk_view(w_a[:, 1, c, ZC:ZC + QK], False), in0=hk_view(Zp[:, c, :], True),
                                               scalar=ln1[:, c:c + 1], in1=hk_view(w_a[:, 0, c, ZC:ZC + QK], False),
                                               op0=ALU.mult, op1=ALU.subtract).then_inc(s["wprep_dve"], 1)
            dve.wait_ge(s["wprep_act"], n + 1)
            nc.vector.tensor_tensor(rw[:, 1, :, :], RWp, rw[:, 0, :, :], ALU.subtract).then_inc(s["wprep_dve"], 1)
            dve.wait_ge(s["rsq_done2"], 1)
            with dve.Fori(0, NT) as t:
                dve.wait_ge(s["anh_ready"], t + 1)
                nc.vector.scalar_tensor_tensor(
                    out=rows16[:, bass.ds(t, 1), D:2 * D].rearrange("p a d -> p (a d)"),
                    in0=xn[:, bass.ds(t, 1), :].rearrange("p a d -> p (a d)"), scalar=r1[:, bass.ds(t, 1)],
                    in1=rows16[:, bass.ds(t, 1), 0:D].rearrange("p a d -> p (a d)"),
                    op0=ALU.mult, op1=ALU.subtract).then_inc(s["anl_ready"], 1)
            cview = rows[:, :, SCALE_C:SCALE_C + 1]
            nc.vector.tensor_tensor(cview, rs_v[:, 2, :].rearrange("p (t a) -> p t a", a=1),
                                    r1[:, :].rearrange("p (t a) -> p t a", a=1), ALU.mult).then_inc(s["cscale"], 1)
            dve.sem_inc(s["evac_dve"], 2)
            dve.sem_inc(s["zls_ready"], 1)
            with dve.Fori(0, B) as b:
                dve.wait_ge(s["zls_ready"], b + 1)
                dve.wait_ge(s["proj_ready"], b * 7 + 2)
                nc.vector.tensor_scalar(zb[:, :], M[1], bz[:, 0:1], None, ALU.add).then_inc(s["evac_dve"], 1)
                dve.wait_ge(s["evac_dve"], b * 3 + 3)
                dve.sem_inc(s["zb_ready"], 1)
                for c in range(2):
                    dve.wait_ge(s["proj_ready"], b * 7 + (4 + c))
                    dve.wait_ge(vt_out[c], b * 16 + 16)
                    nc.vector.tensor_copy(vt[:, c, :], M[(3 + c) % 4]).then_inc(s["evac_dve"], 1)
                    dve.wait_ge(s["evac_dve"], b * 3 + (4 + c))
                    dve.sem_inc(s["vt_ready"], 1)
                dve.wait_ge(s["zln_ready"], b + 1)
                nc.vector.scalar_tensor_tensor(out=zls[:, :], in0=zb[:, :], scalar=0.0, in1=zln[:, :],
                                               op0=ALU.min, op1=ALU.subtract).then_inc(s["zls_ready"], 1)
            dve.sem_inc(s["kv_ready"], 2)
            dve.sem_inc(s["st_ready"], 4)

            def recurrence(a, u):
                r = u % 2
                dve.wait_ge(vr_in[r], a * 16 * U + 32 * (u // 2 + 1))
                dve.wait_ge(s["st_ready"], a * 2 * U + (2 * u + 2))
                nc.vector.tensor_tensor(kv[:, r, :, :], vrep[:, r, :, :], pair_bc(k_sb[:, TOK(a)]),
                                        ALU.mult).then_inc(s["kv_ready"], 1)
                yield
                dve.wait_ge(s["kv_ready"], a * U + (u + 3))
                dve.wait_ge(s["qs_ready"], a * U + (u + 1))
                for j in range(2):
                    nc.vector.tensor_tensor_scan(st[:, r, j, :], a_sb[:, TOK(a)], kv[:, r, j, :], 0.0,
                                                 ALU.mult, ALU.add).then_inc(s["st_ready"], 1)
                    if j == 0:
                        yield

            dve.wait_ge(s["a_ready"], B)
            dve.wait_ge(s["prep_done"], 1)
            for c in range(2):
                dve.wait_ge(vt_out[c], 16 * (B + 1))
            def first_recurrence():
                for u in range(U):
                    yield from recurrence(0, u)
                    yield

            first = first_recurrence()
            early = 6

            def between():
                nonlocal early
                early -= 1
                if early >= 0 or summed:
                    next(first, None)

            summed = False
            step = sem_chain(dve, s["dve_chain"], step(None), between=between)
            dve.wait_ge(s["logits_ready"], NT)
            dve.wait_ge(s["cscale"], 1)
            cb = cview.to_broadcast((P, NT, E))
            LG = O1[:, 0:NT * E].rearrange("p (t e) -> p t e", e=E)
            dve.wait_ge(s["proj_ready"], 7 * B)
            dve.wait_ge(s["zero_fill"], 48)
            nc.vector.tensor_tensor(lg[:, :, :], LG, cb, ALU.mult).then_inc(s["lg_ready"], 1)
            dve.wait_ge(s["lg_ready"], 1)
            step(nc.vector.tensor_tensor(lg[:, :, :], lg[:, :, :],
                                         eb[:, :].rearrange("p (a e) -> p a e", a=1).to_broadcast((P, NT, E)), ALU.add))
            nc.vector.tensor_reduce(mx[:, :], lg[:, :, :], AX.X, ALU.max).then_inc(s["dve_max"], 1)
            for t in range(NT):
                nc.vector.max(m8[:, t, :], lg[:, t, :]).then_inc(s["dve_max"], 1)
            dve.wait_ge(s["dve_max"], NT + 1)
            un = lambda ap: ap.rearrange("p (t a) -> p t a", a=1).to_broadcast((P, NT, E))
            flat = lambda ap: ap.rearrange("p t e -> p (t e)")
            nc.vector.tensor_tensor(prod[:, :, :], lg[:, :, :], un(mx[:, :]), ALU.subtract).then_inc(s["ex_in"], 1)
            v4 = m8[:, :, TOP - 1:TOP].to_broadcast((P, NT, E))
            step(nc.vector.tensor_tensor(gt[:, :, :], lg[:, :, :], v4, ALU.is_gt))
            step(nc.vector.tensor_tensor(eq[:, :, :], lg[:, :, :], v4, ALU.is_equal))
            step(nc.vector.tensor_reduce(need[:, :], gt[:, :, :], AX.X, ALU.add))
            step(nc.vector.tensor_scalar(need[:, :], need[:, :], -1.0, float(TOP), ALU.mult, ALU.add))
            step(nc.vector.tensor_tensor_scan(flat(eqc[:, :, :]), flat(restart[:, :, :]), flat(eq[:, :, :]), 0.0,
                                              ALU.mult, ALU.add))
            step(nc.vector.tensor_tensor(eqc[:, :, :], eqc[:, :, :], un(need[:, :]), ALU.is_le))
            step(nc.vector.tensor_tensor(eq[:, :, :], eq[:, :, :], eqc[:, :, :], ALU.mult))
            step(nc.vector.tensor_tensor(Msel[:, :, :], gt[:, :, :], eq[:, :, :], ALU.add))
            nc.vector.tensor_copy(M16[:, :, :], Msel[:, :, :]).then_inc(s["m16_ready"], 1)
            dve.wait_ge(s["exp_ready"], 1)
            step(nc.vector.tensor_tensor(wgt[:, :, :], ex[:, :, :], Msel[:, :, :], ALU.mult))
            step(nc.vector.tensor_reduce(sm[:, :], wgt[:, :, :], AX.X, ALU.add))
            step(nc.vector.reciprocal(sm[:, :], sm[:, :]))
            step(nc.vector.tensor_tensor(rows[:, :, WEIGHT_C:ROW], wgt[:, :, :], un(sm[:, :]), ALU.mult))
            dve.wait_ge(s["cum_ready"], 1)
            summed = True
            CUM = T0[:, 0:NT * E].rearrange("p (t e) -> p t e", e=E)
            TOT = T0[:, NT * E:2 * NT * E].rearrange("p (t e) -> p e t", e=E)
            step(nc.vector.tensor_copy(tot[:, :, :], TOT))
            step(nc.vector.tensor_tensor_scan(flat(inc[:, :, :]), flat(restart[:, :, :]), flat(tot[:, :, :]), 0.0,
                                              ALU.mult, ALU.add))
            step(nc.vector.tensor_tensor(over[:, :, :], inc[:, :, NT - 1:NT].to_broadcast((P, E, NT)),
                                         steps128[:, :, :], ALU.is_gt))
            step(nc.vector.tensor_reduce(ntl[:, :], over[:, :, :], AX.X, ALU.add))
            step(nc.vector.tensor_tensor_scan(ntc[:, :], one_e[:, :], ntl[:, :], 0.0, ALU.mult, ALU.add))
            step(nc.vector.tensor_tensor(base[:, :], ntc[:, :], ntl[:, :], ALU.subtract))
            step(nc.vector.tensor_scalar(base[:, :], base[:, :], float(P), None, ALU.mult))
            step(nc.vector.tensor_tensor(inc[:, :, :], inc[:, :, :], tot[:, :, :], ALU.subtract))
            step(nc.vector.tensor_tensor(slot[:, :, :], CUM, inc[:, :, :].rearrange("p e t -> p t e"), ALU.add))
            step(nc.vector.tensor_tensor(slot[:, :, :], slot[:, :, :],
                                         base[:, :].rearrange("p (a e) -> p a e", a=1).to_broadcast((P, NT, E)), ALU.add))
            step(nc.vector.tensor_tensor_scan(flat(cnt[:, :, :]), flat(restart[:, :, :]), flat(Msel[:, :, :]), 0.0,
                                              ALU.mult, ALU.add))
            for j in range(TOP):
                step(nc.vector.scalar_tensor_tensor(out=pick[:, :, :], in0=cnt[:, :, :], scalar=float(j + 1),
                                                    in1=Msel[:, :, :], op0=ALU.is_equal, op1=ALU.mult))
                step(nc.vector.tensor_tensor(prod[:, :, :], pick[:, :, :], slot[:, :, :], ALU.mult))
                step(nc.vector.tensor_reduce(slot_f[:, j, :], prod[:, :, :], AX.X, ALU.add))
            step(nc.vector.tensor_copy(slot_u[:, :, :], slot_f[:, :, :]))
            step(nc.vector.tensor_tensor(owner[:, :, :],
                                         ntc[0:1, :].rearrange("p (a e) -> p a e", a=1).to_broadcast((1, SLOT_TILES, E)),
                                         tile_no[:, :].rearrange("p (t a) -> p t a", a=1).to_broadcast((1, SLOT_TILES, E)),
                                         ALU.is_le))
            step(nc.vector.tensor_reduce(own1[:, :], owner[:, :, :], AX.X, ALU.add))
            nc.vector.tensor_scalar(tile_expert[:, 0:SLOT_TILES], own1[:, :], float(E - 1), None, ALU.min)\
                .then_inc(s["route_ready"], 1)

            for _ in first:
                pass
            dve.wait_ge(s["route_ready"], 1)
            dve.sem_inc(s["hf_ready"], 2)
            dve.sem_inc(s["hl_ready"], 2)
            dve.sem_inc(s["xc_ready"], 2)

            def low_h(c, m):
                rows_m = FT[m][1]
                dve.wait_ge(s["hh_ready"], c * NF + (m + 1))
                nc.vector.tensor_tensor(h_l[0:rows_m, m, :], hf[0:rows_m, m % 2, :], h_h[0:rows_m, m, :].bitcast(F32),
                                        ALU.subtract).then_inc(s["hl_ready"], 1)

            def gated(c, m):
                if m:
                    low_h(c, m - 1)
                rows_m = FT[m][1]
                dve.wait_ge(s["sg_ready"], c * NF + (m + 1))
                dve.wait_ge(s["gu_ready"], c * 2 * NF + (2 * m + 2))
                dve.wait_ge(s["hl_ready"], c * NF + (m + 1))
                nc.vector.tensor_tensor(hf[0:rows_m, m % 2, :], M[2 * (m % 2) + 1][0:rows_m, :], sg[0:rows_m, m % 2, :],
                                        ALU.mult).then_inc(s["hf_ready"], 1)

            def step_fn(a, b, c, u):
                if a is not None and not (isinstance(a, int) and a == 0):
                    for _ in recurrence(a, u):
                        pass
                if c is not None:
                    for m in CHUNKS.get(u, ())[:-1]:
                        gated(c, m)
                if b is not None:
                    if u == 1:
                        chain = sem_chain(dve, s["head_dve"], 0, 5, b)
                        dve.wait_ge(s["ot_ready"], b * 2 + 2)
                        ot_h = ot[:, :, :].rearrange("p t (h d) -> p (t h) d", d=HD)
                        chain(nc.vector.tensor_reduce(ghead[3][:, :], ot_h, AX.X, ALU.add))
                        chain(nc.vector.tensor_scalar(ghead[3][:, :], ghead[3][:, :], 1.0 / HD, None, ALU.mult))
                        nc.vector.tensor_tensor(ot_h, ot_h,
                                                ghead[3][:, :].rearrange("p (g a) -> p g a", a=1).to_broadcast((P, TPB * H, HD)),
                                                ALU.subtract).then_inc(s["oc_ready"], 1)
                    if u == 2:
                        chain = sem_chain(dve, s["head_dve"], 2, 5, b)
                        dve.wait_ge(s["sq_ready"], b + 1)
                        chain(nc.vector.tensor_reduce(ghead[0][:, :], on[:, :, :].rearrange("p t (h d) -> p (t h) d", d=HD),
                                                      AX.X, ALU.add))
                        chain(nc.vector.tensor_scalar(ghead[0][:, :], ghead[0][:, :], 0.5 / HD, 0.5 * EPS, ALU.mult, ALU.add))
                        rsqrt_seed(chain, ghead[1][:, :], ghead[0][:, :], HALF_MAGIC).then_inc(s["head_seed"], 1)
                    if u == 3:
                        dve.wait_ge(s["head_rstd"], b + 1)
                        for t in range(TPB):
                            nc.vector.tensor_tensor(
                                on[:, t, :].rearrange("p (d h) -> p h d", d=HD), ot[:, t, :].rearrange("p (h d) -> p h d", d=HD),
                                ghead[1][:, t * H:(t + 1) * H].rearrange("p (h a) -> p h a", a=1).to_broadcast((P, H, HD)),
                                ALU.mult).then_inc(s["on_ready"] if t == TPB - 1 else s["on_part"], 1)
                        dve.wait_ge(s["on_part"], b * (TPB - 1) + (TPB - 1))
                    if u == 4:
                        dve.wait_ge(s["gs_ready"], b + 1)
                        for i in range(2):
                            dve.wait_ge(s["tpb_ready"], b * 2 + (i + 1))
                            nc.vector.tensor_tensor(gs[:, i, :], PS[i], gs[:, i, :], ALU.mult).then_inc(s["og_ready"], 1)
                    if u == 5:
                        for i in range(2):
                            dve.wait_ge(s["ogh_ready"], b * 2 + (i + 1))
                            nc.vector.tensor_tensor(og_l[:, i, :], gs[:, i, :], og_h[:, i, :].bitcast(F32),
                                                    ALU.subtract).then_inc(s["ogl_ready"], 1)
                    if u == 6:
                        for i in range(2):
                            dve.wait_ge(s["wo_ready"], b * 2 + (i + 1))
                            xt = xn[:, TILES(b, 2 * i, 2), :].rearrange("p t d -> p (t d)")
                            nc.vector.tensor_tensor(xt, PS[i], xt, ALU.add).then_inc(s["xb_ready"], 1)
                    if u == 6:
                        if c is not None:
                            low_h(c, NF - 1)
                        chain = sem_chain(dve, s["row_dve"], 0, 2, b)
                        dve.wait_ge(s["ms_ready"], b * 4 + 4)
                        chain(nc.vector.tensor_scalar(grow[0][:, :], grow[3][:, :], 0.5 / D, 0.5 * EPS, ALU.mult, ALU.add))
                        rsqrt_seed(chain, grow[1][:, :], grow[0][:, :], HALF_MAGIC).then_inc(s["row_seed"], 1)
                    if u == 7:
                        for t in range(TPB):
                            dve.wait_ge(s["an2h_ready"], b * 4 + (t + 1))
                            nc.vector.scalar_tensor_tensor(
                                out=an2[:, t, 1, :], in0=xn[:, TILES(b, t, 1), :].rearrange("p a d -> p (a d)"), scalar=grow[1][:, t:t + 1],
                                in1=an2[:, t, 0, :], op0=ALU.mult, op1=ALU.subtract).then_inc(s["an2l_ready"], 1)
                if c is not None:
                    if u == 6 and b is None:
                        low_h(c, NF - 1)
                    for m in CHUNKS.get(u, ())[-1:]:
                        gated(c, m)
                    if u == 7:
                        for i in range(2):
                            dve.wait_ge(s["w2_ready"], c * 2 + (i + 3))
                            xt = xn[:, TILES(c, 2 * i, 2), :].rearrange("p t d -> p (t d)")
                            nc.vector.tensor_tensor(xt, M[i], xt, ALU.add).then_inc(s["xc_ready"], 1)
                for e in experts_at(c, b, u):
                    dve.wait_ge(s["ewh_ready"], e + 1)
                    nc.vector.tensor_tensor(w_gu[:, e, 1, :, :], gu_raw[:, e + 1, :, :], w_gu[:, e, 0, :, :],
                                            ALU.subtract).then_inc(s["ew_ready"], 1)

            turns(dve, step_fn)

            attention_over(dve)
            dve.sem_inc(s["xe_ready"], 2)
            dve.sem_inc(s["hm_ready"], 2)

            def rows_out(g, u):
                dve.wait_ge(s["xt_ready"], g * UN + (u + 1))
                dve.wait_ge(s["eg_ready"], g * UN + (u + 1))
                nc.vector.tensor_copy(xT[:, u % 2, :, :, :].rearrange("p a c n -> p (a c n)"), PS[u % 2]).then_inc(s["xe_ready"], 1)

            def hidden(g, u):
                dve.wait_ge(s["sl_ready"], g * UN + (u + 1))
                dve.wait_ge(s["ht_ready"], g * UN + (u + 1))
                nc.vector.scalar_tensor_tensor(out=h[:, u % 2, :], in0=M[u % 2][:, I:2 * I], scalar=X[:, u, SCALE_C:SCALE_C + 1],
                                               in1=sl[:, u % 2, :], op0=ALU.mult, op1=ALU.mult).then_inc(s["hm_ready"], 1)

            def tiles(g, last):
                for u in range(UN):
                    if not (last and u >= UN - 2):
                        rows_out(g + (u + 2) // UN, (u + 2) % UN)
                    if not (last and u == UN - 1):
                        hidden(g + (u + 1) // UN, (u + 1) % UN)

            rows_out(0, 0)
            rows_out(0, 1)
            hidden(0, 0)
            with dve.Fori(0, GROUPS - 1) as g:
                tiles(g, False)
            tiles(GROUPS - 1, True)
            for c in range(B):
                dve.wait_ge(fin_in[c], 32)
                nc.vector.tensor_tensor(ysum[c], ysum[c], ysum2[c], ALU.add).then_inc(s["ysum_ready"], 1)
            dve.wait_ge(s["xr_in"], 16 * B)
            for c in range(B):
                dve.wait_ge(s["silu_ready"], c + 1)
                nc.vector.tensor_tensor(ysum[c], ysum2[c], xn[:, c * TPB:(c + 1) * TPB, :].rearrange("p t d -> p (t d)"),
                                        ALU.mult).then_inc(s["fin_mul"], 1)
                dve.wait_ge(s["fin_mul"], c + 1)
                nc.vector.tensor_tensor(ysum[c], ysum[c], xback[c], ALU.add).then_inc(s["out_ready"], 1)

        @block.tensor
        def _(pe):
            pe.wait_ge(s["const_pool"], 1)
            pe.wait_ge(s["wz_in"], 48)
            for c in range(KC):
                last = nc.tensor.transpose(WK1p[:, c, :], wk1[:, c, :], ident[:, :])
            last.then_inc(s["wk1_t"], 1)
            for c in range(KC):
                last = nc.tensor.transpose(RWp[:, c, :], rw_raw[:, c * P:(c + 1) * P], ident[0:E, 0:E])
            last.then_inc(s["rw_t"], 1)
            pe.wait_ge(s["wk1_copied"], 1)
            for c in range(KC):
                last = nc.tensor.matmul(Zp[:, c, :], wk1T[:, c, :], wk2[:, :], start=True, stop=True)
            last.then_inc(s["wz_ready"], 1)
            pe.wait_ge(s["wprep_dve"], NWPREP)

            def turn_rows(t, j):
                pe.wait_ge(s["anl_ready"], t + 1)
                pe.wait_ge(s["tp_evac"], t + 1)
                for n in range(2 * KC):
                    last = nc.tensor.matmul(PS[j % 2][:, n * P:(n + 1) * P],
                                            rows16[:, bass.ds(t, 1), n * P:(n + 1) * P].rearrange("p a d -> p (a d)"),
                                            ident16[:, :], start=True, stop=True)
                last.then_inc(s["tp_ready"], 1)

            def turn(b, more):
                cols = [QC, ZC, KCOL, VC, VC + P, GC, GC + P]
                free = [(s["evac_dve"], b * 3 + 2), (s["evac_act"], b * 4 + 1), (s["evac_act"], b * 4 + 2),
                        (s["evac_dve"], b * 3 + 1), (s["evac_act"], b * 4 + 3), (s["evac_dve"], b * 3 + 3),
                        (s["evac_act"], b * 4 + 4)]
                pe.wait_ge(s["tp_evac"], b * TPB + TPB + 2)
                for i, col in enumerate(cols):
                    pe.wait_ge(*free[i])
                    triple(pe, M[i % 4],
                           [(w_a[:, wl, c, col:col + P], anT[:, hl, c, bass.ds(b * L, L)])
                            for c in range(KC) for hl, wl in ((0, 0), (0, 1), (1, 0))]).then_inc(s["proj_ready"], 1)
                    if i < TPB:
                        t = b * TPB + i
                        triple(pe, O1[:, bass.ds(t * E, E)],
                               [(anT[:, hl, c, bass.ds(t * P, P)], rw[:, wl, c, :])
                                for c in range(KC) for hl, wl in ((0, 0), (0, 1), (1, 0))]).then_inc(s["logits_ready"], 1)
                        if more:
                            turn_rows((b + 1) * TPB + i, i)

            for j in range(TPB):
                turn_rows(j, j)
            with pe.Fori(0, B - 1) as b:
                turn(b, True)
            turn(B - 1, False)
            pe.wait_ge(s["m16_ready"], 1)
            pe.wait_ge(s["tp_evac"], NT + 2)
            sel = M16[:, :, :].rearrange("p t e -> p (t e)")
            nc.tensor.matmul(T0[:, 0:NT * E], before16[:, :], sel, start=True, stop=True)
            nc.tensor.matmul(T0[:, NT * E:2 * NT * E], ones16[:, :], sel, start=True, stop=True).then_inc(s["cum_ready"], 1)

            pe.wait_ge(s["lg_ready"], 1)
            pe.wait_ge(s["evac_dve"], 3 * B + 2)
            pe.wait_ge(s["evac_act"], 4 * B + 2)
            pe.sem_inc(s["gla_used"], 2)
            pe.sem_inc(s["w2_ready"], 2)

            def read_out(a, u):
                pe.wait_ge(s["qs_ready"], a * U + (u + 3))
                if u % 4 == 0:
                    pe.wait_ge(s["oT_evac"], a * 2 + (u // 4 + 1))
                for j in range(2):
                    dd = (2 * u + j) % DH
                    off = P - H - dd * H
                    last = nc.tensor.matmul(sum_ps[:, u // 4, :], sumk[:, off:off + P], qs[:, u % 2, j, :],
                                            start=(dd == 0), stop=(dd == DH - 1))
                last.then_inc(s["gla_used"], 1)

            def w2_products(c, u):
                pe.wait_ge(s["hl_ready"], c * NF + (NF + 2))
                for t in (2 * (u - NF), 2 * (u - NF) + 1):
                    last = triple(pe, M[u - NF][:, (t % 2) * D:(t % 2 + 1) * D],
                                  [(h[0:mw, m, t * P:(t + 1) * P], w[0:mw, m, :])
                                   for m, (_, mw) in enumerate(FT)
                                   for h, w in ((h_h, w2_h), (h_h, w2_l), (h_l, w2_h))])
                last.then_inc(s["w2_ready"], 1)

            def gate_up_mlp(c, m):
                f, rows_m = FT[m]
                if m == 0:
                    pe.wait_ge(s["an2T_evac"], c * 4 + 4)
                    pe.wait_ge(s["xc_ready"], c * 2 + 2)
                pe.wait_ge(s["hf_ready"], c * NF + (m + 1))
                for i in range(2):
                    triple(pe, M[2 * (m % 2) + i][0:rows_m, :],
                           [(w13[:, wl, kc, i * F + f:i * F + f + rows_m], an2T[:, hl, kc, :])
                            for kc in range(KC) for hl, wl in ((0, 0), (0, 1), (1, 0))]).then_inc(s["gu_ready"], 1)

            def step_fn(a, b, c, u):
                chunks = CHUNKS.get(u, ()) if c is not None else ()
                for m in chunks[:1]:
                    gate_up_mlp(c, m)
                if a is not None and u > 0:
                    read_out(a, u - 1)
                if b is not None:
                    if u == 0:
                        wait(pe, s["an2T_evac"], b * 4)
                        if isinstance(b, int) and b == 0:
                            pe.wait_ge(s["route_ready"], 1)
                        for i in range(2):
                            for n in range(4):
                                t, kc = 2 * i + n // 2, n % 2
                                pe.wait_ge(s["oT_evac"], b * 2 + (kc + 3))
                                last = nc.tensor.transpose(PS[i][:, n * P:(n + 1) * P], oT[:, kc, t * P:(t + 1) * P], ident[:, :])
                            last.then_inc(s["tpo_ready"], 1)
                    if u == 3:
                        pe.wait_ge(s["on_ready"], b + 1)
                        for i in range(2):
                            for t in range(TPB):
                                last = nc.tensor.transpose(PS[i][:, t * P:(t + 1) * P], on[:, t, i * P:(i + 1) * P], ident[:, :])
                            last.then_inc(s["tpb_ready"], 1)
                    if u == 5:
                        pe.wait_ge(s["ogl_ready"], b * 2 + 2)
                        for t in range(TPB):
                            last = triple(pe, PS[t // 2][:, (t % 2) * D:(t % 2 + 1) * D],
                                          [(og[:, kc, t * P:(t + 1) * P], wo[:, kc, :])
                                           for kc in range(KC) for og, wo in ((og_h, wo_h), (og_h, wo_l), (og_l, wo_h))])
                            if t % 2:
                                last.then_inc(s["wo_ready"], 1)
                    if u == 7:
                        if c is not None:
                            w2_products(c, u)
                        pe.wait_ge(s["an2l_ready"], b * 4 + 4)
                        for part in range(2):
                            for i in range(KC):
                                if part:
                                    pe.wait_ge(s["an2T_evac"], b * 4 + (i + 1))
                                for t in range(TPB):
                                    last = nc.tensor.matmul(PS[i][:, t * P:(t + 1) * P], an2[:, t, part, i * P:(i + 1) * P],
                                                            ident16[:, :], start=True, stop=True)
                                last.then_inc(s["tpn_ready"], 1)
                for m in chunks[1:]:
                    gate_up_mlp(c, m)
                if c is not None and (u == 6 or u == 7 and b is None):
                    w2_products(c, u)
                if a is not None and u == U - 1:
                    read_out(a, u)

            turns(pe, step_fn)

            attention_over(pe)
            pe.sem_inc(s["eg_ready"], 2)
            pe.sem_inc(s["ht_ready"], 2)
            pe.sem_inc(s["dn_ready"], 2)

            def transpose_rows(g, u):
                pe.wait_ge(x_in[u], 16 * (g + 1))
                pe.wait_ge(s["xe_ready"], g * UN + (u + 1))
                for n in range(2 * KC):
                    last = nc.tensor.matmul(PS[u % 2][:, n * P:(n + 1) * P], X16[:, u, n * P:(n + 1) * P], ident16[:, :],
                                            start=True, stop=True)
                last.then_inc(s["xt_ready"], 1)

            def gate_up(g, u, e):
                pe.wait_ge(s["ew_ready"], e + 1)
                pe.wait_ge(s["xe_ready"], g * UN + (u + 3))
                pe.wait_ge(s["hm_ready"], g * UN + (u + 1))
                triple(pe, M[u % 2][:, 0:2 * I],
                       [(xT[:, u % 2, hl, kc, :], w_gu[:, bass.ds(e, 1), wl, kc, :].rearrange("p a n -> p (a n)"))
                        for kc in range(KC) for hl, wl in ((0, 0), (0, 1), (1, 0))]).then_inc(s["eg_ready"], 1)

            def transpose_hidden(g, u):
                pe.wait_ge(s["hm_ready"], g * UN + (u + 3))
                pe.wait_ge(s["he_ready"], g * UN + (u + 1))
                for i in range(IC):
                    last = nc.tensor.transpose(M[2 + u % 2][0:HK, i * P:(i + 1) * P], h[:, u % 2, i * HK:(i + 1) * HK], ident[:, :])
                last.then_inc(s["ht_ready"], 1)

            def down(g, u, e):
                pe.wait_ge(s["he_ready"], g * UN + (u + 3))
                pe.wait_ge(s["ye_ready"], g * UN + (u + 1))
                triple(pe, sum_ps[:, u % 2, 0:D],
                       [(hT[:, u % 2, i, :], wd[:, bass.ds(e, 1), i, :].rearrange("p a n -> p (a n)")) for i in range(IC)])\
                    .then_inc(s["dn_ready"], 1)

            def tiles(g, last):
                e = expert(pe, g * UN)
                for u in range(UN):
                    ahead = not (last and u == UN - 1)
                    if ahead:
                        e_next = expert(pe, g * UN + u + 1)
                        gate_up(g + (u + 1) // UN, (u + 1) % UN, e_next)
                    if not (last and u >= UN - 2):
                        transpose_rows(g + (u + 2) // UN, (u + 2) % UN)
                    transpose_hidden(g, u)
                    if u > 0:
                        down(g, u - 1, e_before)
                    e_before, e = e, e_next
                down(g, UN - 1, e_before)

            transpose_rows(0, 0)
            transpose_rows(0, 1)
            gate_up(0, 0, expert(pe, 0))
            pe.wait_ge(s["wd_in"], 32)
            with pe.Fori(0, GROUPS - 1) as g:
                tiles(g, False)
            tiles(GROUPS - 1, True)


_INS = [f"L0_attn_{n}" for n in ("x", "Wq", "Wk", "Wkg1", "Wkg2", "bkg2", "Wv", "Wg", "bg", "Wo", "ln1_w", "ln2_w",
                                 "W1", "W3", "W2")] + \
       [f"L0_ffn_{n}" for n in ("router_w", "expert_bias", "gate_proj", "up_proj", "down_proj")]
_OUTS = [((4, 512, 256), "float32")]


def kernel(**inputs):
    import numpy as _np
    import concourse.bacc as _bacc
    from concourse import mybir as _mybir
    from concourse.bass_utils import run_bass_kernel_spmd as _run

    nc = _bacc.Bacc("TRN2", target_bir_lowering=False, num_devices=1)
    arrays, args = {}, []
    for name in _INS:
        a = _np.ascontiguousarray(inputs[name])
        arrays[f"in_{name}_dram"] = a
        args.append(nc.dram_tensor(f"in_{name}_dram", a.shape, _mybir.dt.from_np(a.dtype), kind="ExternalInput").ap())
    for i, (shape, dtype) in enumerate(_OUTS):
        dt = _mybir.dt.from_np(_np.dtype(dtype))
        args.append(nc.dram_tensor(f"out_{i}_dram", shape, dt, kind="ExternalOutput").ap())
    build_block(nc, *args)
    r = _run(nc, [arrays], core_ids=[0])
    return r.results[0]["out_0_dram"]
```

```python
from contextlib import ExitStack

import concourse.bass as bass
from concourse import mybir

F32 = mybir.dt.float32
F32R = mybir.dt.float32r
F16 = mybir.dt.float16
I32 = mybir.dt.int32
U32 = mybir.dt.uint32
ALU = mybir.AluOpType
ACT = mybir.ActivationFunctionType
AX = mybir.AxisListType

P = 128
EPS = 1e-5
RSQRT_MAGIC = 0x5F3759DF
NEG_HALF_MAGIC = RSQRT_MAGIC - 0x400000 + 0x40000000
NEWTON = 3

def sem_chain(eng, sem, base, per=0, it=0, between=None):
    count = [base]

    def step(ins):
        if ins is None:
            return count[0]
        count[0] += 1
        ins.then_inc(sem, 1)
        if between:
            between()
        eng.wait_ge(sem, it * per + count[0])
        return count[0]

    return step

def build_block(nc, x, Wq, Wk, Wkg1, Wkg2, bkg2, Wv, Wg, bg, Wo, ln1_w, ln2_w, W1, W3, W2,
                router_w, expert_bias, gate_proj, up_proj, down_proj, out):
    B, L, D = x.shape
    T = B * L
    NT = T // P
    TPB = L // P
    KC = D // P
    E, _, I = gate_proj.shape
    F = W1.shape[1]
    QK = Wq.shape[1]
    R = Wkg1.shape[1]
    H = 16
    KD = QK // H
    HD = D // H
    DH = HD // KC
    KS = float(HD) ** -0.5
    NORMALIZER = 16.0
    TOP = 4
    SLOT_TILES = -(-(T * TOP // P + E - 1) // 4) * 4
    SLOTS = SLOT_TILES * P
    ROW = D + 2 + E
    SCALE_C, TOKEN_C, WEIGHT_C = D, D + 1, D + 2
    HK = I // 2
    IC = 2
    assert QK == P and D == 2 * P and B * H * KD * HD == 4 * P * HD and L == 512

    QC, KCOL, ZC, VC, GC = 0, QK, 2 * QK, 3 * QK, 3 * QK + D
    WA = 3 * QK + 2 * D
    FT = [(c * P, min(P, F - c * P)) for c in range((F + P - 1) // P)]
    NF = len(FT)
    FULL = F // P * P
    REST = F - FULL
    assert 2 * REST == P
    HP = [slice(0, P)] * (NF - 1) + [slice(REST, P)]

    xr = x.rearrange("b l d -> (b l) d").rearrange("(t p) d -> p t d", p=P)
    outr = out.rearrange("b l d -> (b l) d").rearrange("(t p) d -> p t d", p=P)

    v_dram = nc.dram_tensor("v_scratch", (B, HD, H, L), F32, kind="Internal").ap()
    rows_dram = nc.dram_tensor("rows_scratch", (SLOTS, ROW), F32, kind="Internal").ap()
    y_dram = [nc.dram_tensor(f"y_scratch{i}", (T + P, D), F32, kind="Internal").ap() for i in range(2)]

    with ExitStack() as ctx:
        def sem(name):
            return ctx.enter_context(nc.semaphore(name))

        def sb(name, shape, dt, scope=ctx):
            return scope.enter_context(nc.sbuf_tensor(name, shape, dt))

        xn = sb("xn", [P, NT, D], F32)
        ident = sb("ident", [P, P], F32)
        ident16 = sb("ident16", [P, P], F16)
        slot_u = sb("slot_u", [P, TOP, NT], U32)
        tile_expert = sb("tile_expert", [1, SLOT_TILES], U32)

        ones16 = sb("ones16", [P, P], F16)
        before16 = sb("before16", [P, P], F16)
        sumk = sb("sumk", [P, 2 * P - H], F32)
        head_i = sb("head_i", [P, H], I32)
        head_m = sb("head_m", [P, H], I32)
        restart = sb("restart", [P, NT, E], F32)
        one_e = sb("one_e", [P, E], F32)
        steps128 = sb("steps128", [P, E, NT], F32)
        tile_no = sb("tile_no", [1, SLOT_TILES], F32)
        ln1 = sb("ln1", [P, KC], F32)
        ln1k = sb("ln1k", [P, KC], F32)
        ln2 = sb("ln2", [P, KC], F32)
        bz = sb("bz", [P, 1], F32)
        bgT = sb("bgT", [P, KC], F32)
        eb = sb("eb", [P, E], F32)
        bst = sb("bst", [P, NT, 6], F32)
        mv = sb("mv", [P, NT, 2], F32)
        rs_v = sb("rs_v", [P, 4, NT], F32)
        rstd = sb("rstd", [P, NT], F32)
        r1 = sb("r1", [P, NT], F32)
        negmr = sb("negmr", [P, NT], F32)

        att = ExitStack()
        q_sb = sb("q_sb", [P, T], F32, att)
        k_sb = sb("k_sb", [P, T], F32, att)
        a_sb = sb("a_sb", [P, T], F32, att)
        pre1 = ExitStack()
        w13_raw = sb("w13_raw", [P, KC, 2 * F], F32, pre1)
        wo_raw = sb("wo_raw", [P, KC, D], F32, pre1)
        w2_raw = sb("w2_raw", [P, NF, D], F32, pre1)
        vt = sb("vt", [P, 2, L], F32, pre1)
        zb = sb("zb", [P, L], F32, pre1)
        zabs = sb("zabs", [P, L], F32, pre1)
        zexp = sb("zexp", [P, L], F32, pre1)
        zln = sb("zln", [P, L], F32, pre1)
        pre1.close()
        vrep = sb("vrep", [P, 2, 2, L], F32, att)
        kv = sb("kv", [P, 2, 2, L], F32, att)
        st = sb("st", [P, 2, 2, L], F32, att)
        qs = sb("qs", [P, 2, 2, L], F32, att)
        zrow_f = sb("zrow", [P, 2 * P + 32], F32, att)
        zrow = zrow_f[:, 0:ROW]
        sb("fill1", [P, KC * 2 * I - 2 * P - 32], F32, att)
        g_sb = sb("g_sb", [P, KC, T], F32, att)
        wo_h = sb("wo_h", [P, KC, D], F32R, att)
        wo_l = sb("wo_l", [P, KC, D], F32R, att)
        w13 = sb("w13", [P, 2, KC, 2 * F], F16, att)
        w2_h = sb("w2_h", [P, NF, D], F32R, att)
        w2_l = sb("w2_l", [P, NF, D], F32R, att)
        rows = sb("rows", [P, NT, ROW], F32, att)
        rows16 = rows[:, :, :].bitcast(F16)
        pre = ExitStack()
        w_a = sb("w_a", [P, 2, KC, WA], F16, pre)
        anT = sb("anT", [P, 2, KC, T], F16, pre)
        wa_raw = sb("wa_raw", [P, KC, WA], F32, pre)
        wk2 = sb("wk2", [R, QK], F32, pre)
        wk1 = sb("wk1", [P, KC, R], F32, pre)
        wk1T = sb("wk1T", [R, KC, P], F32, pre)
        rw_raw = sb("rw_raw", [E, D], F32, pre)
        rw = sb("rw", [P, 2, KC, E], F16, pre)
        zls = sb("zls", [P, L], F32, pre)
        pre.close()
        oT = sb("oT", [P, KC, L], F32, att)
        ot = sb("ot", [P, TPB, D], F32, att)
        on = sb("on", [P, TPB, D], F32, att)
        gs = sb("gs", [P, KC, L], F32, att)
        og_h = sb("og_h", [P, KC, L], F32R, att)
        og_l = sb("og_l", [P, KC, L], F32R, att)
        an2 = sb("an2", [P, TPB, 2, D], F16, att)
        an2T = sb("an2T", [P, 2, KC, L], F16, att)
        ghead = [sb(f"ghead{i}", [P, TPB * H], F32, att) for i in range(4)]
        grow = [sb(f"grow{i}", [P, TPB], F32, att) for i in range(4)]
        rt = ExitStack()
        def rsb(name, shape=(P, NT, E), dt=F32):
            return sb(name, list(shape), dt, rt)
        lg = rsb("lg")
        mx = rsb("mx", (P, NT))
        m8 = rsb("m8", (P, NT, 8))
        gt = rsb("gt")
        eq = rsb("eq")
        need = rsb("need", (P, NT))
        eqc = rsb("eqc")
        Msel = rsb("Msel")
        M16 = rsb("M16", dt=F16)
        ex = rsb("ex")
        sm = rsb("sm", (P, NT))
        wgt = rsb("wgt")
        tot = rsb("tot", (P, E, NT))
        inc = rsb("inc", (P, E, NT))
        over = rsb("over", (P, E, NT))
        ntl = rsb("ntl", (P, E))
        ntc = rsb("ntc", (P, E))
        base = rsb("base", (P, E))
        slot = rsb("slot")
        cnt = rsb("cnt")
        pick = rsb("pick")
        prod = rsb("prod")
        slot_f = rsb("slot_f", (P, TOP, NT))
        owner = rsb("owner", (1, SLOT_TILES, E))
        own1 = rsb("own1", (1, SLOT_TILES))

        rt.close()
        sg = sb("sg", [P, 2, L], F32, att)
        hf = sb("hf", [P, 2, L], F32, att)
        h_h = sb("h_h", [P, NF, L], F32R, att)
        h_l = sb("h_l", [P, NF, L], F32R, att)
        att.close()

        UN = 16
        w_gu_f = sb("w_gu", [P, E + 1, KC * 2 * I], F32)
        w_gu = w_gu_f[:, :, :].bitcast(F16).rearrange("p e (a c n) -> p e a c n", a=2, c=KC)
        gu_raw = w_gu_f[:, :, :].rearrange("p e (c n) -> p e c n", c=KC)
        X = sb("X", [P, UN, ROW], F32)
        X16 = X[:, :, :].bitcast(F16)
        sb("fill2", [P, KC * T + 2 * KC * D - UN * ROW], F32)
        xT = sb("xT", [P, 2, 2, KC, P], F16)
        y = sb("y", [P, UN, D], F32)
        sl = sb("sl", [P, 2, I], F32)
        h = sb("h", [P, 2, I], F32)
        hT = sb("hT", [HK, 2, IC, P], F32)
        xback_f = sb("xback", [P, NT, D], F32)
        sb("fill3", [P, 2 * KC * F + 2 * NF * D + NT * ROW - UN * D - 2 * KC * P - 4 * I - 2 * IC * P - NT * D], F32)
        wd = sb("wd", [HK, E, IC, D], F32)
        sum_f = w_gu_f[:, :, :].rearrange("p e n -> p (e n)")

        turn_ps = ctx.enter_context(nc.psum_tensor("turn_ps", [P, 2, 512], F32))
        mm_ps = ctx.enter_context(nc.psum_tensor("mm_ps", [P, 4, 512], F32))
        sum_ps = ctx.enter_context(nc.psum_tensor("sum_ps", [P, 2, 512], F32))
        PS = T0, T1 = [turn_ps[:, i, :] for i in range(2)]
        M = [mm_ps[:, i, :] for i in range(4)]
        O0, O1 = [sum_ps[:, i, :] for i in range(2)]

        s = {n: sem(n) for n in """
            const_pool const_dve x_in0 x_in1 x_in2 x_in3 wa_in wz_in small_in stats rsq_seed rsq_done1 rsq_seed2
            rsq_done2 xn_ready anh_ready anl_ready wk1_t wk1_copied wz_ready rw_t wprep_act wprep_dve w13_in
            wo_in w2_in zero_fill tp_ready tp_evac proj_ready evac_act evac_dve zb_ready zln_ready zls_ready
            a_ready logits_ready dve_chain pool_chain act_chain exp_ready m16_ready cum_ready route_ready ex_in
            scatter zero_row ln1k_ready cscale dve_max vt_ready vt_out0 vt_out1 prep_done lg_ready vr_in0 vr_in1
            kv_ready st_ready qs_ready gla_used oT_evac pool_turn act_turn tpo_ready ot_ready oc_ready sq_ready
            head_dve on_ready on_part tpb_ready gs_ready og_ready ogh_ready ogl_ready wo_ready xb_ready ms_ready
            row_dve row_rstd an2h_ready an2l_ready tpn_ready an2T_evac gu_ready sg_ready hf_ready hh_ready
            hl_ready w2_ready xc_ready y_zero ew_ready ewh_ready wd_in xt_ready xe_ready eg_ready sl_ready
            hm_ready ht_ready he_ready dn_ready ye_ready y_out0 y_out1 y_slots act_turn3 xr_in ysum_ready
            silu_ready tile_chain tiles_named fin_mul out_ready out_done""".split()}
        y_out = [s["y_out0"], s["y_out1"]]
        x_in = [sem(f"row_in{i}") for i in range(UN)]
        raw_in = [sem(f"raw_in{i}") for i in range(E // 2)]
        vr_in = [s["vr_in0"], s["vr_in1"]]
        vt_out = [s["vt_out0"], s["vt_out1"]]

        def rsqrt_seed(step, r, v, magic=RSQRT_MAGIC):
            step(nc.vector.tensor_scalar(r.bitcast(I32), v.bitcast(I32), 1, None, ALU.logical_shift_right))
            nc_i = nc.vector.tensor_scalar(r.bitcast(I32), r.bitcast(I32), -1.0, float(magic), ALU.mult, ALU.add)
            return nc_i

        def rsqrt_newton(eng, step, r, v, t):
            for n in range(NEWTON):
                step(eng.tensor_tensor(t, r, r, ALU.mult))
                step(eng.tensor_tensor(t, t, v, ALU.mult))
                step(eng.tensor_scalar(t, t, -0.5, 1.5, ALU.mult, ALU.add))
                ins = eng.tensor_tensor(r, r, t, ALU.mult)
                if n < NEWTON - 1:
                    step(ins)
            return ins

        def rsqrt_newton_neg(step, r, neg_half_v, t):
            for n in range(NEWTON):
                step(nc.vector.tensor_tensor(t, r, r, ALU.mult))
                step(nc.vector.tensor_tensor(t, t, neg_half_v, ALU.mult))
                ins = nc.vector.scalar_tensor_tensor(out=r, in0=t, scalar=1.5, in1=r, op0=ALU.add, op1=ALU.mult)
                if n < NEWTON - 1:
                    step(ins)
            return ins

        xq = [s[f"x_in{c}"] for c in range(B)]
        NSMALL = 2 + 1 + KC + 1
        NWPREP = 4 * KC + KC + 1
        WK1p = T0[0:R, 0:KC * P].rearrange("p (c n) -> p c n", c=KC)
        RWp = T1[:, 0:KC * E].rearrange("p (c n) -> p c n", c=KC)
        Zp = M[0][:, 0:KC * QK].rearrange("p (c n) -> p c n", c=KC)

        def hk_view(ap, from_hk):
            return ap.rearrange("p (h k) -> p k h", k=KD) if from_hk else ap.rearrange("p (k h) -> p k h", k=KD)

        def wparts(c, part):
            w = lambda col: w_a[:, part, c, col:col + QK]
            for col, scale in ((QC, ln1[:, c:c + 1]), (KCOL, ln1k[:, c:c + 1])):
                yield hk_view(w(col), False), hk_view(wa_raw[:, c, col:col + QK], True), scale
            for col in (VC, GC):
                yield (w_a[:, part, c, col:col + D].rearrange("p (d h) -> p d h", d=HD),
                       wa_raw[:, c, col:col + D].rearrange("p (h d) -> p d h", d=HD), ln1[:, c:c + 1])

        def triple(pe, out_ap, pairs):
            for n, (lhsT, rhs) in enumerate(pairs):
                last = nc.tensor.matmul(out_ap, lhsT, rhs, start=(n == 0), stop=(n == len(pairs) - 1))
            return last

        U = HD // 2
        TOK = lambda b: bass.ds(b * L, L)
        TILES = lambda b, i=0, n=TPB: bass.ds(b * TPB + i, n)
        pair_bc = lambda ap: ap.rearrange("p (a l) -> p a l", a=1).to_broadcast((P, 2, L))

        def wait(eng, sem_, value):
            if not isinstance(value, int) or value > 0:
                eng.wait_ge(sem_, value)

        def turns(eng, step_fn):
            for it in (0, 1):
                for u in range(U):
                    step_fn(it, it - 1 if it else None, None, u)
            with eng.Fori(2, B) as it:
                for u in range(U):
                    step_fn(it, it - 1, it - 2, u)
            for it in (B, B + 1):
                for u in range(U):
                    step_fn(None, it - 1 if it == B else None, it - 2, u)

        head4 = lambda ap: ap.rearrange("p (t h) -> p t h", t=TPB)

        def attention_over(eng):
            eng.wait_ge(s["xc_ready"], 2 * B + 2)

        GROUPS = SLOT_TILES // UN

        def expert(eng, t):
            return eng.value_load(tile_expert[0:1, bass.ds(t, 1)], min_val=0, max_val=E - 1)

        PIECES = NT // 2
        TPP = NT // PIECES
        ysum = [sum_f[:, c * TPP * D:(c + 1) * TPP * D] for c in range(PIECES)]
        ysum2 = [sum_f[:, (PIECES + c) * TPP * D:(PIECES + c + 1) * TPP * D] for c in range(PIECES)]
        xback = [xback_f[:, c * TPP:(c + 1) * TPP, :].rearrange("p t d -> p (t d)") for c in range(PIECES)]

        def experts_at(c, u):
            if not isinstance(c, int):
                return ()
            e = (c - B + 2) * U + u - 1
            return (E - 2, E - 1) if e == E - 2 else (e,) if e >= 0 else ()

        block = ctx.enter_context(nc.Block())

        @block.sync
        def _(sp):
            for c in range(B):
                sp.dma_start(xn[:, c * TPB:(c + 1) * TPB, :], xr[:, c * TPB:(c + 1) * TPB, :]).then_inc(xq[c], 16)
            for w, col in ((Wq, QC), (Wk, KCOL)):
                sp.dma_start(wa_raw[:, :, col:col + QK], w.rearrange("(c p) n -> p c n", p=P)).then_inc(s["wa_in"], 16)
            for w, col in ((Wv, VC), (Wg, GC)):
                sp.dma_start(wa_raw[:, :, col:col + D], w.rearrange("(c p) n -> p c n", p=P)).then_inc(s["wa_in"], 16)
            for i, w in enumerate((W1, W3)):
                w_rows = w.rearrange("(c p) n -> p c n", p=P)
                sp.dma_start(w13_raw[:, :, i * FULL:(i + 1) * FULL], w_rows[:, :, 0:FULL]).then_inc(s["w13_in"], 16)
                sp.dma_start(w13_raw[:, :, 2 * FULL + i * REST:2 * FULL + (i + 1) * REST],
                             w_rows[:, :, FULL:F]).then_inc(s["w13_in"], 16)
            for c in range(KC):
                sp.dma_start(wo_raw[:, c, :], bass.AP(tensor=Wo.tensor, offset=Wo.offset + c * DH * D,
                                                      ap=[[D, DH], [HD * D, H], [1, D]])).then_inc(s["wo_in"], 16)
            nfull = F // P
            sp.dma_start(w2_raw[:, 0:nfull, :], W2[0:nfull * P].rearrange("(c p) n -> p c n", p=P)).then_inc(s["w2_in"], 16)
            sp.dma_start(w2_raw[HP[-1], nfull, :], W2[nfull * P:F]).then_inc(s["w2_in"], 16)
            sp.sem_inc(vt_out[0], 16)
            sp.sem_inc(vt_out[1], 16)

            def store_values(b):
                for c in range(2):
                    sp.wait_ge(s["vt_ready"], b * 2 + (c + 1))
                    sp.dma_start(v_dram[bass.ds(b, 1), c * DH:(c + 1) * DH].rearrange("b d h l -> (b d h) l"),
                                 vt[:, c, :]).then_inc(vt_out[c], 16)

            def load_values(b, u):
                for j in range(2):
                    src = v_dram[bass.ds(b, 1), 2 * u + j].rearrange("b h l -> (b h) l")
                    sp.dma_start(vrep[:, u % 2, j, :], bass.AP(tensor=src.tensor, offset=src.offset,
                                                               ap=[[0, KD], [L, H], [1, L]])).then_inc(vr_in[u % 2], 16)

            with sp.Fori(0, B - 1) as b:
                store_values(b)
            sp.wait_ge(vt_out[0], 16 * 2)
            sp.wait_ge(s["prep_done"], 1)
            for u in range(2):
                load_values(0, u)
            store_values(B - 1)
            for c in range(2):
                sp.wait_ge(vt_out[c], 16 * (B + 1))
            for u in range(2, U):
                sp.wait_ge(s["kv_ready"], u + 1)
                load_values(0, u)
            with sp.Fori(1, B) as b:
                for u in range(U):
                    sp.wait_ge(s["kv_ready"], b * U + (u + 1))
                    load_values(b, u)
            sp.wait_ge(s["gla_used"], U * B + 2)
            sp.wait_ge(s["zero_fill"], 16 * NT)
            sp.wait_ge(s["y_zero"], 16 * U)
            for e in range(E):
                for i, w in enumerate((gate_proj, up_proj)):
                    sp.dma_start(gu_raw[:, e + 1, :, i * I:(i + 1) * I],
                                 w[e].rearrange("(c p) n -> p c n", p=P)).then_inc(raw_in[e // 2], 16)
            def load_down(e0, e1):
                sp.dma_start(wd[:, e0:e1, :, :].rearrange("p e i d -> p (e i) d"),
                             down_proj[e0:e1].rearrange("e (i p) d -> p (e i) d", p=HK)).then_inc(s["wd_in"], 16)

            def load_rows(g, u):
                sp.dma_start(X[:, u, :], rows_dram[bass.ds((g * UN + u) * P, P), :]).then_inc(x_in[u], 16)

            sp.wait_ge(s["tpn_ready"], 4 * B)
            load_down(0, E - 2)
            sp.wait_ge(s["scatter"], 16 * NT * TOP)
            for u in range(UN):
                load_rows(0, u)
            sp.wait_ge(s["gu_ready"], 2 * NF * B)
            load_down(E - 2, E)
            attention_over(sp)
            sp.dma_start(xback_f[:, :, :], xr).then_inc(s["xr_in"], 16)
            with sp.Fori(1, GROUPS) as g:
                for u in range(UN):
                    sp.wait_ge(s["y_slots"], g * UN + (u + 3))
                    load_rows(g, u)
            for i in range(2):
                sp.wait_ge(y_out[i], 16 * SLOT_TILES // 2)
            sp.wait_ge(s["eg_ready"], SLOT_TILES + 2)
            for c in range(PIECES):
                for i, dst in enumerate((ysum, ysum2)):
                    sp.dma_start(dst[c].rearrange("p (t d) -> p t d", t=TPP),
                                 y_dram[i].rearrange("(t p) d -> p t d", p=P)[:, c * TPP:(c + 1) * TPP, :])\
                        .then_inc(x_in[c], 16)
            for c in range(PIECES):
                sp.wait_ge(s["out_ready"], c + 1)
                sp.dma_start(outr[:, c * TPP:(c + 1) * TPP, :], ysum[c].rearrange("p (t d) -> p t d", t=TPP))\
                    .then_inc(s["out_done"], 16)
            sp.wait_ge(s["out_done"], 16 * PIECES)

        @block.gpsimd
        def _(pool):
            step = sem_chain(pool, s["pool_chain"], 0)
            step(nc.gpsimd.memset(zrow[:, :], 0.0))
            nc.gpsimd.iota(zrow[:, TOKEN_C:TOKEN_C + 1].bitcast(U32), pattern=[[0, 1]], base=T,
                           channel_multiplier=1).then_inc(s["zero_row"], 1)
            step(nc.gpsimd.iota(rows[:, :, TOKEN_C:TOKEN_C + 1].bitcast(U32), pattern=[[P, NT], [0, 1]], base=0,
                                channel_multiplier=1))
            for m in (ident, ident16):
                step(nc.gpsimd.memset(m[:, :], 0.0))
                step(nc.gpsimd.affine_select(out=m[:, :], in_=m[:, :], compare_op=ALU.not_equal, fill=1.0, base=0,
                                             pattern=[[-1, P]], channel_multiplier=1))
            step(nc.gpsimd.memset(ones16[:, :], 1.0))
            step(nc.gpsimd.affine_select(out=before16[:, :], in_=ones16[:, :], compare_op=ALU.is_gt, fill=0.0, base=0,
                                         pattern=[[1, P]], channel_multiplier=-1))
            step(nc.gpsimd.iota(head_i[:, :], pattern=[[-1, H]], base=H, channel_multiplier=1))
            step(nc.gpsimd.memset(sumk[:, :], 0.0))
            step(nc.gpsimd.memset(restart[:, :, :], 1.0))
            step(nc.gpsimd.memset(restart[:, :, 0:1], 0.0))
            step(nc.gpsimd.memset(one_e[:, :], 1.0))
            step(nc.gpsimd.iota(steps128[:, :, :], pattern=[[0, E], [P, NT]], base=0, channel_multiplier=0,
                                allow_small_or_imprecise_dtypes=True))
            nc.gpsimd.iota(tile_no[:, :], pattern=[[1, SLOT_TILES]], base=0, channel_multiplier=0,
                           allow_small_or_imprecise_dtypes=True).then_inc(s["const_pool"], 1)
            pool.wait_ge(s["rsq_seed"], 1)
            rsqrt_newton(nc.gpsimd, step, rstd[:, :], rs_v[:, 0, :], rs_v[:, 1, :]).then_inc(s["rsq_done1"], 1)
            pool.wait_ge(s["rsq_seed2"], 1)
            rsqrt_newton(nc.gpsimd, step, r1[:, :], rs_v[:, 2, :], rs_v[:, 3, :]).then_inc(s["rsq_done2"], 1)
            pool.wait_ge(s["rsq_done2"], 1)
            for t in range(NT):
                pool.wait_ge(s["xn_ready"], t + 1)
                nc.gpsimd.tensor_scalar(rows16[:, t, 0:D], xn[:, t, :], r1[:, t:t + 1], 1.0, ALU.mult,
                                        ALU.mult).then_inc(s["anh_ready"], 1)
            pool.wait_ge(s["w13_in"], 64)
            pool.wait_ge(s["small_in"], 16 * NSMALL)
            for c in range(KC):
                raw = w13_raw[:, c, :]
                step(nc.gpsimd.tensor_scalar(raw, raw, ln2[:, c:c + 1], 1.0, ALU.mult, ALU.mult))
                step(nc.gpsimd.tensor_scalar(w13[:, 0, c, :], raw, 1.0, 1.0, ALU.mult, ALU.mult))
                step(nc.gpsimd.tensor_tensor(w13[:, 1, c, :], raw, w13[:, 0, c, :], ALU.subtract))
            pool.wait_ge(s["wo_in"], 16 * KC)
            pool.wait_ge(s["w2_in"], 32)
            nf = F // P
            parts = [(wo_raw[:, :, :], wo_h[:, :, :], wo_l[:, :, :]),
                     (w2_raw[:, 0:nf, :], w2_h[:, 0:nf, :], w2_l[:, 0:nf, :]),
                     (w2_raw[HP[-1], nf, :], w2_h[HP[-1], nf, :], w2_l[HP[-1], nf, :])]
            for raw, hi, lo in parts:
                step(nc.gpsimd.tensor_scalar(hi, raw, 1.0, 1.0, ALU.mult, ALU.mult))
                step(nc.gpsimd.tensor_tensor(lo, raw, hi.bitcast(F32), ALU.subtract))
            pool.sem_inc(s["prep_done"], 1)
            scatters = iter([(t, j) for t in range(NT) for j in range(TOP)])

            def scatter(n):
                for _, (t, j) in zip(range(n), scatters):
                    nc.gpsimd.indirect_dma_start(
                        rows_dram, bass.IndirectOffsetOnAxis(ap=slot_u[:, j, t:t + 1], axis=0),
                        rows[:, t, :], None).then_inc(s["scatter"], 16)

            pool.sem_inc(s["qs_ready"], 2)

            def step_fn(a, b, c, u):
                if a is not None:
                    pool.wait_ge(s["st_ready"], a * 2 * U + (2 * u + 6))
                    pool.wait_ge(s["gla_used"], a * U + (u + 1))
                    pool.sem_inc(s["pool_turn"], 1)
                    nc.gpsimd.tensor_tensor(qs[:, u % 2, :, :], st[:, u % 2, :, :], pair_bc(q_sb[:, TOK(a)]),
                                            ALU.mult).then_inc(s["qs_ready"], 1)
                if isinstance(b, int) and b == 0 and u == 0:
                    pool.wait_ge(s["route_ready"], 1)
                    pool.wait_ge(s["zero_fill"], 16 * NT)
                    pool.wait_ge(s["anl_ready"], NT)
                if isinstance(b, int) and b == 0 or a is None:
                    scatter(4 if a is None and b is not None else 2)

            turns(pool, step_fn)
            pool.wait_ge(s["pool_turn"], U * B)
            pool.wait_ge(s["scatter"], 16 * NT * TOP)

            pool.sem_inc(s["y_slots"], UN)
            pool.wait_ge(s["y_zero"], 16 * U)

            def add_out(g, u):
                pool.wait_ge(s["ye_ready"], g * UN + (u + 3))
                wait(pool, y_out[u % 2], g * (16 * UN // 2) + 16 * (u // 2))
                pool.sem_inc(s["y_slots"], 1)
                nc.gpsimd.indirect_dma_start(
                    y_dram[u % 2], bass.IndirectOffsetOnAxis(ap=X[:, u, TOKEN_C:TOKEN_C + 1].bitcast(U32), axis=0),
                    y[:, u, :], None, compute_op=ALU.add).then_inc(y_out[u % 2], 16)

            for u in range(UN):
                add_out(0, u)
            with pool.Fori(1, GROUPS) as g:
                for u in range(UN):
                    add_out(g, u)
            pool.wait_ge(s["xr_in"], 16)
            for c in range(PIECES):
                pool.wait_ge(s["fin_mul"], c + 1)
                nc.gpsimd.tensor_tensor(ysum[c], ysum[c], xback[c], ALU.add).then_inc(s["out_ready"], 1)

        @block.scalar
        def _(act):
            chain = sem_chain(act, s["act_chain"], 0)
            act.dma_start(wk1[:, :, :], Wkg1.rearrange("(c p) n -> p c n", p=P)).then_inc(s["wz_in"], 16)
            act.dma_start(wk2[:, :], Wkg2).then_inc(s["wz_in"], 16)
            act.dma_start(rw_raw[:, :], router_w).then_inc(s["wz_in"], 16)
            with nc.allow_non_contiguous_dma(reason="a few hundred numbers"):
                act.dma_start(ln1[:, :], ln1_w.rearrange("(c p) -> p c", p=P)).then_inc(s["small_in"], 16)
                act.dma_start(ln2[:, :], ln2_w.rearrange("(c p) -> p c", p=P)).then_inc(s["small_in"], 16)
                def strided(w, offset, ap):
                    return bass.AP(tensor=w.tensor, offset=w.offset + offset, ap=ap)

                act.dma_start(bz[:, :], strided(bkg2, 0, [[1, KD], [KD, H], [1, 1]])).then_inc(s["small_in"], 16)
                for c in range(KC):
                    act.dma_start(bgT[:, c:c + 1], strided(bg, c * DH, [[1, DH], [HD, H], [1, 1]])).then_inc(s["small_in"], 16)
                act.dma_start(eb[:, :], expert_bias.rearrange("(a e) -> a e", a=1).to_broadcast((P, E))).then_inc(s["small_in"], 16)
            nc.scalar.preload_act_table_set("natural_log_exp_and_others")
            act.wait_ge(s["wa_in"], 64)
            act.wait_ge(s["small_in"], 16 * NSMALL)
            act.wait_ge(s["ln1k_ready"], 1)
            for c in range(KC):
                for out_ap, in_ap, scale in wparts(c, 0):
                    nc.scalar.activation(out_ap, in_ap, ACT.Copy, scale=scale).then_inc(s["wprep_act"], 1)
            act.wait_ge(s["wz_ready"], 1)
            for c in range(KC):
                nc.scalar.activation(hk_view(w_a[:, 0, c, ZC:ZC + QK], False), hk_view(Zp[:, c, :], True), ACT.Copy,
                                     scale=ln1[:, c:c + 1]).then_inc(s["wprep_act"], 1)
            act.wait_ge(s["rw_t"], 1)
            nc.scalar.activation(rw[:, 0, :, :], RWp, ACT.Copy).then_inc(s["wprep_act"], 1)
            act.sem_inc(s["tp_evac"], 2)
            act.sem_inc(s["evac_act"], 2)
            def zero(rows, sem_):
                n, w = rows.shape[0] // P, rows.shape[1]
                act.dma_start(rows.rearrange("(n p) c -> p n c", p=P),
                              zrow[:, 0:w].rearrange("p (a c) -> p a c", a=1).to_broadcast((P, n, w))).then_inc(s[sem_], 16)

            def evac_rows(t, j):
                act.wait_ge(s["tp_ready"], t + 1)
                nc.scalar.activation(anT[:, :, :, bass.ds(t * P, P)],
                                     PS[j % 2].rearrange("p (a c n) -> p a c n", a=2, c=KC),
                                     ACT.Copy).then_inc(s["tp_evac"], 1)

            def turn(b, more):
                def evac(i, out_ap, **kw):
                    act.wait_ge(s["proj_ready"], b * 7 + (i + 1))
                    nc.scalar.activation(out_ap, M[i % 4], kw.get("func", ACT.Copy),
                                         **({"bias": kw["bias"]} if "bias" in kw else {})).then_inc(s["evac_act"], 1)

                def next_rows(j):
                    zero(rows_dram[bass.ds((b * TPB + j) * (SLOTS // NT), SLOTS // NT)], "zero_fill")
                    if more:
                        evac_rows((b + 1) * TPB + j, j)

                evac(0, q_sb[:, bass.ds(b * L, L)])
                act.wait_ge(s["zb_ready"], b + 1)
                nc.scalar.activation(zabs[:, :], zb[:, :], ACT.Abs).then_inc(s["act_chain"], 1)
                next_rows(0)
                act.wait_ge(s["act_chain"], b * 2 + 1)
                nc.scalar.activation(zexp[:, :], zabs[:, :], ACT.Exp, scale=-1.0).then_inc(s["act_chain"], 1)
                evac(2, k_sb[:, bass.ds(b * L, L)])
                next_rows(1)
                act.wait_ge(s["act_chain"], b * 2 + 2)
                nc.scalar.activation(zln[:, :], zexp[:, :], ACT.Ln, bias=1.0).then_inc(s["zln_ready"], 1)
                next_rows(2)
                next_rows(3)
                evac(5, g_sb[:, 0, bass.ds(b * L, L)], func=ACT.Identity, bias=bgT[:, 0:1])
                evac(6, g_sb[:, 1, bass.ds(b * L, L)], func=ACT.Identity, bias=bgT[:, 1:2])
                act.wait_ge(s["zls_ready"], b + 2)
                nc.scalar.activation(a_sb[:, bass.ds(b * L, L)], zls[:, :], ACT.Exp, scale=1.0 / NORMALIZER)\
                    .then_inc(s["a_ready"], 1)

            act.wait_ge(s["zero_row"], 1)
            for j in range(TPB):
                evac_rows(j, j)
            with act.Fori(0, B - 1) as b:
                turn(b, True)
            turn(B - 1, False)
            act.wait_ge(s["ex_in"], 1)
            nc.scalar.activation(ex[:, :, :], prod[:, :, :], ACT.Exp).then_inc(s["exp_ready"], 1)

            act.wait_ge(s["exp_ready"], 1)
            nc.scalar.preload_act_table(ACT.Silu)
            act.sem_inc(s["oT_evac"], 2)
            act.wait_ge(s["lg_ready"], 1)

            def gate_silu(c, m):
                act.wait_ge(s["gu_ready"], c * 2 * NF + (2 * m + 1))
                act.wait_ge(s["hf_ready"], c * NF + (m + 1))
                nc.scalar.activation(sg[HP[m], m % 2, :], M[2 * (m % 2)][0:FT[m][1], :], ACT.Silu).then_inc(s["sg_ready"], 1)

            def high_h(c, m):
                act.wait_ge(s["hf_ready"], c * NF + (m + 3))
                wait(act, s["w2_ready"], c * 2 + 1)
                nc.scalar.activation(h_h[HP[m], m, :], hf[HP[m], m % 2, :], ACT.Copy).then_inc(s["hh_ready"], 1)

            def step_fn(a, b, c, u):
                if isinstance(b, int) and b == 0:
                    half, n = u % (U // 2), -(-(NT + 1) // (U // 2))
                    zero(y_dram[u // (U // 2)][half * n * P:min((half + 1) * n, NT + 1) * P], "y_zero")
                if c is not None and u < NF:
                    gate_silu(c, u)
                if b is not None:
                    if u == 0:
                        wait(act, s["on_ready"], b)
                        for i in range(2):
                            act.wait_ge(s["tpo_ready"], b * 2 + (i + 1))
                            nc.scalar.activation(
                                ot[:, 2 * i:2 * i + 2, :].rearrange("p t (h d) -> p t d h", d=HD),
                                PS[i].rearrange("p (t d h) -> p t d h", t=2, d=HD), ACT.Copy).then_inc(s["ot_ready"], 1)
                    if u == 1:
                        wait(act, s["tpb_ready"], b * 2)
                        act.wait_ge(s["oc_ready"], b + 1)
                        nc.scalar.activation(on[:, :, :], ot[:, :, :], ACT.Square).then_inc(s["sq_ready"], 1)
                    if u == 2:
                        wait(act, s["ogl_ready"], b * 2)
                        act.sem_inc(s["act_turn"], 1)
                        nc.scalar.activation(gs[:, :, :], g_sb[:, :, TOK(b)], ACT.Silu).then_inc(s["gs_ready"], 1)
                    if u == 4:
                        wait(act, s["wo_ready"], b * 2)
                        for i in range(2):
                            act.wait_ge(s["og_ready"], b * 2 + (i + 1))
                            nc.scalar.activation(og_h[:, i, :], gs[:, i, :], ACT.Copy).then_inc(s["ogh_ready"], 1)
                    if u == 6:
                        for t in range(TPB):
                            if t % 2 == 0:
                                act.wait_ge(s["xb_ready"], b * 2 + (t // 2 + 1))
                                act.sem_inc(s["act_turn"], 1)
                            nc.scalar.activation(ot[:, t, :], xn[:, TILES(b, t, 1), :].rearrange("p a d -> p (a d)"), ACT.Square,
                                                 accum_out=grow[3][:, t:t + 1]).then_inc(s["ms_ready"], 1)
                    if u == 7:
                        act.wait_ge(s["row_rstd"], b + 1)
                        wait(act, s["tpn_ready"], b * 4)
                        act.sem_inc(s["act_turn"], 1)
                        for t in range(TPB):
                            nc.scalar.activation(an2[:, t, 0, :], xn[:, TILES(b, t, 1), :].rearrange("p a d -> p (a d)"), ACT.Copy,
                                                 scale=grow[1][:, t:t + 1]).then_inc(s["an2h_ready"], 1)
                    if u == 7:
                        for part in range(2):
                            for i in range(KC):
                                act.wait_ge(s["tpn_ready"], b * 4 + (part * 2 + i + 1))
                                if part == 0 and i == 0:
                                    wait(act, s["gu_ready"], b * 2 * NF)
                                nc.scalar.activation(an2T[:, part, i, :], PS[i], ACT.Copy).then_inc(s["an2T_evac"], 1)
                if a is not None and u in (4, 7):
                    half = u == 7
                    act.wait_ge(s["gla_used"], a * U + (2 + (8 if half else 4)))
                    wait(act, s["tpo_ready"], a * 2)
                    nc.scalar.activation(oT[:, int(half), :], sum_ps[:, int(half), :], ACT.Copy).then_inc(s["oT_evac"], 1)
                for e in experts_at(c, u):
                    act.wait_ge(raw_in[e // 2], 64)
                    wait(act, s["ew_ready"], e)
                    nc.scalar.activation(w_gu[:, e, 0, :, :], gu_raw[:, e + 1, :, :], ACT.Copy).then_inc(s["ewh_ready"], 1)
                if c is not None and u < NF:
                    high_h(c, u)

            turns(act, step_fn)
            act.wait_ge(s["act_turn"], 4 * B)

            attention_over(act)
            act.sem_inc(s["he_ready"], 2)
            act.sem_inc(s["ye_ready"], 2)

            def tile_silu(g, u):
                t = g * UN
                act.wait_ge(s["eg_ready"], t + (u + 3))
                act.wait_ge(s["hm_ready"], t + (u + 1))
                nc.scalar.activation(sl[:, u % 2, :], M[u % 2][:, 0:I], ACT.Silu, scale=X[:, u, SCALE_C:SCALE_C + 1])\
                    .then_inc(s["sl_ready"], 1)

            def tile_rest(g, u):
                t = g * UN
                act.wait_ge(s["ht_ready"], t + (u + 3))
                act.wait_ge(s["dn_ready"], t + (u + 1))
                nc.scalar.activation(hT[:, u % 2, :, :], M[2 + u % 2][0:HK, 0:IC * P].rearrange("p (i n) -> p i n", i=IC),
                                     ACT.Copy).then_inc(s["he_ready"], 1)

            def tile_out(g, u):
                t = g * UN
                e = expert(act, t + u)
                act.wait_ge(s["dn_ready"], t + (u + 3))
                act.wait_ge(s["y_slots"], g * UN + (u + 3))
                act.sem_inc(s["act_turn3"], 1)
                nc.scalar.activation(y[:, u, :], sum_ps[:, u % 2, 0:D], ACT.Copy, scale=X[:, u, bass.ds(e + WEIGHT_C, 1)])\
                    .then_inc(s["ye_ready"], 1)

            def tiles(g, first, last):
                for u in range(UN):
                    if not (last and u == UN - 1):
                        tile_silu(g + (u + 1) // UN, (u + 1) % UN)
                    tile_rest(g, u)
                    if u > 0:
                        tile_out(g, u - 1)
                    elif not first:
                        tile_out(g - 1, UN - 1)
                if last:
                    tile_out(g, UN - 1)

            act.wait_ge(s["tiles_named"], 1)
            tile_silu(0, 0)
            tiles(0, True, False)
            with act.Fori(1, GROUPS - 1) as g:
                tiles(g, False, False)
            tiles(GROUPS - 1, False, True)
            act.wait_ge(s["act_turn3"], SLOT_TILES)
            for c in range(PIECES):
                act.wait_ge(s["ysum_ready"], c + 1)
                nc.scalar.activation(ysum2[c], ysum[c], ACT.Silu).then_inc(s["silu_ready"], 1)

        @block.vector
        def _(dve):
            step = sem_chain(dve, s["dve_chain"], 0)
            dve.wait_ge(s["const_pool"], 1)
            step(nc.vector.tensor_scalar(head_m[:, :], head_i[:, :], H - 1, None, ALU.bitwise_and))
            nc.vector.tensor_scalar(sumk[:, P - H:P], head_m[:, :], 0.0, None, ALU.is_equal).then_inc(s["const_dve"], 1)
            dve.sem_inc(s["evac_dve"], 2)
            for c in range(B):
                dve.wait_ge(xq[c], 16)
                for t in range(c * TPB, (c + 1) * TPB):
                    nc.vector.bn_stats(bst[:, t, :], xn[:, t, :]).then_inc(s["stats"], 1)
            dve.wait_ge(s["stats"], NT)
            for t in range(NT):
                nc.vector.bn_aggr(mv[:, t, :], bst[:, t, :]).then_inc(s["stats"], 1)
            dve.wait_ge(s["stats"], 2 * NT)
            mean, var = mv[:, :, 0], mv[:, :, 1]
            step(nc.vector.tensor_scalar(rs_v[:, 0, :], var, EPS, None, ALU.add))
            rsqrt_seed(step, rstd[:, :], rs_v[:, 0, :]).then_inc(s["rsq_seed"], 1)
            dve.wait_ge(s["small_in"], 16 * NSMALL)
            nc.vector.tensor_scalar(ln1k[:, :], ln1[:, :], KS, None, ALU.mult).then_inc(s["ln1k_ready"], 1)
            dve.wait_ge(s["wk1_t"], 1)
            nc.vector.tensor_copy(wk1T[:, :, :], WK1p).then_inc(s["wk1_copied"], 1)
            dve.wait_ge(s["ln1k_ready"], 1)
            n = 0
            for c in range(KC):
                for (lo_ap, in_ap, scale), (hi_ap, _, _) in zip(wparts(c, 1), wparts(c, 0)):
                    n += 1
                    dve.wait_ge(s["wprep_act"], n)
                    nc.vector.scalar_tensor_tensor(out=lo_ap, in0=in_ap, scalar=scale, in1=hi_ap,
                                                   op0=ALU.mult, op1=ALU.subtract).then_inc(s["wprep_dve"], 1)
            n += KC
            dve.wait_ge(s["wprep_act"], n)
            for c in range(KC):
                nc.vector.scalar_tensor_tensor(out=hk_view(w_a[:, 1, c, ZC:ZC + QK], False), in0=hk_view(Zp[:, c, :], True),
                                               scalar=ln1[:, c:c + 1], in1=hk_view(w_a[:, 0, c, ZC:ZC + QK], False),
                                               op0=ALU.mult, op1=ALU.subtract).then_inc(s["wprep_dve"], 1)
            dve.wait_ge(s["wprep_act"], n + 1)
            nc.vector.tensor_tensor(rw[:, 1, :, :], RWp, rw[:, 0, :, :], ALU.subtract).then_inc(s["wprep_dve"], 1)
            dve.wait_ge(s["rsq_done1"], 1)
            step(nc.vector.tensor_tensor(rs_v[:, 2, :], rstd[:, :], rstd[:, :], ALU.mult))
            step(nc.vector.tensor_tensor(rs_v[:, 2, :], rs_v[:, 2, :], var, ALU.mult))
            step(nc.vector.tensor_scalar(rs_v[:, 2, :], rs_v[:, 2, :], EPS, None, ALU.add))
            rsqrt_seed(step, r1[:, :], rs_v[:, 2, :]).then_inc(s["rsq_seed2"], 1)
            step(nc.vector.scalar_tensor_tensor(out=negmr[:, :], in0=mean, scalar=-1.0, in1=rstd[:, :],
                                                op0=ALU.mult, op1=ALU.mult))
            for t in range(NT):
                nc.vector.tensor_scalar(xn[:, t, :], xn[:, t, :], rstd[:, t:t + 1], negmr[:, t:t + 1],
                                        ALU.mult, ALU.add).then_inc(s["xn_ready"], 1)
            dve.wait_ge(s["rsq_done2"], 1)
            for t in range(NT):
                dve.wait_ge(s["anh_ready"], t + 1)
                nc.vector.scalar_tensor_tensor(out=rows16[:, t, D:2 * D], in0=xn[:, t, :], scalar=r1[:, t:t + 1],
                                               in1=rows16[:, t, 0:D], op0=ALU.mult, op1=ALU.subtract)\
                    .then_inc(s["anl_ready"], 1)
            cview = rows[:, :, SCALE_C:SCALE_C + 1]
            nc.vector.tensor_tensor(cview, rs_v[:, 2, :].rearrange("p (t a) -> p t a", a=1),
                                    r1[:, :].rearrange("p (t a) -> p t a", a=1), ALU.mult).then_inc(s["cscale"], 1)
            dve.sem_inc(s["zls_ready"], 1)
            with dve.Fori(0, B) as b:
                dve.wait_ge(s["zls_ready"], b + 1)
                dve.wait_ge(s["proj_ready"], b * 7 + 2)
                nc.vector.tensor_scalar(zb[:, :], M[1], bz[:, 0:1], None, ALU.add).then_inc(s["evac_dve"], 1)
                dve.wait_ge(s["evac_dve"], b * 3 + 3)
                dve.sem_inc(s["zb_ready"], 1)
                for c in range(2):
                    dve.wait_ge(s["proj_ready"], b * 7 + (4 + c))
                    dve.wait_ge(vt_out[c], b * 16 + 16)
                    nc.vector.tensor_copy(vt[:, c, :], M[(3 + c) % 4]).then_inc(s["evac_dve"], 1)
                    dve.wait_ge(s["evac_dve"], b * 3 + (4 + c))
                    dve.sem_inc(s["vt_ready"], 1)
                dve.wait_ge(s["zln_ready"], b + 1)
                nc.vector.scalar_tensor_tensor(out=zls[:, :], in0=zb[:, :], scalar=0.0, in1=zln[:, :],
                                               op0=ALU.min, op1=ALU.subtract).then_inc(s["zls_ready"], 1)
            dve.sem_inc(s["kv_ready"], 2)
            dve.sem_inc(s["st_ready"], 4)

            def recurrence(a, u):
                r = u % 2
                dve.wait_ge(vr_in[r], a * 16 * U + 32 * (u // 2 + 1))
                dve.wait_ge(s["st_ready"], a * 2 * U + (2 * u + 2))
                nc.vector.tensor_tensor(kv[:, r, :, :], vrep[:, r, :, :], pair_bc(k_sb[:, TOK(a)]),
                                        ALU.mult).then_inc(s["kv_ready"], 1)
                yield
                dve.wait_ge(s["kv_ready"], a * U + (u + 3))
                if isinstance(a, int) and a == 0 and u == 0:
                    for c in range(2):
                        dve.wait_ge(vt_out[c], 16 * (B + 1))
                dve.wait_ge(s["qs_ready"], a * U + (u + 1))
                for j in range(2):
                    nc.vector.tensor_tensor_scan(st[:, r, j, :], a_sb[:, TOK(a)], kv[:, r, j, :], 0.0,
                                                 ALU.mult, ALU.add).then_inc(s["st_ready"], 1)
                    if j == 0:
                        yield

            dve.wait_ge(s["a_ready"], B)
            dve.wait_ge(s["prep_done"], 1)
            def first_recurrence():
                for u in range(U):
                    yield from recurrence(0, u)
                    yield

            first = first_recurrence()
            early = 6

            def between():
                nonlocal early
                early -= 1
                if early >= 0 or summed:
                    next(first, None)

            summed = False
            step = sem_chain(dve, s["dve_chain"], step(None), between=between)
            dve.wait_ge(s["logits_ready"], NT)
            dve.wait_ge(s["cscale"], 1)
            cb = cview.to_broadcast((P, NT, E))
            LG = O1[:, 0:NT * E].rearrange("p (t e) -> p t e", e=E)
            dve.wait_ge(s["proj_ready"], 7 * B)
            nc.vector.tensor_tensor(lg[:, :, :], LG, cb, ALU.mult).then_inc(s["lg_ready"], 1)
            dve.wait_ge(s["lg_ready"], 1)
            step(nc.vector.tensor_tensor(lg[:, :, :], lg[:, :, :],
                                         eb[:, :].rearrange("p (a e) -> p a e", a=1).to_broadcast((P, NT, E)), ALU.add))
            nc.vector.tensor_reduce(mx[:, :], lg[:, :, :], AX.X, ALU.max).then_inc(s["dve_max"], 1)
            for t in range(NT):
                nc.vector.max(m8[:, t, :], lg[:, t, :]).then_inc(s["dve_max"], 1)
            dve.wait_ge(s["dve_max"], NT + 1)
            un = lambda ap: ap.rearrange("p (t a) -> p t a", a=1).to_broadcast((P, NT, E))
            flat = lambda ap: ap.rearrange("p t e -> p (t e)")
            nc.vector.tensor_tensor(prod[:, :, :], lg[:, :, :], un(mx[:, :]), ALU.subtract).then_inc(s["ex_in"], 1)
            v4 = m8[:, :, TOP - 1:TOP].to_broadcast((P, NT, E))
            step(nc.vector.tensor_tensor(gt[:, :, :], lg[:, :, :], v4, ALU.is_gt))
            step(nc.vector.tensor_tensor(eq[:, :, :], lg[:, :, :], v4, ALU.is_equal))
            step(nc.vector.tensor_reduce(need[:, :], gt[:, :, :], AX.X, ALU.add))
            step(nc.vector.tensor_scalar(need[:, :], need[:, :], -1.0, float(TOP), ALU.mult, ALU.add))
            step(nc.vector.tensor_tensor_scan(flat(eqc[:, :, :]), flat(restart[:, :, :]), flat(eq[:, :, :]), 0.0,
                                              ALU.mult, ALU.add))
            step(nc.vector.tensor_tensor(eqc[:, :, :], eqc[:, :, :], un(need[:, :]), ALU.is_le))
            step(nc.vector.tensor_tensor(eq[:, :, :], eq[:, :, :], eqc[:, :, :], ALU.mult))
            step(nc.vector.tensor_tensor(Msel[:, :, :], gt[:, :, :], eq[:, :, :], ALU.add))
            nc.vector.tensor_copy(M16[:, :, :], Msel[:, :, :]).then_inc(s["m16_ready"], 1)
            dve.wait_ge(s["exp_ready"], 1)
            step(nc.vector.tensor_tensor(wgt[:, :, :], ex[:, :, :], Msel[:, :, :], ALU.mult))
            step(nc.vector.tensor_reduce(sm[:, :], wgt[:, :, :], AX.X, ALU.add))
            step(nc.vector.reciprocal(sm[:, :], sm[:, :]))
            step(nc.vector.tensor_tensor(rows[:, :, WEIGHT_C:ROW], wgt[:, :, :], un(sm[:, :]), ALU.mult))
            dve.wait_ge(s["cum_ready"], 1)
            summed = True
            CUM = T0[:, 0:NT * E].rearrange("p (t e) -> p t e", e=E)
            TOT = T0[:, NT * E:2 * NT * E].rearrange("p (t e) -> p e t", e=E)
            step(nc.vector.tensor_copy(tot[:, :, :], TOT))
            step(nc.vector.tensor_tensor_scan(flat(inc[:, :, :]), flat(restart[:, :, :]), flat(tot[:, :, :]), 0.0,
                                              ALU.mult, ALU.add))
            step(nc.vector.tensor_tensor(over[:, :, :], inc[:, :, NT - 1:NT].to_broadcast((P, E, NT)),
                                         steps128[:, :, :], ALU.is_gt))
            step(nc.vector.tensor_reduce(ntl[:, :], over[:, :, :], AX.X, ALU.add))
            step(nc.vector.tensor_tensor_scan(ntc[:, :], one_e[:, :], ntl[:, :], 0.0, ALU.mult, ALU.add))
            step(nc.vector.tensor_tensor(base[:, :], ntc[:, :], ntl[:, :], ALU.subtract))
            step(nc.vector.tensor_scalar(base[:, :], base[:, :], float(P), None, ALU.mult))
            step(nc.vector.tensor_tensor(inc[:, :, :], inc[:, :, :], tot[:, :, :], ALU.subtract))
            step(nc.vector.tensor_tensor(slot[:, :, :], CUM, inc[:, :, :].rearrange("p e t -> p t e"), ALU.add))
            step(nc.vector.tensor_tensor(slot[:, :, :], slot[:, :, :],
                                         base[:, :].rearrange("p (a e) -> p a e", a=1).to_broadcast((P, NT, E)), ALU.add))
            step(nc.vector.tensor_tensor_scan(flat(cnt[:, :, :]), flat(restart[:, :, :]), flat(Msel[:, :, :]), 0.0,
                                              ALU.mult, ALU.add))
            for j in range(TOP):
                step(nc.vector.scalar_tensor_tensor(out=pick[:, :, :], in0=cnt[:, :, :], scalar=float(j + 1),
                                                    in1=Msel[:, :, :], op0=ALU.is_equal, op1=ALU.mult))
                step(nc.vector.tensor_tensor(prod[:, :, :], pick[:, :, :], slot[:, :, :], ALU.mult))
                step(nc.vector.tensor_reduce(slot_f[:, j, :], prod[:, :, :], AX.X, ALU.add))
            nc.vector.tensor_copy(slot_u[:, :, :], slot_f[:, :, :]).then_inc(s["route_ready"], 1)

            def name_tiles():
                step = sem_chain(dve, s["tile_chain"], 0)
                step(nc.vector.tensor_tensor(owner[:, :, :],
                                             ntc[0:1, :].rearrange("p (a e) -> p a e", a=1).to_broadcast((1, SLOT_TILES, E)),
                                             tile_no[:, :].rearrange("p (t a) -> p t a", a=1).to_broadcast((1, SLOT_TILES, E)),
                                             ALU.is_le))
                step(nc.vector.tensor_reduce(own1[:, :], owner[:, :, :], AX.X, ALU.add))
                nc.vector.tensor_scalar(tile_expert[:, 0:SLOT_TILES], own1[:, :], float(E - 1), None, ALU.min)\
                    .then_inc(s["tiles_named"], 1)

            for _ in first:
                pass
            dve.wait_ge(s["route_ready"], 1)
            dve.sem_inc(s["hf_ready"], 2)
            dve.sem_inc(s["hl_ready"], 2)
            dve.sem_inc(s["xc_ready"], 2)

            def split_low(c, u):
                for e in experts_at(c, u - 1):
                    dve.wait_ge(s["ewh_ready"], e + 1)
                    nc.vector.tensor_tensor(w_gu[:, e, 1, :, :], gu_raw[:, e + 1, :, :], w_gu[:, e, 0, :, :],
                                            ALU.subtract).then_inc(s["ew_ready"], 1)

            dve.sem_inc(s["xe_ready"], 2)

            def rows_out(g, u):
                dve.wait_ge(s["xt_ready"], g * UN + (u + 1))
                wait(dve, s["eg_ready"], g * UN + (u + 1) if not (isinstance(g, int) and g == 0 and u < 2) else 0)
                nc.vector.tensor_copy(xT[:, u % 2, :, :, :].rearrange("p a c n -> p (a c n)"), PS[u % 2]).then_inc(s["xe_ready"], 1)

            def low_h(c, m):
                dve.wait_ge(s["hh_ready"], c * NF + (m + 1))
                nc.vector.tensor_tensor(h_l[HP[m], m, :], hf[HP[m], m % 2, :], h_h[HP[m], m, :].bitcast(F32),
                                        ALU.subtract).then_inc(s["hl_ready"], 1)

            def gated(c, m):
                if m:
                    low_h(c, m - 1)
                up = M[2 * (m % 2) + 1] if m < NF - 1 else M[2 * (m % 2)]
                dve.wait_ge(s["sg_ready"], c * NF + (m + 1))
                dve.wait_ge(s["gu_ready"], c * 2 * NF + (2 * m + 2))
                dve.wait_ge(s["hl_ready"], c * NF + (m + 1))
                nc.vector.tensor_tensor(hf[HP[m], m % 2, :], up[HP[m], :], sg[HP[m], m % 2, :],
                                        ALU.mult).then_inc(s["hf_ready"], 1)

            AHEAD = {0: (0, 1), 1: (2,), 2: (3,), 3: ()}

            def step_fn(a, b, c, u):
                if a is not None and not (isinstance(a, int) and a == 0):
                    for ahead in AHEAD.get(u, (u,)):
                        for _ in recurrence(a, ahead):
                            pass
                if c is not None and u == NF:
                    low_h(c, NF - 1)
                if isinstance(b, int) and b == 0 and u == 0:
                    name_tiles()
                if b is not None:
                    if u == 1:
                        chain = sem_chain(dve, s["head_dve"], 0, 6 + 3 * NEWTON, b)
                        dve.wait_ge(s["ot_ready"], b * 2 + 2)
                        ot_h = ot[:, :, :].rearrange("p t (h d) -> p (t h) d", d=HD)
                        chain(nc.vector.tensor_reduce(ghead[3][:, :], ot_h, AX.X, ALU.add))
                        chain(nc.vector.tensor_scalar(ghead[3][:, :], ghead[3][:, :], 1.0 / HD, None, ALU.mult))
                        nc.vector.tensor_tensor(ot_h, ot_h,
                                                ghead[3][:, :].rearrange("p (g a) -> p g a", a=1).to_broadcast((P, TPB * H, HD)),
                                                ALU.subtract).then_inc(s["oc_ready"], 1)
                    if u == 2:
                        chain = sem_chain(dve, s["head_dve"], 2, 6 + 3 * NEWTON, b)
                        dve.wait_ge(s["sq_ready"], b + 1)
                        chain(nc.vector.tensor_reduce(ghead[0][:, :], on[:, :, :].rearrange("p t (h d) -> p (t h) d", d=HD),
                                                      AX.X, ALU.add))
                        chain(nc.vector.tensor_scalar(ghead[0][:, :], ghead[0][:, :], -0.5 / HD, -0.5 * EPS, ALU.mult, ALU.add))
                        chain(rsqrt_seed(chain, ghead[1][:, :], ghead[0][:, :], NEG_HALF_MAGIC))
                        chain(rsqrt_newton_neg(chain, ghead[1][:, :], ghead[0][:, :], ghead[2][:, :]))
                    if u == 3:
                        for t in range(TPB):
                            nc.vector.tensor_tensor(
                                on[:, t, :].rearrange("p (d h) -> p h d", d=HD), ot[:, t, :].rearrange("p (h d) -> p h d", d=HD),
                                ghead[1][:, t * H:(t + 1) * H].rearrange("p (h a) -> p h a", a=1).to_broadcast((P, H, HD)),
                                ALU.mult).then_inc(s["on_ready"] if t == TPB - 1 else s["on_part"], 1)
                        dve.wait_ge(s["on_part"], b * (TPB - 1) + (TPB - 1))
                    if u == 5:
                        for i in range(2):
                            dve.wait_ge(s["ogh_ready"], b * 2 + (i + 1))
                            nc.vector.tensor_tensor(og_l[:, i, :], gs[:, i, :], og_h[:, i, :].bitcast(F32),
                                                    ALU.subtract).then_inc(s["ogl_ready"], 1)
                    if u == 6:
                        for i in range(2):
                            dve.wait_ge(s["wo_ready"], b * 2 + (i + 1))
                            xt = xn[:, TILES(b, 2 * i, 2), :].rearrange("p t d -> p (t d)")
                            nc.vector.tensor_tensor(xt, PS[i], xt, ALU.add).then_inc(s["xb_ready"], 1)
                    if u == 6:
                        chain = sem_chain(dve, s["row_dve"], 0, 2 + 3 * NEWTON, b)
                        dve.wait_ge(s["ms_ready"], b * 4 + 4)
                        chain(nc.vector.tensor_scalar(grow[0][:, :], grow[3][:, :], -0.5 / D, -0.5 * EPS, ALU.mult, ALU.add))
                        chain(rsqrt_seed(chain, grow[1][:, :], grow[0][:, :], NEG_HALF_MAGIC))
                        rsqrt_newton_neg(chain, grow[1][:, :], grow[0][:, :], grow[2][:, :])\
                            .then_inc(s["row_rstd"], 1)
                    if u == 7:
                        for t in range(TPB):
                            dve.wait_ge(s["an2h_ready"], b * 4 + (t + 1))
                            nc.vector.scalar_tensor_tensor(
                                out=an2[:, t, 1, :], in0=xn[:, TILES(b, t, 1), :].rearrange("p a d -> p (a d)"), scalar=grow[1][:, t:t + 1],
                                in1=an2[:, t, 0, :], op0=ALU.mult, op1=ALU.subtract).then_inc(s["an2l_ready"], 1)
                if c is not None:
                    split_low(c, u)
                    if u < NF:
                        gated(c, u)
                if b is not None and u == 4:
                    dve.wait_ge(s["gs_ready"], b + 1)
                    for i in range(2):
                        dve.wait_ge(s["tpb_ready"], b * 2 + (i + 1))
                        nc.vector.tensor_tensor(gs[:, i, :], PS[i], gs[:, i, :], ALU.mult).then_inc(s["og_ready"], 1)
                if c is not None:
                    if u == 7 and isinstance(c, int) and c == B - 1:
                        rows_out(0, 0)
                        rows_out(0, 1)
                        split_low(c, u + 1)
                    if u == 7:
                        for i in range(2):
                            dve.wait_ge(s["w2_ready"], c * 2 + (i + 3))
                            xt = xn[:, TILES(c, 2 * i, 2), :].rearrange("p t d -> p (t d)")
                            nc.vector.tensor_tensor(xt, M[i], xt, ALU.add).then_inc(s["xc_ready"], 1)
            turns(dve, step_fn)

            attention_over(dve)
            dve.sem_inc(s["hm_ready"], 2)

            def hidden(g, u):
                dve.wait_ge(s["sl_ready"], g * UN + (u + 1))
                dve.wait_ge(s["ht_ready"], g * UN + (u + 1))
                nc.vector.scalar_tensor_tensor(out=h[:, u % 2, :], in0=M[u % 2][:, I:2 * I], scalar=X[:, u, SCALE_C:SCALE_C + 1],
                                               in1=sl[:, u % 2, :], op0=ALU.mult, op1=ALU.mult).then_inc(s["hm_ready"], 1)

            def tiles(g, last):
                for u in range(UN):
                    if not (last and u >= UN - 2):
                        rows_out(g + (u + 2) // UN, (u + 2) % UN)
                    if not (last and u == UN - 1):
                        hidden(g + (u + 1) // UN, (u + 1) % UN)

            hidden(0, 0)
            with dve.Fori(0, GROUPS - 1) as g:
                tiles(g, False)
            tiles(GROUPS - 1, True)
            def scaled(c):
                dve.wait_ge(s["silu_ready"], c + 1)
                nc.vector.tensor_tensor(ysum[c], ysum2[c], xn[:, c * TPP:(c + 1) * TPP, :].rearrange("p t d -> p (t d)"),
                                        ALU.mult).then_inc(s["fin_mul"], 1)

            for c in range(PIECES):
                dve.wait_ge(x_in[c], 16 * GROUPS + 32)
                nc.vector.tensor_tensor(ysum[c], ysum[c], ysum2[c], ALU.add).then_inc(s["ysum_ready"], 1)
                if c > 0:
                    scaled(c - 1)
            scaled(PIECES - 1)

        @block.tensor
        def _(pe):
            pe.wait_ge(s["const_pool"], 1)
            pe.wait_ge(s["wz_in"], 48)
            for c in range(KC):
                last = nc.tensor.transpose(WK1p[:, c, :], wk1[:, c, :], ident[:, :])
            last.then_inc(s["wk1_t"], 1)
            for c in range(KC):
                last = nc.tensor.transpose(RWp[:, c, :], rw_raw[:, c * P:(c + 1) * P], ident[0:E, 0:E])
            last.then_inc(s["rw_t"], 1)
            pe.wait_ge(s["wk1_copied"], 1)
            for c in range(KC):
                last = nc.tensor.matmul(Zp[:, c, :], wk1T[:, c, :], wk2[:, :], start=True, stop=True)
            last.then_inc(s["wz_ready"], 1)
            pe.wait_ge(s["wprep_dve"], NWPREP)

            def turn_rows(t, j):
                pe.wait_ge(s["anl_ready"], t + 1)
                pe.wait_ge(s["tp_evac"], t + 1)
                for n in range(2 * KC):
                    last = nc.tensor.matmul(PS[j % 2][:, n * P:(n + 1) * P],
                                            rows16[:, bass.ds(t, 1), n * P:(n + 1) * P].rearrange("p a d -> p (a d)"),
                                            ident16[:, :], start=True, stop=True)
                last.then_inc(s["tp_ready"], 1)

            def turn(b, more):
                cols = [QC, ZC, KCOL, VC, VC + P, GC, GC + P]
                free = [(s["evac_dve"], b * 3 + 2), (s["evac_act"], b * 4 + 1), (s["evac_act"], b * 4 + 2),
                        (s["evac_dve"], b * 3 + 1), (s["evac_act"], b * 4 + 3), (s["evac_dve"], b * 3 + 3),
                        (s["evac_act"], b * 4 + 4)]
                pe.wait_ge(s["tp_evac"], b * TPB + TPB + 2)
                for i, col in enumerate(cols):
                    pe.wait_ge(*free[i])
                    triple(pe, M[i % 4],
                           [(w_a[:, wl, c, col:col + P], anT[:, hl, c, bass.ds(b * L, L)])
                            for c in range(KC) for hl, wl in ((0, 0), (0, 1), (1, 0))]).then_inc(s["proj_ready"], 1)
                    if i < TPB:
                        t = b * TPB + i
                        triple(pe, O1[:, bass.ds(t * E, E)],
                               [(anT[:, hl, c, bass.ds(t * P, P)], rw[:, wl, c, :])
                                for c in range(KC) for hl, wl in ((0, 0), (0, 1), (1, 0))]).then_inc(s["logits_ready"], 1)
                        if more:
                            turn_rows((b + 1) * TPB + i, i)

            for j in range(TPB):
                turn_rows(j, j)
            with pe.Fori(0, B - 1) as b:
                turn(b, True)
            turn(B - 1, False)
            pe.wait_ge(s["m16_ready"], 1)
            pe.wait_ge(s["tp_evac"], NT + 2)
            sel = M16[:, :, :].rearrange("p t e -> p (t e)")
            nc.tensor.matmul(T0[:, 0:NT * E], before16[:, :], sel, start=True, stop=True)
            nc.tensor.matmul(T0[:, NT * E:2 * NT * E], ones16[:, :], sel, start=True, stop=True).then_inc(s["cum_ready"], 1)

            pe.wait_ge(s["lg_ready"], 1)
            pe.wait_ge(s["evac_dve"], 3 * B + 2)
            pe.wait_ge(s["evac_act"], 4 * B + 2)
            pe.sem_inc(s["gla_used"], 2)
            pe.sem_inc(s["w2_ready"], 2)

            def read_out(a, u):
                pe.wait_ge(s["qs_ready"], a * U + (u + 3))
                if u % 4 == 0:
                    pe.wait_ge(s["oT_evac"], a * 2 + (u // 4 + 1))
                for j in range(2):
                    dd = (2 * u + j) % DH
                    off = P - H - dd * H
                    last = nc.tensor.matmul(sum_ps[:, u // 4, :], sumk[:, off:off + P], qs[:, u % 2, j, :],
                                            start=(dd == 0), stop=(dd == DH - 1))
                last.then_inc(s["gla_used"], 1)

            def transpose_rows(g, u):
                pe.wait_ge(x_in[u], 16 * (g + 1))
                pe.wait_ge(s["xe_ready"], g * UN + (u + 1))
                for n in range(2 * KC):
                    last = nc.tensor.matmul(PS[u % 2][:, n * P:(n + 1) * P], X16[:, u, n * P:(n + 1) * P], ident16[:, :],
                                            start=True, stop=True)
                last.then_inc(s["xt_ready"], 1)

            def w2_products(c, u):
                if isinstance(c, int) and c == B - 1 and u == 6:
                    pe.wait_ge(s["an2T_evac"], 4 * B)
                    transpose_rows(0, 0)
                    transpose_rows(0, 1)
                pe.wait_ge(s["hl_ready"], c * NF + (NF + 2))
                for t in (2 * (u - NF), 2 * (u - NF) + 1):
                    last = triple(pe, M[u - NF][:, (t % 2) * D:(t % 2 + 1) * D],
                                  [(h[HP[m], m, t * P:(t + 1) * P], w[HP[m], m, :])
                                   for m in range(NF)
                                   for h, w in ((h_h, w2_h), (h_h, w2_l), (h_l, w2_h))])
                last.then_inc(s["w2_ready"], 1)

            def gate_up_mlp(c, m):
                if m == 0:
                    pe.wait_ge(s["an2T_evac"], c * 4 + 4)
                    pe.wait_ge(s["xc_ready"], c * 2 + 2)
                pe.wait_ge(s["hf_ready"], c * NF + (m + 1))
                last = m == NF - 1
                for i in range(1 if last else 2):
                    col = 2 * FULL if last else i * FULL + m * P
                    triple(pe, M[2 * (m % 2) + i],
                           [(w13[:, wl, kc, col:col + P], an2T[:, hl, kc, :])
                            for kc in range(KC) for hl, wl in ((0, 0), (0, 1), (1, 0))])\
                        .then_inc(s["gu_ready"], 2 if last else 1)

            def step_fn(a, b, c, u):
                if c is not None and u < NF:
                    gate_up_mlp(c, u)
                if a is not None and u > 0:
                    read_out(a, u - 1)
                if b is not None:
                    if u == 0:
                        wait(pe, s["an2T_evac"], b * 4)
                        if isinstance(b, int) and b == 0:
                            pe.wait_ge(s["route_ready"], 1)
                        for i in range(2):
                            for n in range(4):
                                t, kc = 2 * i + n // 2, n % 2
                                pe.wait_ge(s["oT_evac"], b * 2 + (kc + 3))
                                last = nc.tensor.transpose(PS[i][:, n * P:(n + 1) * P], oT[:, kc, t * P:(t + 1) * P], ident[:, :])
                            last.then_inc(s["tpo_ready"], 1)
                    if u == 4:
                        pe.wait_ge(s["on_ready"], b + 1)
                        for i in range(2):
                            for t in range(TPB):
                                last = nc.tensor.transpose(PS[i][:, t * P:(t + 1) * P], on[:, t, i * P:(i + 1) * P], ident[:, :])
                            last.then_inc(s["tpb_ready"], 1)
                    if u == 5:
                        pe.wait_ge(s["ogl_ready"], b * 2 + 2)
                        for t in range(TPB):
                            last = triple(pe, PS[t // 2][:, (t % 2) * D:(t % 2 + 1) * D],
                                          [(og[:, kc, t * P:(t + 1) * P], wo[:, kc, :])
                                           for kc in range(KC) for og, wo in ((og_h, wo_h), (og_h, wo_l), (og_l, wo_h))])
                            if t % 2:
                                last.then_inc(s["wo_ready"], 1)
                    if u == 7:
                        if c is not None:
                            w2_products(c, u)
                        pe.wait_ge(s["an2l_ready"], b * 4 + 4)
                        for part in range(2):
                            for i in range(KC):
                                if part:
                                    pe.wait_ge(s["an2T_evac"], b * 4 + (i + 1))
                                for t in range(TPB):
                                    last = nc.tensor.matmul(PS[i][:, t * P:(t + 1) * P], an2[:, t, part, i * P:(i + 1) * P],
                                                            ident16[:, :], start=True, stop=True)
                                last.then_inc(s["tpn_ready"], 1)
                if c is not None and (u == 6 or u == 7 and b is None):
                    w2_products(c, u)
                if a is not None and u == U - 1:
                    read_out(a, u)

            turns(pe, step_fn)

            pe.wait_ge(s["tiles_named"], 1)
            e_first = expert(pe, 0)
            attention_over(pe)
            pe.sem_inc(s["eg_ready"], 2)
            pe.sem_inc(s["ht_ready"], 2)
            pe.sem_inc(s["dn_ready"], 2)

            def gate_up(g, u, e):
                pe.wait_ge(s["ew_ready"], e + 1)
                pe.wait_ge(s["xe_ready"], g * UN + (u + 3))
                pe.wait_ge(s["hm_ready"], g * UN + (u + 1))
                triple(pe, M[u % 2][:, 0:2 * I],
                       [(xT[:, u % 2, hl, kc, :], w_gu[:, bass.ds(e, 1), wl, kc, :].rearrange("p a n -> p (a n)"))
                        for kc in range(KC) for hl, wl in ((0, 0), (0, 1), (1, 0))]).then_inc(s["eg_ready"], 1)

            def transpose_hidden(g, u):
                pe.wait_ge(s["hm_ready"], g * UN + (u + 3))
                pe.wait_ge(s["he_ready"], g * UN + (u + 1))
                for i in range(IC):
                    last = nc.tensor.transpose(M[2 + u % 2][0:HK, i * P:(i + 1) * P], h[:, u % 2, i * HK:(i + 1) * HK], ident[:, :])
                last.then_inc(s["ht_ready"], 1)

            def down(g, u, e):
                pe.wait_ge(s["he_ready"], g * UN + (u + 3))
                pe.wait_ge(s["ye_ready"], g * UN + (u + 1))
                triple(pe, sum_ps[:, u % 2, 0:D],
                       [(hT[:, u % 2, i, :], wd[:, bass.ds(e, 1), i, :].rearrange("p a n -> p (a n)")) for i in range(IC)])\
                    .then_inc(s["dn_ready"], 1)

            def tiles(g, first, last):
                for u in range(UN):
                    if not (last and u == UN - 1):
                        e_next = expert(pe, g * UN + u + 1)
                    if not (last and u >= UN - 2):
                        transpose_rows(g + (u + 2) // UN, (u + 2) % UN)
                    if not (last and u == UN - 1):
                        gate_up(g + (u + 1) // UN, (u + 1) % UN, e_next)
                    transpose_hidden(g, u)
                    if u > 0:
                        down(g, u - 1, e_before)
                    elif not first:
                        down(g - 1, UN - 1, expert(pe, g * UN - 1))
                    e_before = e if u > 0 else expert(pe, g * UN)
                    e = e_next
                if last:
                    down(g, UN - 1, e_before)

            gate_up(0, 0, e_first)
            pe.wait_ge(s["wd_in"], 32)
            tiles(0, True, False)
            with pe.Fori(1, GROUPS - 1) as g:
                tiles(g, False, False)
            tiles(GROUPS - 1, False, True)

_INS = [f"L0_attn_{n}" for n in ("x", "Wq", "Wk", "Wkg1", "Wkg2", "bkg2", "Wv", "Wg", "bg", "Wo", "ln1_w", "ln2_w",
                                 "W1", "W3", "W2")] + \
       [f"L0_ffn_{n}" for n in ("router_w", "expert_bias", "gate_proj", "up_proj", "down_proj")]
_OUTS = [((4, 512, 256), "float32")]

def kernel(**inputs):
    import numpy as _np
    import concourse.bacc as _bacc
    from concourse import mybir as _mybir
    from concourse.bass_utils import run_bass_kernel_spmd as _run

    nc = _bacc.Bacc("TRN2", target_bir_lowering=False, num_devices=1)
    arrays, args = {}, []
    for name in _INS:
        a = _np.ascontiguousarray(inputs[name])
        arrays[f"in_{name}_dram"] = a
        args.append(nc.dram_tensor(f"in_{name}_dram", a.shape, _mybir.dt.from_np(a.dtype), kind="ExternalInput").ap())
    for i, (shape, dtype) in enumerate(_OUTS):
        dt = _mybir.dt.from_np(_np.dtype(dtype))
        args.append(nc.dram_tensor(f"out_{i}_dram", shape, dt, kind="ExternalOutput").ap())
    build_block(nc, *args)
    r = _run(nc, [arrays], core_ids=[0])
    return r.results[0]["out_0_dram"]
```
